# Optimizing a Trainium2 kernel written in Bass

```python
import numpy as np
import jax
import jax.numpy as jnp

def _softmax(x, axis=-1):
    return jax.nn.softmax(x, axis=axis)

def _gelu(x):
    return jax.nn.gelu(x, approximate=True)

def _silu(x):
    return jax.nn.silu(x)

def _sigmoid(x):
    return jax.nn.sigmoid(x)

def _layernorm(x, axis=-1, eps=1e-05):
    m = jnp.mean(x, axis=axis, keepdims=True)
    v = jnp.var(x, axis=axis, keepdims=True)
    return (x - m) / jnp.sqrt(v + eps)

def _scatter_add(tgt, idx, src, axis=0):
    return tgt.at[idx].add(src)

def _segment_sum(src, seg, n):
    return jax.ops.segment_sum(src, seg, n)
kernel_name = 'mk_decoder_postln_d2_seqx_r8_0da58d'

def setup_inputs(seed: int=0):
    np.random.seed(seed)
    _w = jnp.asarray

    def _rec_inputs():
        import jax
        import jax.numpy as jnp
        _rk = jax.random.key(seed)
        x = -0.0003929 + 0.9999 * jax.random.normal(jax.random.fold_in(_rk, 1), (8, 128, 256), jnp.float32)
        _lenS = 128 - jax.random.randint(jax.random.fold_in(_rk, 7), (8,), 0, max(1, 128 // 4) + 1, jnp.int32)
        _lenS2 = 128 - jax.random.randint(jax.random.fold_in(_rk, 8), (8,), 0, max(1, 128 // 4) + 1, jnp.int32)
        _ctx_2048P = jax.random.normal(jax.random.fold_in(_rk, 11), (8, 16, 256), jnp.float32)
        _ctx_2048c = jax.random.dirichlet(jax.random.fold_in(_rk, 511), 0.3 * jnp.ones((16,), jnp.float32), (8, 128))
        _ctx_2048t = jnp.einsum('bsk,bkd->bsd', _ctx_2048c, _ctx_2048P)
        _ctx_2048t = _ctx_2048t * jax.lax.rsqrt(jnp.mean(jnp.square(_ctx_2048t)) + 1e-12) * 0.953939
        ctx_2048 = -1.39393e-06 + 0.999914 * (_ctx_2048t + 0.3 * jax.random.normal(jax.random.fold_in(_rk, 611), (8, 128, 256), jnp.float32))
        itok_BxS_0_1023 = jax.random.randint(jax.random.fold_in(_rk, 12), (8, 128), 0, 128, jnp.int32)
        pos_BxS2 = jnp.broadcast_to(jnp.arange(128, dtype=jnp.int32), (8, 128))
        itok_BxS_4096_4607 = jax.random.randint(jax.random.fold_in(_rk, 14), (8, 128), 512, 576, jnp.int32)
        return (x, ctx_2048, itok_BxS_0_1023, pos_BxS2, itok_BxS_4096_4607)
    x, ctx_2048, itok_BxS_0_1023, pos_BxS2, itok_BxS_4096_4607 = _rec_inputs()

    def _L0_attn_setup():
        import jax, jax.numpy as jnp
        import numpy as np
        B, S, HID = (2, 256, 256)
        NH, DN, DR, DV, RANK = (16, 128, 64, 128, 64)
        DQK = DN + DR
        SCALE = DQK ** (-0.5)
        EPS = 1e-05

        def _rope(x, theta):
            x1, x2 = (x[..., 0::2], x[..., 1::2])
            c, s = (jnp.cos(theta), jnp.sin(theta))
            return jnp.stack([x1 * c - x2 * s, x1 * s + x2 * c], axis=-1).reshape(x.shape)

        def _layernorm(x, gamma, beta):
            mu = jnp.mean(x, axis=-1, keepdims=True)
            var = jnp.var(x, axis=-1, keepdims=True)
            return (x - mu) * jax.lax.rsqrt(var + EPS) * gamma + beta
        key = jax.random.key(seed)
        ks = jax.random.split(key, 8)

        def xavier(k, fan_in, fan_out, gain=1.0):
            lim = gain * np.sqrt(6.0 / (fan_in + fan_out))
            return jax.random.uniform(k, (fan_in, fan_out), jnp.float32, -lim, lim)
        return {'hidden_states': jax.random.normal(ks[0], (B, S, HID), jnp.float32), 'freqs_cis': jax.random.uniform(ks[1], (S, DR // 2), jnp.float32) * 2.0 * np.pi, 'Wq': xavier(ks[2], HID, NH * DQK), 'Wkv_a': xavier(ks[3], HID, RANK + DR), 'kv_gamma': jnp.ones((RANK,), jnp.float32), 'kv_beta': jnp.zeros((RANK,), jnp.float32), 'Wkv_b': xavier(ks[4], RANK, NH * (DN + DV)), 'Wout': xavier(ks[5], NH * DV, HID, gain=1.0 / np.sqrt(2.0))}
    _L0_attn_all = _L0_attn_setup()
    _L0_attn_in = {k: v for k, v in _L0_attn_all.items() if k in ('freqs_cis', 'Wq', 'Wkv_a', 'kv_gamma', 'kv_beta', 'Wkv_b', 'Wout')}
    del _L0_attn_all

    def _L0_xattn_setup():
        import jax, jax.numpy as jnp
        import numpy as np
        B, Lq, Lk = (2, 512, 128)
        Q_DIM, KV_DIM = (256, 256)
        H, HD = (16, 128)
        KVC, QC, R = (64, 96, 64)
        LOOKBACK = 8
        NEG = -1e+30

        def _rope(x, L):
            half = x.shape[-1] // 2
            inv_freq = 1.0 / 10000.0 ** (jnp.arange(half, dtype=jnp.float32) / half)
            ang = jnp.arange(L, dtype=jnp.float32)[:, None] * inv_freq
            cos, sin = (jnp.cos(ang), jnp.sin(ang))
            x1, x2 = (x[..., :half], x[..., half:])
            return jnp.concatenate([x1 * cos - x2 * sin, x1 * sin + x2 * cos], axis=-1)
        key = jax.random.key(seed)
        ks = jax.random.split(key, 11)

        def w(k, shape, fan_in):
            return jax.random.normal(k, shape, jnp.float32) / np.sqrt(fan_in).astype(np.float32)
        return {'q': jax.random.normal(ks[0], (B, Lq, Q_DIM), jnp.float32), 'kv': jax.random.normal(ks[1], (B, Lk, KV_DIM), jnp.float32), 'seg_id': jnp.sort(jax.random.randint(ks[2], (B, Lq), 0, Lk), axis=-1), 'W_kvc': w(ks[3], (KV_DIM, KVC), KV_DIM), 'W_dq': w(ks[4], (Q_DIM, QC), Q_DIM), 'W_uq': w(ks[5], (QC, H * HD), QC), 'W_qr': w(ks[6], (QC, H * R), QC), 'W_uk': w(ks[7], (KVC, H * HD), KVC), 'W_kr': w(ks[8], (KVC, R), KVC), 'W_uv': w(ks[9], (KVC, H * HD), KVC), 'W_o': w(ks[10], (H * HD, Q_DIM), H * HD)}
    _L0_xattn_all = _L0_xattn_setup()
    _L0_xattn_in = {k: v for k, v in _L0_xattn_all.items() if k in ('W_kvc', 'W_dq', 'W_uq', 'W_qr', 'W_uk', 'W_kr', 'W_uv', 'W_o')}
    del _L0_xattn_all

    def _L0_ffn_setup():
        import jax, jax.numpy as jnp
        import numpy as np
        ALPHA = 1.702
        LIMIT = 7.0
        EPS = 1e-05
        TOP_K = 4
        key = jax.random.key(seed)
        ks = jax.random.split(key, 8)
        B, S, H, I, E = (2, 64, 256, 256, 16)
        return {'x': jax.random.normal(ks[0], (B, S, H), jnp.float32), 'norm_w': jnp.ones((H,), jnp.float32), 'gate_w': jax.random.normal(ks[1], (E, H), jnp.float32) * 0.02, 'gate_b': jax.random.normal(ks[2], (E,), jnp.float32) * 0.02, 'w1': jax.random.normal(ks[3], (E, 2 * I, H), jnp.float32) * 0.02, 'b1': jax.random.normal(ks[4], (E, 2 * I), jnp.float32) * 0.02, 'w2': jax.random.normal(ks[5], (E, H, I), jnp.float32) * 0.02, 'b2': jax.random.normal(ks[6], (E, H), jnp.float32) * 0.02}
    _L0_ffn_all = _L0_ffn_setup()
    _L0_ffn_in = {k: v for k, v in _L0_ffn_all.items() if k in ('norm_w', 'gate_w', 'gate_b', 'w1', 'b1', 'w2', 'b2')}
    del _L0_ffn_all

    def _L1_attn_setup():
        import jax, jax.numpy as jnp
        import numpy as np
        from jax import lax
        key = jax.random.key(seed)
        ks = jax.random.split(key, 8)
        B, L, H = (2, 128, 256)
        E = 2
        d = H * E
        S = 16
        R = 128
        sc = lambda fan_in: 1.0 / np.sqrt(fan_in)
        return {'x': jax.random.normal(ks[0], (B, L, H), jnp.float32), 'W_in': jax.random.normal(ks[1], (H, 2 * d), jnp.float32) * sc(H), 'conv_w': jax.random.normal(ks[2], (d, 1, 3), jnp.float32) * sc(3), 'conv_b': jnp.zeros((d,), jnp.float32), 'W_x': jax.random.normal(ks[3], (d, R + 2 * S), jnp.float32) * sc(d), 'W_dt': jax.random.normal(ks[4], (R, d), jnp.float32) * sc(R), 'b_dt': jnp.zeros((d,), jnp.float32), 'A_log': jnp.log(jnp.tile(jnp.arange(1, S + 1, dtype=jnp.float32), (d, 1))), 'D': jnp.ones((d,), jnp.float32), 'W_out': jax.random.normal(ks[5], (d, H), jnp.float32) * sc(d)}
    _L1_attn_all = _L1_attn_setup()
    _L1_attn_in = {k: v for k, v in _L1_attn_all.items() if k in ('W_in', 'conv_w', 'conv_b', 'W_x', 'W_dt', 'b_dt', 'A_log', 'D', 'W_out')}
    del _L1_attn_all

    def _L1_xattn_setup():
        import jax, jax.numpy as jnp
        import numpy as np
        B, CTX, DRAFT, D = (2, 512, 64, 256)
        H, KVH, HD = (16, 4, 128)
        N_REP = H // KVH
        EPS = 1e-06
        THETA = 10000.0
        SCALE = 1.0 / np.sqrt(HD).astype(np.float32)

        def _rms_norm(x, w):
            v = jnp.mean(jnp.square(x.astype(jnp.float32)), axis=-1, keepdims=True)
            return (w * (x.astype(jnp.float32) * jax.lax.rsqrt(v + EPS))).astype(x.dtype)

        def _rotate_half(x):
            x1, x2 = jnp.split(x, 2, axis=-1)
            return jnp.concatenate((-x2, x1), axis=-1)

        def _rope(x, pos):
            inv_freq = 1.0 / THETA ** (jnp.arange(0, HD, 2, dtype=jnp.float32) / HD)
            freqs = pos.astype(jnp.float32)[:, None, :, None] * inv_freq
            emb = jnp.concatenate((freqs, freqs), axis=-1)
            return x * jnp.cos(emb) + _rotate_half(x) * jnp.sin(emb)
        key = jax.random.key(seed)
        ks = jax.random.split(key, 6)
        return {'draft_hidden': jax.random.normal(ks[0], (B, DRAFT, D), jnp.float32), 'context_hidden': jax.random.normal(ks[1], (B, CTX, D), jnp.float32), 'Wq': jax.random.normal(ks[2], (H * HD, D), jnp.float32) * 0.02, 'Wk': jax.random.normal(ks[3], (KVH * HD, D), jnp.float32) * 0.02, 'Wv': jax.random.normal(ks[4], (KVH * HD, D), jnp.float32) * 0.02, 'Wo': jax.random.normal(ks[5], (D, H * HD), jnp.float32) * 0.02, 'q_norm_w': jnp.ones((HD,), jnp.float32), 'k_norm_w': jnp.ones((HD,), jnp.float32), 'context_position_ids': jnp.broadcast_to(jnp.arange(CTX, dtype=jnp.int32), (B, CTX)), 'draft_position_ids': jnp.broadcast_to(CTX + jnp.arange(DRAFT, dtype=jnp.int32), (B, DRAFT))}
    _L1_xattn_all = _L1_xattn_setup()
    _L1_xattn_in = {k: v for k, v in _L1_xattn_all.items() if k in ('Wq', 'Wk', 'Wv', 'Wo', 'q_norm_w', 'k_norm_w')}
    del _L1_xattn_all

    def _L1_ffn_setup():
        import jax, jax.numpy as jnp
        import numpy as np
        HIDDEN = 256
        INTER = 1024
        SCALE = 64.0

        def fwht(x):
            orig_shape = x.shape
            n = orig_shape[-1]
            x = x.reshape(-1, n)
            h = 1
            while h < n:
                x = x.reshape(-1, n // (2 * h), 2, h)
                a, b = (x[:, :, 0, :], x[:, :, 1, :])
                x = jnp.stack([a + b, a - b], axis=2).reshape(-1, n)
                h *= 2
            return (x / jnp.sqrt(jnp.asarray(n, x.dtype))).reshape(orig_shape)
        key = jax.random.key(seed)
        ks = jax.random.split(key, 8)
        inp = jax.random.normal(ks[0], (4, 256, HIDDEN), dtype=jnp.float32)
        SU_ug = jnp.where(jax.random.bernoulli(ks[1], 0.5, (HIDDEN,)), 1.0, -1.0).astype(jnp.float32)
        SU_dp = jnp.where(jax.random.bernoulli(ks[2], 0.5, (INTER,)), 1.0, -1.0).astype(jnp.float32)
        Wscale_ug = jax.random.uniform(ks[3], (2 * INTER,), jnp.float32, 0.5, 1.5)
        Wscale_dp = jax.random.uniform(ks[4], (HIDDEN,), jnp.float32, 0.5, 1.5)
        W_up = jax.random.normal(ks[5], (INTER, HIDDEN), dtype=jnp.float32) * 0.02
        W_gate = jax.random.normal(ks[6], (INTER, HIDDEN), dtype=jnp.float32) * 0.02
        W_down = jax.random.normal(ks[7], (HIDDEN, INTER), dtype=jnp.float32) * 0.02
        return {'input': inp, 'SU_ug': SU_ug, 'SU_dp': SU_dp, 'Wscale_ug': Wscale_ug, 'Wscale_dp': Wscale_dp, 'W_up': W_up, 'W_gate': W_gate, 'W_down': W_down}
    _L1_ffn_all = _L1_ffn_setup()
    _L1_ffn_in = {k: v for k, v in _L1_ffn_all.items() if k in ('SU_ug', 'SU_dp', 'Wscale_ug', 'Wscale_dp', 'W_up', 'W_gate', 'W_down')}
    del _L1_ffn_all
    return {'x': x, 'ctx_2048': ctx_2048, 'itok_BxS_0_1023': itok_BxS_0_1023, 'pos_BxS2': pos_BxS2, 'itok_BxS_4096_4607': itok_BxS_4096_4607, 'L0_attn_freqs_cis': _L0_attn_in['freqs_cis'], 'L0_attn_Wq': _L0_attn_in['Wq'], 'L0_attn_Wkv_a': _L0_attn_in['Wkv_a'], 'L0_attn_kv_gamma': _L0_attn_in['kv_gamma'], 'L0_attn_kv_beta': _L0_attn_in['kv_beta'], 'L0_attn_Wkv_b': _L0_attn_in['Wkv_b'], 'L0_attn_Wout': _L0_attn_in['Wout'], 'L0_xattn_W_kvc': _L0_xattn_in['W_kvc'], 'L0_xattn_W_dq': _L0_xattn_in['W_dq'], 'L0_xattn_W_uq': _L0_xattn_in['W_uq'], 'L0_xattn_W_qr': _L0_xattn_in['W_qr'], 'L0_xattn_W_uk': _L0_xattn_in['W_uk'], 'L0_xattn_W_kr': _L0_xattn_in['W_kr'], 'L0_xattn_W_uv': _L0_xattn_in['W_uv'], 'L0_xattn_W_o': _L0_xattn_in['W_o'], 'L0_ffn_norm_w': _L0_ffn_in['norm_w'], 'L0_ffn_gate_w': _L0_ffn_in['gate_w'], 'L0_ffn_gate_b': _L0_ffn_in['gate_b'], 'L0_ffn_w1': _L0_ffn_in['w1'], 'L0_ffn_b1': _L0_ffn_in['b1'], 'L0_ffn_w2': _L0_ffn_in['w2'], 'L0_ffn_b2': _L0_ffn_in['b2'], 'L1_attn_W_in': _L1_attn_in['W_in'], 'L1_attn_conv_w': _L1_attn_in['conv_w'], 'L1_attn_conv_b': _L1_attn_in['conv_b'], 'L1_attn_W_x': _L1_attn_in['W_x'], 'L1_attn_W_dt': _L1_attn_in['W_dt'], 'L1_attn_b_dt': _L1_attn_in['b_dt'], 'L1_attn_A_log': _L1_attn_in['A_log'], 'L1_attn_D': _L1_attn_in['D'], 'L1_attn_W_out': _L1_attn_in['W_out'], 'L1_xattn_Wq': _L1_xattn_in['Wq'], 'L1_xattn_Wk': _L1_xattn_in['Wk'], 'L1_xattn_Wv': _L1_xattn_in['Wv'], 'L1_xattn_Wo': _L1_xattn_in['Wo'], 'L1_xattn_q_norm_w': _L1_xattn_in['q_norm_w'], 'L1_xattn_k_norm_w': _L1_xattn_in['k_norm_w'], 'L1_ffn_SU_ug': _L1_ffn_in['SU_ug'], 'L1_ffn_SU_dp': _L1_ffn_in['SU_dp'], 'L1_ffn_Wscale_ug': _L1_ffn_in['Wscale_ug'], 'L1_ffn_Wscale_dp': _L1_ffn_in['Wscale_dp'], 'L1_ffn_W_up': _L1_ffn_in['W_up'], 'L1_ffn_W_gate': _L1_ffn_in['W_gate'], 'L1_ffn_W_down': _L1_ffn_in['W_down']}

def reference(x, ctx_2048, itok_BxS_0_1023, pos_BxS2, itok_BxS_4096_4607, L0_attn_freqs_cis, L0_attn_Wq, L0_attn_Wkv_a, L0_attn_kv_gamma, L0_attn_kv_beta, L0_attn_Wkv_b, L0_attn_Wout, L0_xattn_W_kvc, L0_xattn_W_dq, L0_xattn_W_uq, L0_xattn_W_qr, L0_xattn_W_uk, L0_xattn_W_kr, L0_xattn_W_uv, L0_xattn_W_o, L0_ffn_norm_w, L0_ffn_gate_w, L0_ffn_gate_b, L0_ffn_w1, L0_ffn_b1, L0_ffn_w2, L0_ffn_b2, L1_attn_W_in, L1_attn_conv_w, L1_attn_conv_b, L1_attn_W_x, L1_attn_W_dt, L1_attn_b_dt, L1_attn_A_log, L1_attn_D, L1_attn_W_out, L1_xattn_Wq, L1_xattn_Wk, L1_xattn_Wv, L1_xattn_Wo, L1_xattn_q_norm_w, L1_xattn_k_norm_w, L1_ffn_SU_ug, L1_ffn_SU_dp, L1_ffn_Wscale_ug, L1_ffn_Wscale_dp, L1_ffn_W_up, L1_ffn_W_gate, L1_ffn_W_down):
    import jax
    import jax.numpy as jnp

    def _L0_attn_ref(hidden_states, freqs_cis, Wq, Wkv_a, kv_gamma, kv_beta, Wkv_b, Wout):
        import jax, jax.numpy as jnp
        import numpy as np
        B, S, HID = (2, 256, 256)
        NH, DN, DR, DV, RANK = (16, 128, 64, 128, 64)
        DQK = DN + DR
        SCALE = DQK ** (-0.5)
        EPS = 1e-05

        def _rope(x, theta):
            x1, x2 = (x[..., 0::2], x[..., 1::2])
            c, s = (jnp.cos(theta), jnp.sin(theta))
            return jnp.stack([x1 * c - x2 * s, x1 * s + x2 * c], axis=-1).reshape(x.shape)

        def _layernorm(x, gamma, beta):
            mu = jnp.mean(x, axis=-1, keepdims=True)
            var = jnp.var(x, axis=-1, keepdims=True)
            return (x - mu) * jax.lax.rsqrt(var + EPS) * gamma + beta
        b, s, _ = hidden_states.shape
        max_len = freqs_cis.shape[0]
        pos = jnp.arange(s) % max_len
        theta = freqs_cis[pos]
        q = (hidden_states @ Wq).reshape(b, s, NH, DQK)
        q_nope, q_rope = (q[..., :DN], q[..., DN:])
        q_rope = _rope(q_rope, theta[None, :, None, :])
        kv = hidden_states @ Wkv_a
        kv_c, k_rope = (kv[..., :RANK], kv[..., RANK:])
        k_rope = _rope(k_rope, theta[None, :, :])
        kv_c = _layernorm(kv_c, kv_gamma, kv_beta)
        kvb = (kv_c @ Wkv_b).reshape(b, s, NH, DN + DV)
        k_nope, v = (kvb[..., :DN], kvb[..., DN:])
        k = jnp.concatenate([k_nope, jnp.broadcast_to(k_rope[:, :, None, :], (b, s, NH, DR))], axis=-1)
        q = jnp.concatenate([q_nope, q_rope], axis=-1)
        scores = jnp.einsum('bthd,bshd->btsh', q, k) * SCALE
        weights = jax.nn.softmax(scores.astype(jnp.float32), axis=2).astype(q.dtype)
        attn = jnp.einsum('btsh,bshd->bthd', weights, v).reshape(b, s, NH * DV)
        return attn @ Wout

    def _L0_xattn_ref(q, kv, seg_id, W_kvc, W_dq, W_uq, W_qr, W_uk, W_kr, W_uv, W_o):
        import jax, jax.numpy as jnp
        import numpy as np
        B, Lq, Lk = (2, 512, 128)
        Q_DIM, KV_DIM = (256, 256)
        H, HD = (16, 128)
        KVC, QC, R = (64, 96, 64)
        LOOKBACK = 8
        NEG = -1e+30

        def _rope(x, L):
            half = x.shape[-1] // 2
            inv_freq = 1.0 / 10000.0 ** (jnp.arange(half, dtype=jnp.float32) / half)
            ang = jnp.arange(L, dtype=jnp.float32)[:, None] * inv_freq
            cos, sin = (jnp.cos(ang), jnp.sin(ang))
            x1, x2 = (x[..., :half], x[..., half:])
            return jnp.concatenate([x1 * cos - x2 * sin, x1 * sin + x2 * cos], axis=-1)
        b, lq, _ = q.shape
        lk = kv.shape[1]
        kv_c = kv @ W_kvc
        q_c = q @ W_dq
        q_nope = (q_c @ W_uq).reshape(b, lq, H, HD).transpose(0, 2, 1, 3)
        q_rope = (q_c @ W_qr).reshape(b, lq, H, R).transpose(0, 2, 1, 3)
        k_nope = (kv_c @ W_uk).reshape(b, lk, H, HD)
        v = (kv_c @ W_uv).reshape(b, lk, H, HD)
        k_rope = kv_c @ W_kr
        q_rope = _rope(q_rope, lq)
        k_rope = _rope(k_rope, lk)
        scale = 1.0 / np.sqrt(HD + R).astype(np.float32)
        scores = (jnp.einsum('bhqd,bkhd->bhqk', q_nope, k_nope) + jnp.einsum('bhqr,bkr->bhqk', q_rope, k_rope)) * scale
        k_ids = jnp.arange(lk)[None, None, :]
        qs = seg_id[:, :, None]
        good = (k_ids <= qs) & (k_ids >= qs - LOOKBACK)
        scores = jnp.where(good[:, None, :, :], scores, NEG)
        attn = jax.nn.softmax(scores, axis=-1)
        out = jnp.einsum('bhqk,bkhd->bqhd', attn, v).reshape(b, lq, H * HD)
        return out @ W_o

    def _L0_ffn_ref(x, norm_w, gate_w, gate_b, w1, b1, w2, b2):
        import jax, jax.numpy as jnp
        import numpy as np
        ALPHA = 1.702
        LIMIT = 7.0
        EPS = 1e-05
        TOP_K = 4
        B, S, H = x.shape
        M = B * S
        E = gate_w.shape[0]
        xf = x.reshape(M, H)
        t = xf * jax.lax.rsqrt(jnp.mean(xf * xf, axis=-1, keepdims=True) + EPS) * norm_w
        logits = t @ gate_w.T + gate_b
        vals, idx = jax.lax.top_k(logits, TOP_K)
        gates_k = jax.nn.softmax(vals, axis=-1)
        G = jnp.zeros((M, E), x.dtype).at[jnp.arange(M)[:, None], idx].set(gates_k)
        h = jnp.einsum('mh,eoh->emo', t, w1) + b1[:, None, :]
        a = jnp.minimum(h[..., ::2], LIMIT)
        b = jnp.clip(h[..., 1::2], -LIMIT, LIMIT)
        act = a * jax.nn.sigmoid(ALPHA * a) * (b + 1.0)
        y = jnp.einsum('emi,edi->emd', act, w2) + b2[:, None, :]
        delta = jnp.einsum('me,emd->md', G, y)
        return x + delta.reshape(B, S, H)

    def _L1_attn_ref(x, W_in, conv_w, conv_b, W_x, W_dt, b_dt, A_log, D, W_out):
        import jax, jax.numpy as jnp
        import numpy as np
        from jax import lax
        d = conv_b.shape[0]
        S = A_log.shape[1]
        R = W_dt.shape[0]
        xz = x @ W_in
        xp, z = jnp.split(xz, 2, axis=-1)
        xc = lax.conv_general_dilated(jnp.transpose(xp, (0, 2, 1)), conv_w, (1,), [(1, 1)], feature_group_count=d, dimension_numbers=('NCH', 'OIH', 'NCH'))
        xc = jnp.transpose(xc + conv_b[None, :, None], (0, 2, 1))
        xc = jax.nn.silu(xc)
        x_dbl = xc @ W_x
        dt_in = x_dbl[..., :R]
        Bm = x_dbl[..., R:R + S]
        Cm = x_dbl[..., R + S:]
        dt = jax.nn.softplus(dt_in @ W_dt + b_dt)
        A = -jnp.exp(A_log)

        def step(h, ins):
            u_t, dt_t, B_t, C_t = ins
            dA = jnp.exp(dt_t[:, :, None] * A)
            h = dA * h + dt_t[:, :, None] * B_t[:, None, :] * u_t[:, :, None]
            y_t = jnp.einsum('bds,bs->bd', h, C_t)
            return (h, y_t)
        h0 = jnp.zeros((x.shape[0], d, S), xc.dtype)
        xsT = (jnp.swapaxes(xc, 0, 1), jnp.swapaxes(dt, 0, 1), jnp.swapaxes(Bm, 0, 1), jnp.swapaxes(Cm, 0, 1))
        _, yT = lax.scan(step, h0, xsT)
        y = jnp.swapaxes(yT, 0, 1) + xc * D
        y = y * jax.nn.silu(z)
        return y @ W_out

    def _L1_xattn_ref(draft_hidden, context_hidden, Wq, Wk, Wv, Wo, q_norm_w, k_norm_w, context_position_ids, draft_position_ids):
        import jax, jax.numpy as jnp
        import numpy as np
        B, CTX, DRAFT, D = (2, 512, 64, 256)
        H, KVH, HD = (16, 4, 128)
        N_REP = H // KVH
        EPS = 1e-06
        THETA = 10000.0
        SCALE = 1.0 / np.sqrt(HD).astype(np.float32)

        def _rms_norm(x, w):
            v = jnp.mean(jnp.square(x.astype(jnp.float32)), axis=-1, keepdims=True)
            return (w * (x.astype(jnp.float32) * jax.lax.rsqrt(v + EPS))).astype(x.dtype)

        def _rotate_half(x):
            x1, x2 = jnp.split(x, 2, axis=-1)
            return jnp.concatenate((-x2, x1), axis=-1)

        def _rope(x, pos):
            inv_freq = 1.0 / THETA ** (jnp.arange(0, HD, 2, dtype=jnp.float32) / HD)
            freqs = pos.astype(jnp.float32)[:, None, :, None] * inv_freq
            emb = jnp.concatenate((freqs, freqs), axis=-1)
            return x * jnp.cos(emb) + _rotate_half(x) * jnp.sin(emb)
        bsz, draft_len, _ = draft_hidden.shape
        ctx_len = context_hidden.shape[1]
        total_len = ctx_len + draft_len
        q = (draft_hidden @ Wq.T).reshape(bsz, draft_len, H, HD)
        q = _rms_norm(q, q_norm_w).transpose(0, 2, 1, 3)
        kv_in = jnp.concatenate([context_hidden, draft_hidden], axis=1)
        k = (kv_in @ Wk.T).reshape(bsz, total_len, KVH, HD)
        v = (kv_in @ Wv.T).reshape(bsz, total_len, KVH, HD).transpose(0, 2, 1, 3)
        k = _rms_norm(k, k_norm_w).transpose(0, 2, 1, 3)
        full_position_ids = jnp.concatenate([context_position_ids, draft_position_ids], axis=1)
        q = _rope(q, draft_position_ids)
        k = _rope(k, full_position_ids)
        k = jnp.repeat(k, N_REP, axis=1)
        v = jnp.repeat(v, N_REP, axis=1)
        scores = jnp.einsum('bhqd,bhkd->bhqk', q, k) * SCALE
        probs = jax.nn.softmax(scores, axis=-1)
        attn = jnp.einsum('bhqk,bhkd->bhqd', probs, v)
        attn = attn.transpose(0, 2, 1, 3).reshape(bsz, draft_len, H * HD)
        return attn @ Wo.T

    def _L1_ffn_ref(input, SU_ug, SU_dp, Wscale_ug, Wscale_dp, W_up, W_gate, W_down):
        import jax, jax.numpy as jnp
        import numpy as np
        HIDDEN = 256
        INTER = 1024
        SCALE = 64.0

        def fwht(x):
            orig_shape = x.shape
            n = orig_shape[-1]
            x = x.reshape(-1, n)
            h = 1
            while h < n:
                x = x.reshape(-1, n // (2 * h), 2, h)
                a, b = (x[:, :, 0, :], x[:, :, 1, :])
                x = jnp.stack([a + b, a - b], axis=2).reshape(-1, n)
                h *= 2
            return (x / jnp.sqrt(jnp.asarray(n, x.dtype))).reshape(orig_shape)
        n = SU_ug.shape[0]
        x = input.reshape(-1, n)
        x = fwht(x * SU_ug) / SCALE
        x_up = x @ W_up.T * (Wscale_ug[:INTER] * SCALE)
        x_gate = x @ W_gate.T * (Wscale_ug[INTER:] * SCALE)
        x = jax.nn.silu(x_gate) * x_up
        x = fwht(x * SU_dp) / SCALE
        x = x @ W_down.T * (Wscale_dp * SCALE)
        return x.reshape(input.shape)
    x = _layernorm(x + _L0_attn_ref(x, L0_attn_freqs_cis, L0_attn_Wq, L0_attn_Wkv_a, L0_attn_kv_gamma, L0_attn_kv_beta, L0_attn_Wkv_b, L0_attn_Wout), axis=-1)
    x = _layernorm(x + _L0_xattn_ref(x, ctx_2048, itok_BxS_0_1023, L0_xattn_W_kvc, L0_xattn_W_dq, L0_xattn_W_uq, L0_xattn_W_qr, L0_xattn_W_uk, L0_xattn_W_kr, L0_xattn_W_uv, L0_xattn_W_o), axis=-1)
    x = _layernorm(x + _L0_ffn_ref(x, L0_ffn_norm_w, L0_ffn_gate_w, L0_ffn_gate_b, L0_ffn_w1, L0_ffn_b1, L0_ffn_w2, L0_ffn_b2), axis=-1)
    x = _layernorm(x + _L1_attn_ref(x, L1_attn_W_in, L1_attn_conv_w, L1_attn_conv_b, L1_attn_W_x, L1_attn_W_dt, L1_attn_b_dt, L1_attn_A_log, L1_attn_D, L1_attn_W_out), axis=-1)
    x = _layernorm(x + _L1_xattn_ref(x, ctx_2048, L1_xattn_Wq, L1_xattn_Wk, L1_xattn_Wv, L1_xattn_Wo, L1_xattn_q_norm_w, L1_xattn_k_norm_w, pos_BxS2, itok_BxS_4096_4607), axis=-1)
    x = _layernorm(x + _L1_ffn_ref(x, L1_ffn_SU_ug, L1_ffn_SU_dp, L1_ffn_Wscale_ug, L1_ffn_Wscale_dp, L1_ffn_W_up, L1_ffn_W_gate, L1_ffn_W_down), axis=-1)
    return x

_drawn_inputs = setup_inputs


def setup_inputs(seed=0):
    import zlib

    import numpy as np

    out = dict(_drawn_inputs(seed))
    spreads = {'L0_attn_kv_gamma': (1.0, 0.6),
     'L0_attn_kv_beta': (0.0, 0.361),
     'L0_ffn_norm_w': (1.0, 0.6),
     'L1_attn_conv_b': (0.0, 0.1),
     'L1_attn_b_dt': (0.0, 0.341),
     'L1_attn_D': (1.0, 0.2),
     'L1_xattn_q_norm_w': (1.0, 0.6),
     'L1_xattn_k_norm_w': (1.0, 0.6)}
    factors = {'L0_attn_freqs_cis': 8.0,
     'L0_attn_Wq': 8.0,
     'L0_attn_Wkv_a': 3.151,
     'L0_ffn_gate_w': 3.193,
     'L0_ffn_gate_b': 8.0,
     'L0_ffn_w1': 2.879,
     'L0_ffn_b1': 8.0,
     'L0_ffn_w2': 2.831,
     'L0_ffn_b2': 8.0,
     'L1_ffn_Wscale_ug': 4.009,
     'L1_ffn_Wscale_dp': 5.536}
    for name, (base, spread) in spreads.items():
        noise = np.random.default_rng([zlib.crc32(name.encode()), seed]).standard_normal(out[name].shape)
        drawn = base * np.exp(spread * noise) if base else spread * noise
        out[name] = jnp.asarray(drawn.astype(out[name].dtype))
    for name, factor in factors.items():
        out[name] = (out[name] * factor).astype(out[name].dtype)
    return out
```

```python
from contextlib import ExitStack

import concourse.bass as bass
from concourse import mybir

F32 = mybir.dt.float32
F32R = mybir.dt.float32r
I32 = mybir.dt.int32
ALU = mybir.AluOpType
ACT = mybir.ActivationFunctionType
AX_X = mybir.AxisListType.X

P = 128
NB = 8
D = 256
KD = D // P
NT = NB * P
NH = 16
HG = 4
NG = NH // HG
RK = 64
RR = 64
DH = 128
QC = 96
NE = 16
TOPK = 4
DI = 512
MD = DI // P
NS = 16
DTR = 128
KVH = 4
FF = 1024
NF = FF // P
LN_EPS = 1e-5
RMS_EPS = 1e-6
CHUNK = 512
NC_ = NT // CHUNK
FINAL = ("F_ln", 8)
CREDIT = 6

PI = 3.14159265358979
TWO_PI_HI = 6.28125
TWO_PI_MID = 0.0019350051879882812
TWO_PI_LO = 2 * PI - TWO_PI_HI - TWO_PI_MID
ROUND = 12582912.0
PI_SAFE = 3.1415925


GROUPS = NB * NG
ATTEND = dict(xt=NB + 1, q=GROUPS + 1, tq=GROUPS, sc=GROUPS, tp=GROUPS, pv=GROUPS, to=GROUPS, y=NB, xs=NB + 1,
              qabs=GROUPS + 1, qt=GROUPS, exp=GROUPS, ot=GROUPS, rs=2 * NB, u=GROUPS + 1, rope=GROUPS + 1, max=GROUPS,
              pt=GROUPS, on=GROUPS, ln=NB, lna=NB, xb=NB + 1, band=GROUPS)
EVENTS = {
    "A": dict(ATTEND, v=4 * NB, sm=GROUPS, kvp=1, kvt=1, kvr=2, kvc=2, kve=1),
    "B": dict(ATTEND, v=2 * NB, sm=2 * GROUPS, kvp=1, kvt=1, kvr=2, kvc=2, kve=1),
    "C": dict(y=2 * NE, rs=2, ln=NB),
    "K": dict(xt=NB, xs=NB, rs=4 * NB, u=2 * NB, xb=NB, q=2 * NB, pv=2 * NB, tab=NB, ss=2 * NB),
    "D": dict(xt=NB, xT=4, ln=NB, m=NC_, st=9 * NC_, rs=2 * NC_, o=NC_),
}
SHARED = {"A": "ABCKE", "B": "ABCKE", "C": "ABCKE", "K": "ABCKE", "E": "ABCKE", "D": "DF", "F": "DF"}


def physical(name):
    st, _, n = name.partition("_")
    order = SHARED.get(st, st)
    for first in order[:order.index(st)]:
        if n in EVENTS[first]:
            return f"{first}_{n}"
    return name


def at(name, n):
    st, _, short = name.partition("_")
    order = SHARED.get(st, st)
    return n + CREDIT + sum(EVENTS[x].get(short, 0) for x in order[:order.index(st)])


def build(nc, a, out):
    ctx = ExitStack()
    with ctx:
        sems = {}

        def sem(name):
            name = physical(name)
            if name not in sems:
                sems[name] = ctx.enter_context(nc.semaphore(name))
            return sems[name]

        def sb(name, shape, dt=F32):
            return ctx.enter_context(nc.sbuf_tensor(f"{name}_sb", shape, dt))

        X = sb("X", [P, NB + 1, D])
        consts = sb("consts", [P, 3 * P])
        ident, hadamard, key_ids = consts[:, 0:P], consts[:, P:2 * P], consts[:, 2 * P:3 * P]
        small = sb("small", [P, 2256])
        angles = sb("angles", [P, 32 + 2 * NB * 64])
        cosines = sb("cosines", [P, 32 + 2 * NB * 64])
        sines = sb("sines", [P, 32 + 2 * NB * 64])
        AREA_0, AREA_G, AREA_1, AREA_2 = 10240, 16640, 24320, 28800

        def parts(start, n):
            with nc.sbuf_tensor(f"before_{start}_sb", [P, start], F32), \
                    nc.sbuf_tensor(f"parts_{start}_sb", [P, n], F32R) as t:
                return t[:, :]

        at_tT, at_w1, at_w2, at_act = AREA_2 + 2048, AREA_1, AREA_2 + 10880, AREA_2 + 7168
        tT_hi_parts, tT_lo_parts = parts(at_tT, KD * NT), parts(AREA_0 + 3360, KD * NT)
        expert_parts = [parts(start, KD * 2 * (512 + D)) for start in (at_w1, at_w2)]
        act_hi_parts, act_lo_parts = parts(at_act, 4 * CHUNK), parts(AREA_G + 4224, 4 * CHUNK)
        area = sb("area", [P, 42760])
        area_f, area_0 = area[:, 0:10240], area[:, 10240:16640]
        area_g, area_1, area_2 = area[:, 16640:24320], area[:, 24320:28800], area[:, 28800:42760]
        PS = ctx.enter_context(nc.psum_tensor("PS", [P, 8, 512], F32))

        def place(area, start, *shape):
            n = 1
            for k in shape:
                n *= k
            v = area[:, start:start + n]
            if len(shape) == 2:
                v = v.rearrange("p (a b) -> p a b", a=shape[0])
            if len(shape) == 3:
                v = v.rearrange("p (a b c) -> p a b c", a=shape[0], b=shape[1])
            return v

        def bank(i, *shape):
            v = PS[:, i, :]
            n = 1
            for k in shape:
                n *= k
            v = PS[:, i, 0:n]
            if len(shape) == 2:
                v = v.rearrange("p (a b) -> p a b", a=shape[0])
            if len(shape) == 3:
                v = v.rearrange("p (a b c) -> p a b c", a=shape[0], b=shape[1])
            return v

        used = [0]

        def little(*shape):
            n = 1
            for k in shape:
                n *= k
            v = place(small, used[0], *shape)
            used[0] += n
            assert used[0] <= 2256
            return v

        gamma, beta = little(64), little(64)
        norm_w, gate_b = little(D), little(NE)
        qk_w = little(2, 128)
        inv_freq = little(64)
        rope_x = little(2, 64)
        rope_0 = little(2, 64)
        seg = little(NB)
        eps_ln, eps_rms = little(1), little(1)
        negmax = little(2, HG)
        rinv = little(2, HG)
        stats6, mv, rstd = little(6), little(2), little(1)
        stats8, mv8, rstd8 = little(NB, 6), little(NB, 2), little(NB)
        spare = little(1)
        b1 = little(NE, 4)
        gates = little(NB, NE)
        b2_bias = little(NE, 2)
        stats4, mv4, rstd4 = little(4, 6), little(4, 2), little(4)
        one = little(1)
        qk_signed = little(2, 128)
        sumsq, rms = little(2, HG), little(2, HG)
        prob_sum = little(2, HG)
        ffn_cols = little(2 * NF + KD + NF)
        wsd = little(D)
        signs16, eps_q = little(KD), little(1)
        ssm_cols = little(MD, 24)

        int_ids = ctx.enter_context(nc.sbuf_tensor("int_ids", [P, 3, NB], I32))
        float_ids = sb("float_ids", [P, 3, NB])

        wq_nopeT = place(area_f, 0, NH, D)
        wk_upT = place(area_f, 4096, NH, RK)
        wv_upT = place(area_f, 5120, NH, RK)
        w_out = place(area_f, 6144, NH, D)
        wq0 = place(area_0, 0, KD, NH, DH)
        wkv0 = place(area_0, 4096, KD, DH)
        wo0 = place(area_0, 4352, NH // 2, D)
        wuqT = place(area_g, 0, NH, QC)
        wukT = place(area_g, 1536, NH, RK)
        wuvT = place(area_g, 2560, NH, RK)
        w_ox = place(area_g, 3584, NH, D)
        wqx = place(area_1, 0, NH, DH)
        wdq = place(area_1, 2048, KD, QC)
        wkvc = place(area_1, 2240, KD, RK)
        wkr = place(area_1, 2368, RR)
        wox = place(area_1, 2432, NH // 2, D)
        xs = place(area_2, 0, KD, P)
        q_tok = place(area_2, 256, 2, HG * DH)
        qT = place(area_2, 1280, 2, HG * P)
        prob = place(area_2, 2304, 2, HG * P)
        masked = place(area_2, 3328, 2, HG * P)
        probT = place(area_2, 4352, HG * P)
        o_norm = place(area_2, 4864, 2 * HG * RK // 2)
        oT = place(area_2, 5376, NH // 2, P)
        keyT = [place(area_2, 6400, NB, P), place(area_2, 7424, NB, P)]
        val = [place(area_2, 8448, NB, RK + 1), place(area_2, 8968, NB, RK + 1)]
        qcT = place(area_2, 9488, P)
        band = place(area_2, 9616, NB, P)
        rope_u = place(area_2, 10640, 2, HG * RR)
        rope_v = place(area_2, 11152, 2, HG * RR)
        x_now = place(area_2, 11920, D)
        k_tok = place(area_2, 256, NB, DH)
        z = place(area_2, 11664, D)
        x0T = place(area_2, 1280, KD, NT)
        ctxT_flat = sb("ctxT", [P, KD * NT])
        ctxT = place(ctxT_flat, 0, KD, NT)
        kt_tmp = place(area_2, 3328, NB, RR)

        kv_cT = place(area_2, 4352, NT)

        def place_q(slot):
            return q_tok[:, slot % 2, :].rearrange("p (h d) -> p h d", h=HG)

        V_BASE = {"A": 2 * NB, "B": 0}

        w1_e = [place(area_0, 1536 * i, KD, 512) for i in range(2)]
        w2_e = [place(area_0, 1536 * i + 1024, KD, D) for i in range(2)]
        gate_wT = place(area_0, 3072, KD, NE)
        b2_all = place(area_0, 3104, D)
        tT = place(area_2, 0, KD, NT)
        t_tok = place(area_2, 2048, NB, D)
        exact = lambda t: t.bitcast(F32)
        tT_hi, tT_hi_f = place(tT_hi_parts, 0, KD, NT), place(exact(tT_hi_parts), 0, KD, NT)
        tT_lo = place(tT_lo_parts, 0, KD, NT)
        w1_hi, w1_lo = ([place(t, start, KD, 512) for t in expert_parts] for start in (0, 1024))
        w2_hi, w2_lo = ([place(t, start, KD, D) for t in expert_parts] for start in (2048, 2560))
        w1_hi_f = [place(exact(t), 0, KD, 512) for t in expert_parts]
        w2_hi_f = [place(exact(t), 2048, KD, D) for t in expert_parts]
        act_out = place(area_1, 3072, 2, CHUNK)
        act_hi, act_hi_f = place(act_hi_parts, 0, 2, 2, CHUNK), place(exact(act_hi_parts), 0, 2, 2, CHUNK)
        act_lo = place(act_lo_parts, 0, 2, 2, CHUNK)
        act_lin = place(area_2, 4096, 2, CHUNK)
        act_up = place(area_2, 5120, 2, CHUNK)
        act_gl = place(area_2, 6144, 2, CHUNK)
        logits = place(area_2, 9216, NB, NE + TOPK)
        top8 = place(area_2, 9376, NB, 8)
        picked = place(area_2, 9440, NB, NE + TOPK)
        expl = place(area_2, 9600, NB, NE)
        gatesT = place(area_2, 9728, NT)
        gsum = place(area_2, 10752, NB)
        ssq8 = place(area_2, 10760, NB)
        w_in = place(area_g, 0, KD, 2 * DI)
        w_x = place(area_g, 2048, MD, DTR + 2 * NS)
        w_dt = place(area_g, 2688, DI)
        w_ssm = place(area_g, 3200, MD, D)
        sz = place(area_g, 4224, MD, CHUNK)
        xT = place(area_2, 0, KD, NT)
        u_c = place(area_2, 2048, MD, CHUNK)
        dt = place(area_2, 4096, MD, CHUNK)
        dtu = place(area_2, 6144, MD, CHUNK)
        yg = place(area_2, 8192, MD, CHUNK)
        sp_tmp = place(area_2, 8192, MD, CHUNK)
        bcT = place(area_2, 10240, CHUNK)
        dt_in = place(area_2, 10752, CHUNK)
        decay = place(area_2, 11264, 4, CHUNK)
        z4 = place(area_1, 0, 4, D)
        drive = place(area_1, 0, 4, CHUNK)
        state = place(area_1, 2048, 4, CHUNK)
        read_out = place(area_2, 8192, 4, CHUNK)
        b_rep = [place(area_g, 6272, CHUNK), place(area_g, 6784, CHUNK), place(area_2, 13312, CHUNK)]
        wq1 = place(area_f, 0, KD, NH * DH)
        wk1 = place(area_f, 4096, KD, KVH * DH)
        wv1 = place(area_f, 5120, KD, KVH * DH)
        wo1 = place(area_f, 6144, NH, D)
        keyT1 = area[:, 16640:16640 + 8192].rearrange("p (b g k) -> p b g k", b=NB, g=KVH)
        val1 = area[:, 24832:24832 + 8192].rearrange("p (b h n) -> p b h n", b=NB, h=2)
        area_e = area[:, 33024:42760]
        xs1 = place(area_e, 0, KD, P)
        x_now1 = place(area_e, 256, D)
        q_tok1 = place(area_e, 512, 2, HG * DH)
        k_tok1 = q_tok1
        rope_u1, rope_v1 = place(area_e, 1536, HG * DH), place(area_e, 2048, HG * DH)
        qT1 = place(area_e, 2560, 2, HG * P)
        probs1 = place(area_e, 3584, 2, HG * 2 * P)
        probT1 = place(area_e, 5632, 2, HG * P)
        squares = probT1
        o_norm1 = place(area_e, 6656, HG * DH)
        oT1 = place(area_e, 7168, NH, P)
        cs1 = place(area_e, 7168, KD, P)
        xs_next = place(area_0, 2 * 2 * FF + NF * D, KD * P)
        q_sq = place(area_e, 9216, HG * DH)
        rope_kt = place(angles, 0, 2, 2, DH)
        rope_qt = place(angles, 512, 2, DH)
        z1 = place(angles, 768, D)
        fly = place(angles, 0, 2, NF, FF // P * 4)
        w_ug = place(area_0, 0, KD, 2 * FF)
        w_down = place(area_0, 2 * 2 * FF, NF, D)
        sgate = place(area_2, 2048, 2, CHUNK)
        hid = place(area_2, 3072, NF, CHUNK)
        block = ctx.enter_context(nc.Block())

        L0_OWNED = {
            "pe": "xt q tq sc tp pv to y qc kvp kvt",
            "act": "xs qabs qt exp ot qcs rs kvrs kvc kve",
            "dve": "rope u max on pt ln lna kvn kvr sm v band",
            "pool": "xb",
        }
        OWNED = {
            "A": L0_OWNED,
            "B": L0_OWNED,
            "C": {"pe": "tt lg gt gb ha hb y", "act": "r tT gT gl e rs th wh ah", "pool": "tl wl al",
                  "dve": "t up lin act acc lgs g x ln v2"},
            "D": {"pe": "xt xp zp bc dtp rep rb y o", "act": "xT c1 u sz ev sp b da rs",
                  "dve": "cv v dt dtu rd h hc yg ln m st", "pool": "dbu"},
            "K": {"pe": "xt q pv kt", "act": "xs cs sq vc rs tc", "dve": "u ss kx kr", "pool": "xb tab"},
            "E": {"pe": "xt q tq sc tp pv to y", "act": "xa qabs qt exp ot rs rq",
                  "dve": "u rope ss nm max pt rc on lna v ln", "pool": "xb tab sq fly xsp"},
            "F": {"pe": "fold fd xt g up o", "act": "fu xT sg rs", "dve": "fe hid m st ln"},
        }

        def start_counts(eng, who):
            for st in OWNED:
                for n in OWNED[st].get(who, "").split():
                    if physical(f"{st}_{n}") != f"{st}_{n}":
                        continue
                    eng.sem_inc(sem(f"{st}_{n}"), CREDIT)

        N_CONST = 7
        FOLDS = 4 + 4 + 2 + 4

        @block.sync
        def _(sp):
            def load(dst, src, s):
                sp.dma_start(dst, src).then_inc(sem(s), 16)

            load(x0T, a["xT"], "d_kv")
            load(wkv0, a["a_wkva"], "d_kv")
            load(consts[:, :], a["consts"], "d_const")
            load(rope_x, a["rope_x"], "d_const")
            load(inv_freq, a["inv_freq"], "d_const")
            load(gamma, a["gamma"].partition_broadcast(P), "d_const")
            load(beta, a["beta"].partition_broadcast(P), "d_const")
            load(norm_w, a["norm_w"].partition_broadcast(P), "d_const")
            load(gate_b, a["gate_b"].partition_broadcast(P), "d_const")
            load(int_ids[:, :, :], a["ids"], "d_ids")
            load(angles[:, 0:32], a["freqs"], "d_ids")
            load(X[:, 0:NB, :], a["x"], "d_x")
            load(wq_nopeT, a["a_wqnT"], "d_foldq")
            load(wk_upT, a["a_wkbT"], "d_foldq")
            load(wq0[:, :, :, RK:DH], a["a_wqr"], "d_wq0")
            load(wv_upT, a["a_wvbT"], "d_foldo")
            load(w_out, a["a_wout"], "d_foldo")
            load(ctxT[:, :, :], a["ctxT"], "d_ctx")
            load(wdq, a["b_wdq"], "d_ctx")
            load(wkvc, a["b_wkvc"], "d_ctx")
            load(wkr[0:RK, :], a["b_wkr"], "d_ctx")
            load(wuqT, a["b_wuqT"], "d_foldbq")
            load(wukT, a["b_wukT"], "d_foldbq")
            load(wqx[0:QC, :, RK:DH], a["b_wqr"], "d_wqx")
            load(wuvT, a["b_wuvT"], "d_foldbo")
            load(w_ox, a["b_wo"], "d_foldbo")
            load(b1, a["b1"], "d_moe")
            load(ssm_cols, a["ssm_cols"], "d_ssm")
            sp.wait_ge(sem("A_q"), at("A_q", NG * NB + 1))
            load(gate_wT, a["gate_w"], "d_moe")
            load(b2_all[0:NE, :], a["b2"], "d_moe")
            for i in range(2):
                load(w1_e[i], a["w1"][i], f"d_expert{i}")
                load(w2_e[i], a["w2"][i], f"d_expert{i}")
            load(w_in, a["w_in"], "d_ssm")
            load(w_x, a["w_x"], "d_ssm")
            load(w_dt, a["w_dt"], "d_ssm")
            load(w_ssm, a["w_ssm"], "d_ssm")
            sp.wait_ge(sem("fold_mm"), FOLDS)
            load(wq1, a["e_wq"], "d_e")
            load(wk1, a["e_wk"], "d_e")
            load(wv1, a["e_wv"], "d_e")
            load(wo1, a["e_wo"], "d_e")
            load(qk_w[:, 0, :], a["q_norm"].partition_broadcast(P), "d_rows")
            load(qk_w[:, 1, :], a["k_norm"].partition_broadcast(P), "d_rows")
            load(ffn_cols, a["ffn_cols"], "d_rows")
            load(wsd, a["ws_down"].partition_broadcast(P), "d_rows")
            with sp.Fori(1, NE // 2) as pair:
                for i in range(2):
                    sp.wait_ge(sem("C_wl"), at("C_wl", 4 * pair + 2 * i - 2))
                    load(w1_e[i], a["w1"][2 * pair + i], f"d_expert{i}")
                    load(w2_e[i], a["w2"][2 * pair + i], f"d_expert{i}")
            sp.wait_ge(sem("C_y"), at("C_y", 2 * NE))
            load(w_ug, a["w_ug"], "d_ffn")
            load(w_down, a["w_down"], "d_ffn")
            sp.wait_ge(sem(FINAL[0]), at(FINAL[0], FINAL[1]))
            sp.dma_start(out, X[:, 0:NB, :]).then_inc(sem("d_out"), 16)
            sp.wait_ge(sem("d_out"), 16)


        class Stage:

            def __init__(self, name, i, scale):
                self.name, self.i, self.scale = name, i, scale
                self.x = i == 1
                self.keyT, self.val = keyT[i], val[i]
                self.wo = wox if self.x else wo0
                self.rope = rope_x if self.x else rope_0

            def s(self, n):
                return sem(f"{self.name}_{n}")

        stages = [Stage("A", 0, float((DH + RR) ** -0.5)), Stage("B", 1, float((DH + RR) ** -0.5))]

        @block.tensor
        def _(pe):
            start_counts(pe, "pe")
            mm = nc.tensor.matmul
            tr = nc.tensor.transpose

            def keys_values(st):
                if st.x:
                    pe.wait_ge(sem("d_ctx"), 64)
                    pe.wait_ge(sem("A_kvr"), at("A_kvr", 2))
                    for c in range(NC_):
                        for k in range(KD):
                            ins = mm(PS[0:RK, 4 + c, :], wkvc[:, k, :], ctxT[:, k, c * CHUNK:(c + 1) * CHUNK],
                                     start=k == 0, stop=k == KD - 1)
                    ins.then_inc(sem("kvcT"), 1)
                    for b in range(NB):
                        for k in range(KD):
                            mm(bank(b // 4, 4, DH)[:, b % 4, 0:RK], ctxT[:, k, b * P:(b + 1) * P], wkvc[:, k, :],
                               start=k == 0, stop=k == KD - 1)
                    pe.wait_ge(st.s("kvc"), at(st.name + "_kvc", 1))
                    for b in range(NB):
                        ins = mm(bank(b // 4, 4, DH)[:, b % 4, RK:DH], kv_cT[0:RK, b * P:(b + 1) * P], wkr[0:RK, :],
                                 start=True, stop=True)
                    ins.then_inc(st.s("kvp"), 1)
                else:
                    pe.wait_ge(sem("d_kv"), 32)
                    for b in range(NB):
                        for k in range(KD):
                            ins = mm(bank(b // 4, 4, DH)[:, b % 4, :], x0T[:, k, b * P:(b + 1) * P], wkv0[:, k, :],
                                     start=k == 0, stop=k == KD - 1)
                    ins.then_inc(st.s("kvp"), 1)
                pe.wait_ge(st.s("kvr"), at(st.name + "_kvr", 2))
                pe.wait_ge(st.s("kve"), at(st.name + "_kve", 1))
                for b in range(NB):
                    ins = tr(bank(2 + b // 4, 4, P)[:, b % 4, :], k_tok[:, b, :], ident)
                ins.then_inc(st.s("kvt"), 1)

            def fold(st, n0):
                s = sem("fold_mm")
                up_q, up_k = (wuqT, wukT) if st.x else (wq_nopeT, wk_upT)
                up_v, w_o = (wuvT, w_ox) if st.x else (wv_upT, w_out)
                pe.wait_ge(sem("d_foldbq" if st.x else "d_foldq"), 32)
                n = n0
                rows = [(0, QC)] if st.x else [(0, P), (P, P)]
                for r0, nr in rows:
                    for hh in range(2):
                        if n >= 2:
                            pe.wait_ge(sem("fold_ev"), n - 1)
                        for h in range(8):
                            ins = mm(bank(4 + n % 2, 8, RK)[0:nr, h, :], up_q[:, 8 * hh + h, r0:r0 + nr],
                                     up_k[:, 8 * hh + h, :], start=True, stop=True)
                        ins.then_inc(s, 1)
                        n += 1
                pe.wait_ge(sem("d_foldbo" if st.x else "d_foldo"), 32)
                for jj in range(NH // 4):
                    if n >= 2:
                        pe.wait_ge(sem("fold_ev"), n - 1)
                    for j in range(2):
                        for h in range(2):
                            ins = mm(bank(4 + n % 2, 2, D)[RK * h:RK * h + RK, j, :], up_v[:, 4 * jj + 2 * j + h, :],
                                     w_o[:, 4 * jj + 2 * j + h, :], start=True, stop=True)
                    ins.then_inc(s, 1)
                    n += 1
                return n

            def attend(st):
                s = st.s

                def turn_x(b):
                    pe.wait_ge(s("xb"), at(st.name + "_xb", b + 1))
                    pe.wait_ge(s("xs"), at(st.name + "_xs", b))
                    if st.x:
                        pe.wait_ge(s("qcs"), at(st.name + "_qcs", b))
                    for k in range(KD):
                        ins = tr(PS[:, 6, k * P:(k + 1) * P], x_now[:, k * P:(k + 1) * P], ident)
                    ins.then_inc(s("xt"), 1)

                def compress(b):
                    pe.wait_ge(s("xs"), at(st.name + "_xs", b + 1))
                    for k in range(KD):
                        ins = mm(PS[0:QC, 6, 256:256 + P], wdq[:, k, :], xs[:, k, :], start=k == 0, stop=k == KD - 1)
                    ins.then_inc(s("qc"), 1)

                def queries(n, b, g):
                    if g == 0:
                        pe.wait_ge(s("qcs" if st.x else "xs"), at(st.name + "_" + ("qcs" if st.x else "xs"), b + 1))
                    pe.wait_ge(s("qabs"), at(st.name + "_qabs", n))
                    if st.x:
                        ins = mm(bank(0, HG, DH), qcT[0:QC, :], wqx[0:QC, HG * g:HG * g + HG, :], start=True, stop=True)
                    else:
                        for k in range(KD):
                            ins = mm(bank(0, HG, DH), xs[:, k, :], wq0[:, k, HG * g:HG * g + HG, :],
                                     start=k == 0, stop=k == KD - 1)
                    ins.then_inc(s("q"), 1)

                def turn_q(n, g):
                    pe.wait_ge(s("rope"), at(st.name + "_rope", n + 1))
                    pe.wait_ge(s("ot"), at(st.name + "_ot", n - 2))
                    for j in range(HG):
                        ins = tr(bank(1, HG, P)[:, j, :], q_tok[:, g % 2, j * DH:(j + 1) * DH], ident)
                    ins.then_inc(s("tq"), 1)

                def scores(n, b, g):
                    pe.wait_ge(s("qt"), at(st.name + "_qt", n + 1))
                    pe.wait_ge(s("max"), at(st.name + "_max", n - 1))
                    if not st.x:
                        pe.wait_ge(s("exp"), at(st.name + "_exp", n - 1))
                    for j in range(HG):
                        ins = mm(bank(2 + g % 2, HG, P)[:, j, :], qT[:, g % 2, j * P:(j + 1) * P], st.keyT[:, b, :],
                                 start=True, stop=True)
                    ins.then_inc(s("sc"), 1)

                def turn_p(n, g):
                    pe.wait_ge(s("exp"), at(st.name + "_exp", n + 1))
                    pe.wait_ge(s("pt"), at(st.name + "_pt", n))
                    for j in range(HG):
                        ins = tr(bank(4, HG, P)[:, j, :], prob[:, g % 2, j * P:(j + 1) * P], ident)
                    ins.then_inc(s("tp"), 1)

                def mix(n, b):
                    pe.wait_ge(s("pt"), at(st.name + "_pt", n + 1))
                    pe.wait_ge(s("on"), at(st.name + "_on", n))
                    for j in range(HG):
                        ins = mm(bank(5, HG, RK + 1)[:, j, :], probT[:, j * P:(j + 1) * P], st.val[:, b, :],
                                 start=True, stop=True)
                    ins.then_inc(s("pv"), 1)

                def turn_o(n):
                    pe.wait_ge(s("on"), at(st.name + "_on", n + 1))
                    for j in range(HG // 2):
                        ins = tr(PS[:, 1, j * P:(j + 1) * P], o_norm[:, j * P:(j + 1) * P], ident)
                    ins.then_inc(s("to"), 1)

                def project(b):
                    pe.wait_ge(s("ot"), at(st.name + "_ot", NG * b + NG))
                    pe.wait_ge(s("lna"), at(st.name + "_lna", b))
                    for c in range(NH // 2):
                        ins = mm(PS[:, 7, 0:D], oT[:, c, :], st.wo[:, c, :], start=c == 0, stop=c == NH // 2 - 1)
                    ins.then_inc(s("y"), 1)

                def sequence(b, first=False, last=False):
                    for g in range(NG):
                        n = NG * b + g
                        if not last:
                            turn_q(n, g)
                            queries(n + 1, b + (g + 1) // NG, (g + 1) % NG)
                        if not (first and g < 2) and not (last and g > 1):
                            mix(n - 2, b if g >= 2 else b - 1)
                        if not last:
                            scores(n, b, g)
                            if g == 2 and st.x:
                                compress(b + 1)
                        if not (first and g < 2) and not (last and g > 1):
                            pe.wait_ge(s("qt"), at(st.name + "_qt", GROUPS if last else n + 1))
                            pe.wait_ge(s("ot"), at(st.name + "_ot", n - 2))
                            turn_o(n - 2)
                        if not (first and g < 1) and not (last and g > 0):
                            turn_p(n - 1, g + 1)
                        if g == 1 and not last:
                            turn_x(b + 1)
                        if g == 2 and not first:
                            project(b - 1)

                pe.wait_ge(s("kvc"), at(st.name + "_kvc", 2))
                turn_x(0)
                if st.x:
                    compress(0)
                queries(0, 0, 0)
                sequence(0, first=True)
                with pe.Fori(1, NB) as b:
                    sequence(b)
                sequence(NB, last=True)

            pe.wait_ge(sem("d_const"), 16 * N_CONST)
            keys_values(stages[0])
            n = fold(stages[0], 0)
            pe.wait_ge(sem("fold_ev"), n)
            pe.wait_ge(sem("A_kvc"), at("A_kvc", 2))
            keys_values(stages[1])
            n = fold(stages[1], n)
            pe.wait_ge(sem("fold_ev"), n)
            pe.wait_ge(sem("d_wq0"), 16)
            pe.wait_ge(sem("d_wqx"), 16)
            pe.wait_ge(sem("B_kvc"), at("B_kvc", 2))
            attend(stages[0])
            for n, count in (("lna", NB), ("ot", NB * NG), ("on", NB * NG), ("pt", NB * NG), ("exp", NB * NG),
                             ("qt", NB * NG), ("qabs", NB * NG + 1), ("xs", NB + 1)):
                pe.wait_ge(sem("A_" + n), at("A_" + n, count))
            attend(stages[1])

            def gates_pe():
                pe.wait_ge(sem("C_g"), at("C_g", 1))
                for b in range(NB):
                    ins = tr(PS[0:NE, 5 + b // 4, (b % 4) * P:(b % 4 + 1) * P], gates[:, b, :], ident)
                ins.then_inc(sem("C_gt"), 1)
                pe.wait_ge(sem("C_gT"), at("C_gT", 1))
                for b in range(NB):
                    ins = mm(bank(4 + b // 2, 2, D)[:, b % 2, :], gatesT[0:NE, b * P:(b + 1) * P], b2_all[0:NE, :],
                             start=True, stop=True)
                ins.then_inc(sem("C_gb"), 1)

            def hidden(k, j):
                slot, c = j // 2, j % 2
                for m in range(2):
                    for part, name in ((0, "ha"), (1, "hb")):
                        pe.wait_ge(sem("C_lin" if part == 0 else "C_up"), at("C_lin" if part == 0 else "C_up", 2 * k + m - 1))
                        cols, toks = slice((2 * part + m) * P, (2 * part + m + 1) * P), slice(c * CHUNK, (c + 1) * CHUNK)
                        for kk in range(KD):
                            for i, (w, t) in enumerate(((w1_hi, tT_hi), (w1_hi, tT_lo), (w1_lo, tT_hi))):
                                ins = mm(PS[:, 2 * m + part, :], w[slot][:, kk, cols], t[:, kk, toks],
                                         start=kk == 0 and i == 0, stop=kk == KD - 1 and i == 2)
                        ins.then_inc(sem("C_" + name), 1)

            def outputs(k, j):
                slot, c = j // 2, j % 2
                pe.wait_ge(sem("C_al"), at("C_al", 2 * k + 2))
                if j % 2 == 0:
                    pe.wait_ge(sem("C_wl"), at("C_wl", k + 2))
                pe.wait_ge(sem("C_acc"), at("C_acc", k - 1))
                for t in range(4):
                    for m in range(2):
                        for i, (x, w) in enumerate(((act_hi, w2_hi), (act_hi, w2_lo), (act_lo, w2_hi))):
                            ins = mm(bank(4 + 2 * c + t // 2, 2, D)[:, t % 2, :], x[:, c, m, t * P:(t + 1) * P],
                                     w[slot][:, m, :], start=m == 0 and i == 0, stop=m == 1 and i == 2)
                ins.then_inc(sem("C_y"), 1)

            def experts(pair, first=False, last=False):
                for j in range(4):
                    k = 4 * pair + j
                    if not last:
                        if j % 2 == 0:
                            pe.wait_ge(sem("C_wl"), at("C_wl", k + 1))
                        hidden(k, j)
                    if first and j == 0:
                        gates_pe()
                        pe.wait_ge(sem("C_x"), at("C_x", 1))
                    elif not (last and j > 0):
                        outputs(k - 1, (j - 1) % 4)

            for n, count in (("lna", NB), ("ot", NB * NG), ("on", NB * NG), ("pt", NB * NG), ("exp", NB * NG),
                             ("qt", NB * NG), ("qabs", NB * NG + 1), ("xs", NB + 1), ("qcs", NB + 1)):
                pe.wait_ge(sem("B_" + n), at("B_" + n, count))
            for b in range(NB):
                pe.wait_ge(sem("C_t"), at("C_t", b + 1))
                for k in range(KD):
                    ins = tr(PS[:, b // 2, ((b % 2) * KD + k) * P:((b % 2) * KD + k + 1) * P],
                             t_tok[:, b, k * P:(k + 1) * P], ident)
                ins.then_inc(sem("C_tt"), 1)
            pe.wait_ge(sem("C_tT"), at("C_tT", 4))
            pe.wait_ge(sem("d_moe"), 48)
            for b in range(NB):
                for k in range(KD):
                    ins = mm(bank(4, NB, NE)[:, b, :], tT[:, k, b * P:(b + 1) * P], gate_wT[:, k, :],
                             start=k == 0, stop=k == KD - 1)
            ins.then_inc(sem("C_lg"), 1)
            pe.wait_ge(sem("C_tl"), at("C_tl", 4))
            experts(0, first=True)
            with pe.Fori(1, NE // 2) as pair:
                experts(pair)
            experts(NE // 2, last=True)

            pe.wait_ge(sem("C_lin"), at("C_lin", 4 * NE))
            pe.wait_ge(sem("C_acc"), at("C_acc", 2 * NE))
            for b in range(NB):
                pe.wait_ge(sem("C_ln"), at("C_ln", b + 1))
                for k in range(KD):
                    ins = tr(PS[:, b // 2, ((b % 2) * KD + k) * P:((b % 2) * KD + k + 1) * P],
                             X[:, b, k * P:(k + 1) * P], ident)
                ins.then_inc(sem("D_xt"), 1)
            pe.wait_ge(sem("D_xT"), at("D_xT", 4))
            pe.wait_ge(sem("d_ssm"), 80)
            with pe.Fori(0, NC_) as c:
                pe.wait_ge(sem("D_o"), at("D_o", c))
                pe.wait_ge(sem("D_m"), at("D_m", c))
                for m in range(MD):
                    for k in range(KD):
                        ins = mm(PS[:, m, :], w_in[:, k, m * P:(m + 1) * P], xT[:, k, bass.ds(c * CHUNK, CHUNK)],
                                 start=k == 0, stop=k == KD - 1)
                    ins.then_inc(sem("D_xp"), 1)
                for m in range(MD):
                    for k in range(KD):
                        ins = mm(PS[:, 4 + m, :], w_in[:, k, DI + m * P:DI + (m + 1) * P],
                                 xT[:, k, bass.ds(c * CHUNK, CHUNK)], start=k == 0, stop=k == KD - 1)
                    ins.then_inc(sem("D_zp"), 1)
                pe.wait_ge(sem("D_u"), at("D_u", c + 1))
                pe.wait_ge(sem("D_sz"), at("D_sz", c + 1))
                for k in range(MD):
                    mm(PS[:, 4, :], w_x[:, k, 0:DTR], u_c[:, k, :], start=k == 0, stop=k == MD - 1)
                for k in range(MD):
                    ins = mm(PS[0:2 * NS, 5, :], w_x[:, k, DTR:], u_c[:, k, :], start=k == 0, stop=k == MD - 1)
                ins.then_inc(sem("D_bc"), 1)
                pe.wait_ge(sem("D_ev"), at("D_ev", 2 * c + 2))
                for m in range(MD):
                    ins = mm(PS[:, m, :], w_dt[:, m * P:(m + 1) * P], dt_in, start=True, stop=True)
                ins.then_inc(sem("D_dtp"), 1)

                def replicate(row, to):
                    return mm(PS[:, to, :], ident[0:2 * NS, row:row + 1].broadcast_to([2 * NS, P]), bcT[0:2 * NS, :],
                              start=True, stop=True)

                def replicate_b(s):
                    if s < NS:
                        pe.wait_ge(sem("D_b"), at("D_b", NS * c + s - 1))
                        replicate(s, 4 + s % 2).then_inc(sem("D_rb"), 1)

                def replicate_c(s):
                    if s < NS:
                        pe.wait_ge(sem("D_hc"), at("D_hc", (NS * c + s - 1) * MD))
                        replicate(NS + s, 6 + s % 2).then_inc(sem("D_rep"), 1)

                pe.wait_ge(sem("D_v"), at("D_v", c + 1))
                replicate_b(0)
                replicate_c(0)
                replicate_b(1)
                for s in range(NS):
                    for m in range(MD):
                        if m == 0:
                            replicate_b(s + 2)
                            replicate_c(s + 1)
                        pe.wait_ge(sem("D_hc"), at("D_hc", (NS * c + s) * MD + m + 1))
                        mm(PS[:, m, :], ident, read_out[:, m, :], start=s == 0, stop=s == NS - 1)\
                            .then_inc(sem("D_y"), 1)
                pe.wait_ge(sem("D_yg"), at("D_yg", c + 1))
                for t in range(4):
                    for k in range(MD):
                        ins = mm(bank(t // 2, 2, D)[:, t % 2, :], yg[:, k, t * P:(t + 1) * P], w_ssm[:, k, :],
                                 start=k == 0, stop=k == MD - 1)
                ins.then_inc(sem("D_o"), 1)

            def project_keys(b):
                pe.wait_ge(sem("K_xb"), at("K_xb", b + 1))
                pe.wait_ge(sem("K_xs"), at("K_xs", b))
                for k in range(KD):
                    ins = tr(PS[:, 6, k * P:(k + 1) * P], x_now1[:, k * P:(k + 1) * P], ident)
                ins.then_inc(sem("K_xt"), 1)
                for half in range(2):
                    n = 2 * b + half
                    src = xs1 if half else cs1
                    pe.wait_ge(sem("K_xs" if half else "K_cs"), at("K_xs" if half else "K_cs", b + 1))
                    pe.wait_ge(sem("K_u"), at("K_u", n - 1))
                    for k in range(KD):
                        ins = mm(PS[:, half, :], src[:, k, :], wk1[:, k, :], start=k == 0, stop=k == KD - 1)
                    ins.then_inc(sem("K_q"), 1)
                    pe.wait_ge(sem("K_vc"), at("K_vc", n - 1))
                    for k in range(KD):
                        ins = mm(PS[:, 2 + half, :], src[:, k, :], wv1[:, k, :], start=k == 0, stop=k == KD - 1)
                    ins.then_inc(sem("K_pv"), 1)

            def turn_keys(b):
                for half in range(2):
                    n = 2 * b + half
                    pe.wait_ge(sem("K_kr"), at("K_kr", n + 1))
                    pe.wait_ge(sem("K_tc"), at("K_tc", n - 1))
                    for g in range(KVH):
                        ins = tr(bank(4 + half, KVH, P)[:, g, :], k_tok1[:, half, g * DH:(g + 1) * DH], ident)
                    ins.then_inc(sem("K_kt"), 1)

            pe.wait_ge(sem("D_m"), at("D_m", NC_))
            pe.wait_ge(sem("d_e"), 64)
            project_keys(0)
            with pe.Fori(1, NB) as b:
                project_keys(b)
                turn_keys(b - 1)
            turn_keys(NB - 1)

            def turn_x1(b):
                pe.wait_ge(sem("E_xb"), at("E_xb", b + 1))
                pe.wait_ge(sem("E_xa"), at("E_xa", b))
                pe.wait_ge(sem("E_lna"), at("E_lna", b - 2))
                for k in range(KD):
                    ins = tr(PS[:, 7, 256 + k * P:256 + (k + 1) * P], x_now1[:, k * P:(k + 1) * P], ident)
                ins.then_inc(sem("E_xt"), 1)

            def queries1(n, b, g):
                if g == 0:
                    pe.wait_ge(sem("E_xsp"), at("E_xsp", b + 1))
                pe.wait_ge(sem("E_qabs"), at("E_qabs", n))
                for k in range(KD):
                    ins = mm(PS[:, 0, :], xs1[:, k, :], wq1[:, k, g * 512:(g + 1) * 512], start=k == 0, stop=k == KD - 1)
                ins.then_inc(sem("E_q"), 1)

            def turn_q1(n, g):
                pe.wait_ge(sem("E_rope"), at("E_rope", n + 1))
                pe.wait_ge(sem("E_ot"), at("E_ot", n - 2))
                for j in range(HG):
                    ins = tr(bank(1, HG, P)[:, j, :], q_tok1[:, g % 2, j * DH:(j + 1) * DH], ident)
                ins.then_inc(sem("E_tq"), 1)

            def mix1(n, b, g):
                pe.wait_ge(sem("E_pt"), at("E_pt", n + 1))
                pe.wait_ge(sem("E_on"), at("E_on", n))
                for j in range(HG):
                    for half in range(2):
                        ins = mm(bank(6, HG, DH)[:, j, :], probT1[:, half, j * P:(j + 1) * P],
                                 val1[:, b, half, g * DH:(g + 1) * DH], start=half == 0, stop=half == 1)
                ins.then_inc(sem("E_pv"), 1)

            def scores1(n, b, g):
                pe.wait_ge(sem("E_qt"), at("E_qt", n + 1))
                pe.wait_ge(sem("E_nm"), at("E_nm", n))
                pe.wait_ge(sem("E_exp"), at("E_exp", n))
                for j in range(HG):
                    ins = mm(PS[:, 2 + j // 2, (j % 2) * 256:(j % 2 + 1) * 256], qT1[:, g % 2, j * P:(j + 1) * P],
                             keyT1[:, b, g, :], start=True, stop=True)
                ins.then_inc(sem("E_sc"), 1)

            def turn_o1(n):
                pe.wait_ge(sem("E_on"), at("E_on", n + 1))
                pe.wait_ge(sem("E_qt"), at("E_qt", n + 3))
                for j in range(HG):
                    ins = tr(bank(1, HG, P)[:, j, :], o_norm1[:, j * DH:(j + 1) * DH], ident)
                ins.then_inc(sem("E_to"), 1)

            def turn_p1(n, g):
                pe.wait_ge(sem("E_exp"), at("E_exp", n + 1))
                pe.wait_ge(sem("E_pt"), at("E_pt", n))
                for half in range(2):
                    for j in range(HG):
                        ins = tr(bank(4 + half, HG, P)[:, j, :],
                                 probs1[:, g % 2, j * 256 + half * P:j * 256 + (half + 1) * P], ident)
                ins.then_inc(sem("E_tp"), 1)

            def project1(b, turned):
                pe.wait_ge(sem("E_ot"), at("E_ot", NG * b + NG))
                pe.wait_ge(sem("E_lna"), at("E_lna", b))
                pe.wait_ge(sem("E_xa"), at("E_xa", turned))
                for h in range(NH):
                    ins = mm(PS[:, 7, 0:D], oT1[:, h, :], wo1[:, h, :], start=h == 0, stop=h == NH - 1)
                ins.then_inc(sem("E_y"), 1)

            def sequence1(b, first=False, last=False):
                for g in range(NG):
                    n = NG * b + g
                    if not last:
                        turn_q1(n, g)
                        queries1(n + 1, b + (g + 1) // NG, (g + 1) % NG)
                    if not (first and g < 2) and not (last and g > 1):
                        mix1(n - 2, b if g >= 2 else b - 1, (g - 2) % NG)
                    if not last:
                        scores1(n, b, g)
                    if not (first and g < 2) and not (last and g > 1):
                        if last:
                            pe.wait_ge(sem("E_ot"), at("E_ot", n - 2))
                            pe.wait_ge(sem("E_on"), at("E_on", n - 1))
                            for j in range(HG):
                                ins = tr(bank(1, HG, P)[:, j, :], o_norm1[:, j * DH:(j + 1) * DH], ident)
                            ins.then_inc(sem("E_to"), 1)
                        else:
                            turn_o1(n - 2)
                    if not (first and g < 1) and not (last and g > 0):
                        turn_p1(n - 1, (g - 1) % NG)
                    if g == 1 and not last:
                        turn_x1(b + 1)
                    if g == 2 and not first:
                        project1(b - 1, NB + 1 if last else b + 2)

            pe.wait_ge(sem("K_tc"), at("K_tc", 2 * NB))
            pe.wait_ge(sem("K_vc"), at("K_vc", 2 * NB))
            turn_x1(0)
            queries1(0, 0, 0)
            sequence1(0, first=True)
            with pe.Fori(1, NB) as b:
                sequence1(b)
            sequence1(NB, last=True)

            for n, count in (("lna", NB), ("ot", NB * NG), ("on", NB * NG), ("pt", NB * NG), ("exp", NB * NG),
                             ("qabs", NB * NG + 1), ("xa", NB + 1), ("fly", NB)):
                pe.wait_ge(sem("E_" + n), at("E_" + n, count))
            for i in range(KD):
                src = ctxT_flat if i == 0 else w_ug[:, 0, :]
                for q in range(4):
                    ins = mm(PS[:, 4 * i + q, :], hadamard, src[:, q * 512:(q + 1) * 512], start=True, stop=True)
                ins.then_inc(sem("F_fold"), 1)
            pe.wait_ge(sem("F_fu"), at("F_fu", 4))
            wd_flat = w_down.rearrange("p f d -> p (f d)")
            for q in range(4):
                ins = mm(PS[:, q, :], hadamard, wd_flat[:, q * 512:(q + 1) * 512], start=True, stop=True)
            ins.then_inc(sem("F_fd"), 1)
            pe.wait_ge(sem("F_fu"), at("F_fu", 8))
            for b in range(NB):
                pe.wait_ge(sem("E_ln"), at("E_ln", b + 1))
                for k in range(KD):
                    ins = tr(PS[:, 4 + b // 2, ((b % 2) * KD + k) * P:((b % 2) * KD + k + 1) * P],
                             X[:, b, k * P:(k + 1) * P], ident)
                ins.then_inc(sem("F_xt"), 1)
            pe.wait_ge(sem("F_xT"), at("F_xT", 4))
            pe.wait_ge(sem("F_fe"), at("F_fe", 2))
            with pe.Fori(0, NC_) as c:
                for f in range(NF):
                    n = NF * c + f
                    for part, name in ((1, "g"), (0, "up")):
                        pe.wait_ge(sem("F_sg" if part else "F_hid"), at("F_sg" if part else "F_hid", n - 1))
                        for k in range(KD):
                            ins = mm(PS[:, 2 * part + f % 2, :], w_ug[:, 1 - k, part * FF + f * P:part * FF + (f + 1) * P],
                                     xT[:, k, bass.ds(c * CHUNK, CHUNK)], start=k == 0, stop=k == KD - 1)
                        ins.then_inc(sem("F_" + name), 1)
                pe.wait_ge(sem("F_hid"), at("F_hid", NF * c + NF))
                pe.wait_ge(sem("F_m"), at("F_m", c))
                for t in range(4):
                    for f in range(NF):
                        ins = mm(bank(4 + t // 2, 2, D)[:, t % 2, :], hid[:, f, t * P:(t + 1) * P], w_down[:, f, :],
                                 start=f == 0, stop=f == NF - 1)
                ins.then_inc(sem("F_o"), 1)

        @block.scalar
        def _(act):
            start_counts(act, "act")
            nc.scalar.preload_act_table_set("natural_log_exp_and_others")

            def keys_values(st):
                s = st.s
                if st.x:
                    act.wait_ge(sem("kvcT"), 1)
                    act.activation(kv_cT[0:RK, :], PS[0:RK, 4:6, :], ACT.Copy).then_inc(s("kvc"), 1)
                    act.wait_ge(s("kvr"), at(st.name + "_kvr", 2))
                    act.activation(k_tok[:, :, 0:RK], PS[:, 0:2, :].rearrange("p c (a d) -> p (c a) d", a=4)[:, :, 0:RK],
                                   ACT.Copy).then_inc(s("kve"), 1)
                else:
                    act.wait_ge(s("v"), at(st.name + "_v", 2 * NB))
                    act.activation(rstd8, mv8[:, :, 1], ACT.Ln, bias=eps_ln[:, 0:1]).then_inc(s("kvc"), 1)
                    act.wait_ge(s("kvc"), at(st.name + "_kvc", 1))
                    act.activation(rstd8, rstd8, ACT.Exp, scale=-0.5).then_inc(s("kvrs"), 1)
                    act.wait_ge(s("kvn"), at(st.name + "_kvn", 1))
                    act.activation(k_tok[:, :, 0:RK], st.val[:, :, 0:RK], ACT.Copy).then_inc(s("kve"), 1)
                act.wait_ge(s("kvt"), at(st.name + "_kvt", 1))
                act.activation(st.keyT.rearrange("p b k -> p (b k)"), PS[:, 2:4, :].rearrange("p c k -> p (c k)"),
                               ACT.Copy).then_inc(s("kvc"), 1)

            def fold(st, n0):
                n = n0
                rows = [(0, QC)] if st.x else [(0, P), (P, P)]
                for i, (r0, nr) in enumerate(rows):
                    for hh in range(2):
                        act.wait_ge(sem("fold_mm"), n + 1)
                        dst = wqx[0:QC, 8 * hh:8 * hh + 8, 0:RK] if st.x else wq0[:, i, 8 * hh:8 * hh + 8, 0:RK]
                        act.activation(dst, bank(4 + n % 2, 8, RK)[0:nr], ACT.Copy).then_inc(sem("fold_ev"), 1)
                        n += 1
                for jj in range(NH // 4):
                    act.wait_ge(sem("fold_mm"), n + 1)
                    act.activation(st.wo[:, 2 * jj:2 * jj + 2, :], bank(4 + n % 2, 2, D), ACT.Copy)\
                       .then_inc(sem("fold_ev"), 1)
                    n += 1
                return n

            def attend(st):
                s = st.s

                def copy_x(b):
                    act.wait_ge(s("xt"), at(st.name + "_xt", b + 1))
                    act.wait_ge(s("qc" if st.x else "q"), at(st.name + "_" + ("qc" if st.x else "q"), b if st.x else NG * b))
                    act.activation(xs, PS[:, 6, 0:256].rearrange("p (k t) -> p k t", k=KD), ACT.Copy)\
                       .then_inc(s("xs"), 1)

                def copy_compressed(b):
                    act.wait_ge(s("qc"), at(st.name + "_qc", b + 1))
                    act.wait_ge(s("q"), at(st.name + "_q", NG * b))
                    act.activation(qcT[0:QC, :], PS[0:QC, 6, 256:256 + P], ACT.Copy).then_inc(s("qcs"), 1)

                def copy_queries(n, slot):
                    act.wait_ge(s("q"), at(st.name + "_q", n + 1))
                    act.wait_ge(s("tq"), at(st.name + "_tq", n - 1))
                    act.activation(q_tok[:, slot % 2, :], PS[:, 0, :], ACT.Copy).then_inc(s("qabs"), 1)

                def copy_q(n, g):
                    act.wait_ge(s("tq"), at(st.name + "_tq", n + 1))
                    act.wait_ge(s("sc"), at(st.name + "_sc", n - 1))
                    act.activation(qT[:, g % 2, :], PS[:, 1, :], ACT.Copy).then_inc(s("qt"), 1)

                def softmax(n, g):
                    act.wait_ge(s("max"), at(st.name + "_max", n + 1))
                    act.wait_ge(s("tp"), at(st.name + "_tp", n - 1))
                    src = masked[:, g % 2, :] if st.x else PS[:, 2 + g % 2, :]
                    for j in range(HG):
                        ins = act.activation(prob[:, g % 2, j * P:(j + 1) * P], src[:, j * P:(j + 1) * P], ACT.Exp,
                                             bias=negmax[:, g % 2, j:j + 1], scale=st.scale)
                    ins.then_inc(s("exp"), 1)

                def copy_o(n, g):
                    act.wait_ge(s("to"), at(st.name + "_to", n + 1))
                    if g == 0:
                        act.wait_ge(s("y"), at(st.name + "_y", n_b(n)))
                    act.activation(oT[:, 2 * g:2 * g + 2, :], PS[:, 1, 0:256].rearrange("p (a t) -> p a t", a=2),
                                   ACT.Copy).then_inc(s("ot"), 1)

                def inv_std(b):
                    act.wait_ge(s("v"), at(st.name + "_v", V_BASE[st.name] + 2 * b + 2))
                    act.wait_ge(s("ln"), at(st.name + "_ln", b))
                    act.activation(rstd, mv[:, 1:2], ACT.Ln, bias=eps_ln[:, 0:1]).then_inc(s("rs"), 1)
                    act.wait_ge(s("rs"), at(st.name + "_rs", 2 * b + 1))
                    act.activation(rstd, rstd, ACT.Exp, scale=-0.5).then_inc(s("rs"), 1)

                cur = [0]

                def n_b(n):
                    return cur[0]

                def sequence(b, first=False, last=False):
                    for g in range(NG):
                        n = NG * b + g
                        if not last:
                            copy_q(n, g)
                        if not (first and g < 1) and not (last and g > 0):
                            softmax(n - 1, (g - 1) % NG)
                        if not last:
                            if g == 2 and st.x:
                                copy_x(b + 1)
                            copy_queries(n + 1, g + 1)
                            if g == 2:
                                (copy_compressed if st.x else copy_x)(b + 1)
                        if not (first and g < 2) and not (last and g > 1):
                            cur[0] = b if g >= 2 else b - 1
                            copy_o(n - 2, (g - 2) % NG)
                        if g == 3 and not first:
                            inv_std(b - 1)

                copy_x(0)
                if st.x:
                    copy_compressed(0)
                copy_queries(0, 0)
                sequence(0, first=True)
                with act.Fori(1, NB) as b:
                    sequence(b)
                sequence(NB, last=True)

            act.wait_ge(sem("eps"), 3)
            act.wait_ge(sem("ang"), 1)
            act.activation(sines[:, :], sines[:, :], ACT.Sin).then_inc(sem("trig"), 1)
            act.activation(cosines[:, :], cosines[:, :], ACT.Sin).then_inc(sem("trig"), 1)
            nc.scalar.preload_act_table_set("natural_log_exp_and_others")
            keys_values(stages[0])
            n = fold(stages[0], 0)
            keys_values(stages[1])
            fold(stages[1], n)
            act.wait_ge(sem("d_ssm"), 16)
            act.activation(ssm_cols[:, :, 6:22], ssm_cols[:, :, 6:22], ACT.Exp).then_inc(sem("A_log"), 1)
            attend(stages[0])
            attend(stages[1])

            def weights_hi(e, slot, second):
                act.wait_ge(sem(f"d_expert{slot}"), 16 * e + 32 - 16 * slot)
                if second:
                    act.wait_ge(sem("C_y"), at("C_y", 2 * e - 2))
                    act.activation(w2_hi[slot], w2_e[slot], ACT.Copy).then_inc(sem("C_wh"), 1)
                else:
                    act.wait_ge(sem("C_hb"), at("C_hb", 4 * e - 4))
                    act.activation(w1_hi[slot], w1_e[slot], ACT.Copy).then_inc(sem("C_wh"), 1)

            for b in range(NB):
                act.wait_ge(sem("B_ln"), at("B_ln", b + 1))
                ins = act.activation(t_tok[:, b, :], X[:, b, :], ACT.Square, accum_out=ssq8[:, b:b + 1])
            ins.then_inc(sem("C_r"), 1)
            act.wait_ge(sem("C_r"), at("C_r", 1))
            act.activation(ssq8, ssq8, ACT.Ln, scale=1.0 / D, bias=eps_ln[:, 0:1]).then_inc(sem("C_r"), 1)
            act.wait_ge(sem("C_r"), at("C_r", 2))
            act.activation(ssq8, ssq8, ACT.Exp, scale=-0.5).then_inc(sem("C_r"), 1)
            for i in range(4):
                act.wait_ge(sem("C_tt"), at("C_tt", 2 * i + 2))
                act.activation(tT[:, :, i * 2 * P:(i + 1) * 2 * P].rearrange("p k (b t) -> p b k t", b=2),
                               bank(i, 2, KD, P), ACT.Copy).then_inc(sem("C_tT"), 1)
                act.wait_ge(sem("C_tT"), at("C_tT", i + 1))
                act.wait_ge(sem("C_tt"), at("C_tt", NB))
                cols = slice(i * 2 * P, (i + 1) * 2 * P)
                act.activation(tT_hi[:, :, cols], tT[:, :, cols], ACT.Copy).then_inc(sem("C_th"), 1)
            weights_hi(0, 0, False)
            weights_hi(0, 0, True)
            act.wait_ge(sem("C_lgs"), at("C_lgs", 1))
            act.activation(expl, expl, ACT.Exp).then_inc(sem("C_e"), 1)
            act.wait_ge(sem("C_gt"), at("C_gt", 1))
            act.activation(gatesT[0:NE, :], PS[0:NE, 5:7, :].rearrange("p a b -> p (a b)"), ACT.Copy)\
               .then_inc(sem("C_gT"), 1)
            nc.scalar.preload_act_table(ACT.Gelu_apprx_sigmoid)

            def experts(pair, last=False):
                for j in range(4):
                    for m in range(2):
                        n = 8 * pair + 2 * j + m
                        act.wait_ge(sem("C_lin"), at("C_lin", n + 1))
                        act.wait_ge(sem("C_act"), at("C_act", n - 1))
                        act.activation(act_gl[:, m, :], act_lin[:, m, :], ACT.Gelu_apprx_sigmoid)\
                           .then_inc(sem("C_gl"), 1)
                    for m in range(2):
                        n = 8 * pair + 2 * j + m
                        act.wait_ge(sem("C_act"), at("C_act", n + 1))
                        act.wait_ge(sem("C_y"), at("C_y", 4 * pair + j - 1))
                        act.activation(act_hi[:, j % 2, m, :], act_out[:, m, :], ACT.Copy).then_inc(sem("C_ah"), 1)
                    if not (last and j > 1):
                        weights_hi(2 * pair + 1 + j // 2, (1 + j // 2) % 2, j % 2 == 1)

            with act.Fori(0, NE // 2 - 1) as pair:
                experts(pair)
            experts(NE // 2 - 1, last=True)
            nc.scalar.preload_act_table_set("natural_log_exp_and_others")

            def inv_std8():
                act.wait_ge(sem("C_v2"), at("C_v2", 2 * NB))
                act.activation(rstd8, mv8[:, :, 1], ACT.Ln, bias=eps_ln[:, 0:1]).then_inc(sem("C_rs"), 1)
                act.wait_ge(sem("C_rs"), at("C_rs", 1))
                act.activation(rstd8, rstd8, ACT.Exp, scale=-0.5).then_inc(sem("C_rs"), 1)

            inv_std8()

            for i in range(4):
                act.wait_ge(sem("D_xt"), at("D_xt", 2 * i + 2))
                act.activation(xT[:, :, i * 2 * P:(i + 1) * 2 * P].rearrange("p k (b t) -> p b k t", b=2),
                               bank(i, 2, KD, P), ACT.Copy).then_inc(sem("D_xT"), 1)
            with act.Fori(0, NC_) as c:
                nc.scalar.preload_act_table(ACT.Silu)
                for m in range(MD):
                    act.wait_ge(sem("D_xp"), at("D_xp", MD * c + m + 1))
                    act.activation(u_c[:, m, :], PS[:, m, :], ACT.Identity, bias=ssm_cols[:, m, 3:4],
                                   scale=ssm_cols[:, m, 1:2]).then_inc(sem("D_c1"), 1)
                for m in range(MD):
                    act.wait_ge(sem("D_zp"), at("D_zp", MD * c + m + 1))
                    ins = act.activation(sz[:, m, :], PS[:, 4 + m, :], ACT.Silu)
                ins.then_inc(sem("D_sz"), 1)
                for m in range(MD):
                    act.wait_ge(sem("D_cv"), at("D_cv", 2 * (MD * c + m) + 2))
                    ins = act.activation(u_c[:, m, :], u_c[:, m, :], ACT.Silu)
                ins.then_inc(sem("D_u"), 1)
                act.wait_ge(sem("D_bc"), at("D_bc", c + 1))
                act.activation(dt_in, PS[:, 4, :], ACT.Copy).then_inc(sem("D_ev"), 1)
                act.activation(bcT[0:2 * NS, :], PS[0:2 * NS, 5, :], ACT.Copy).then_inc(sem("D_ev"), 1)
                nc.scalar.preload_act_table_set("natural_log_exp_and_others")
                act.wait_ge(sem("D_v"), at("D_v", c + 1))
                act.activation(sp_tmp, dt, ACT.Abs).then_inc(sem("D_sp"), 1)
                act.wait_ge(sem("D_sp"), at("D_sp", 3 * c + 1))
                act.activation(sp_tmp, sp_tmp, ACT.Exp, scale=-1.0).then_inc(sem("D_sp"), 1)
                act.wait_ge(sem("D_sp"), at("D_sp", 3 * c + 2))
                act.activation(sp_tmp, sp_tmp, ACT.Ln, bias=one[:, 0:1]).then_inc(sem("D_sp"), 1)

                def copy_b(s):
                    act.wait_ge(sem("D_rb"), at("D_rb", NS * c + s + 1))
                    if s > 1:
                        act.wait_ge(sem("D_dbu"), at("D_dbu", (NS * c + s - 2) * MD))
                    act.activation(b_rep[s % 3], PS[:, 4 + s % 2, :], ACT.Copy).then_inc(sem("D_b"), 1)

                copy_b(0)
                act.wait_ge(sem("D_dtu"), at("D_dtu", 2 * c + 2))
                for s in range(NS):
                    for m in range(MD):
                        n = (NS * c + s) * MD + m
                        act.wait_ge(sem("D_h"), at("D_h", n - 3))
                        act.activation(decay[:, m, :], dt[:, m, :], ACT.Exp, scale=ssm_cols[:, m, 6 + s:7 + s])\
                           .then_inc(sem("D_da"), 1)
                        if m == 0 and s < NS - 1:
                            copy_b(s + 1)
                act.wait_ge(sem("D_st"), at("D_st", 9 * c + 9))
                act.activation(rstd4, mv4[:, :, 1], ACT.Ln, bias=eps_ln[:, 0:1]).then_inc(sem("D_rs"), 1)
                act.wait_ge(sem("D_rs"), at("D_rs", 2 * c + 1))
                act.activation(rstd4, rstd4, ACT.Exp, scale=-0.5).then_inc(sem("D_rs"), 1)

            def keys_act(b):
                act.wait_ge(sem("K_pv"), at("K_pv", 2 * b))
                act.activation(cs1, ctxT[:, :, bass.ds(b * P, P)], ACT.Copy).then_inc(sem("K_cs"), 1)
                act.wait_ge(sem("K_xt"), at("K_xt", b + 1))
                act.activation(xs1, PS[:, 6, 0:256].rearrange("p (k t) -> p k t", k=KD), ACT.Copy)\
                   .then_inc(sem("K_xs"), 1)
                for half in range(2):
                    n = 2 * b + half
                    act.wait_ge(sem("K_q"), at("K_q", n + 1))
                    act.wait_ge(sem("K_ss"), at("K_ss", n - 1))
                    act.activation(squares[:, half, :], PS[:, half, :], ACT.Square).then_inc(sem("K_sq"), 1)
                    act.wait_ge(sem("K_pv"), at("K_pv", n + 1))
                    act.activation(val1[:, b, half, :], PS[:, 2 + half, :], ACT.Copy).then_inc(sem("K_vc"), 1)
                for half in range(2):
                    n = 2 * b + half
                    act.wait_ge(sem("K_ss"), at("K_ss", n + 1))
                    act.wait_ge(sem("K_kr"), at("K_kr", n - 1))
                    act.activation(rms[:, half, :], sumsq[:, half, :], ACT.Ln, scale=1.0 / DH, bias=eps_rms[:, 0:1])\
                       .then_inc(sem("K_rs"), 1)
                    act.wait_ge(sem("K_rs"), at("K_rs", 2 * n + 1))
                    act.activation(rms[:, half, :], rms[:, half, :], ACT.Exp, scale=-0.5).then_inc(sem("K_rs"), 1)

            def copy_keys(b):
                for half in range(2):
                    act.wait_ge(sem("K_kt"), at("K_kt", 2 * b + half + 1))
                    act.activation(keyT1[:, b, :, half * P:(half + 1) * P], bank(4 + half, KVH, P), ACT.Copy)\
                       .then_inc(sem("K_tc"), 1)

            act.wait_ge(sem("eps"), 4)
            act.wait_ge(sem("signed"), 1)
            nc.scalar.preload_act_table_set("natural_log_exp_and_others")
            act.wait_ge(sem("D_ln"), at("D_ln", NB))
            keys_act(0)
            with act.Fori(1, NB) as b:
                keys_act(b)
                copy_keys(b - 1)
            copy_keys(NB - 1)

            def copy_x1(b):
                act.wait_ge(sem("E_xt"), at("E_xt", b + 1))
                act.wait_ge(sem("E_xsp"), at("E_xsp", b))
                act.activation(xs_next, PS[:, 7, 256:512], ACT.Copy).then_inc(sem("E_xa"), 1)

            def copy_queries1(n, slot):
                act.wait_ge(sem("E_q"), at("E_q", n + 1))
                act.wait_ge(sem("E_tq"), at("E_tq", n - 1))
                act.activation(q_tok1[:, slot, :], PS[:, 0, :], ACT.Copy).then_inc(sem("E_qabs"), 1)

            def inv_rms(n, slot):
                act.wait_ge(sem("E_ss"), at("E_ss", n + 1))
                act.wait_ge(sem("E_exp"), at("E_exp", n - 1))
                act.wait_ge(sem("E_max"), at("E_max", n - 1))
                act.activation(rms[:, slot, :], sumsq[:, slot, :], ACT.Ln, bias=eps_q[:, 0:1]).then_inc(sem("E_rq"), 1)
                act.wait_ge(sem("E_rq"), at("E_rq", 2 * n + 1))
                act.activation(rms[:, slot, :], rms[:, slot, :], ACT.Exp, scale=-0.5).then_inc(sem("E_rq"), 1)

            def copy_q1(n, g):
                act.wait_ge(sem("E_tq"), at("E_tq", n + 1))
                act.wait_ge(sem("E_sc"), at("E_sc", n - 1))
                act.activation(qT1[:, g % 2, :], PS[:, 1, :], ACT.Copy).then_inc(sem("E_qt"), 1)

            def softmax1(n, slot):
                act.wait_ge(sem("E_max"), at("E_max", n + 1))
                act.wait_ge(sem("E_tp"), at("E_tp", n - 1))
                act.wait_ge(sem("E_on"), at("E_on", n - 1))
                for j in range(HG):
                    ins = act.activation(probs1[:, slot, j * 256:(j + 1) * 256],
                                         PS[:, 2 + j // 2, (j % 2) * 256:(j % 2 + 1) * 256], ACT.Exp,
                                         bias=negmax[:, slot, j:j + 1], scale=rms[:, slot, j:j + 1],
                                         accum_out=prob_sum[:, slot, j:j + 1])
                ins.then_inc(sem("E_exp"), 1)

            def copy_o1(n, g, done):
                act.wait_ge(sem("E_to"), at("E_to", n + 1))
                if g == 0:
                    act.wait_ge(sem("E_y"), at("E_y", done))
                act.activation(oT1[:, HG * g:HG * g + HG, :], bank(1, HG, P), ACT.Copy).then_inc(sem("E_ot"), 1)

            def inv_std1(b):
                act.wait_ge(sem("E_v"), at("E_v", 2 * b + 2))
                act.wait_ge(sem("E_ln"), at("E_ln", b))
                act.activation(rstd, mv[:, 1:2], ACT.Ln, bias=eps_ln[:, 0:1]).then_inc(sem("E_rs"), 1)
                act.wait_ge(sem("E_rs"), at("E_rs", 2 * b + 1))
                act.activation(rstd, rstd, ACT.Exp, scale=-0.5).then_inc(sem("E_rs"), 1)

            def sequence1(b, first=False, last=False):
                for g in range(NG):
                    n = NG * b + g
                    if not last:
                        copy_q1(n, g)
                    if not (first and g < 1) and not (last and g > 0):
                        softmax1(n - 1, (g - 1) % 2)
                    if not last:
                        if g == 2:
                            copy_x1(b + 1)
                        copy_queries1(n + 1, (g + 1) % 2)
                    if not (first and g < 2) and not (last and g > 1):
                        copy_o1(n - 2, (g - 2) % NG, b if g >= 2 else b - 1)
                    if not last:
                        inv_rms(n + 1, (g + 1) % 2)
                    if g == 3 and not first:
                        inv_std1(b - 1)

            copy_x1(0)
            copy_queries1(0, 0)
            inv_rms(0, 0)
            sequence1(0, first=True)
            with act.Fori(1, NB) as b:
                sequence1(b)
            sequence1(NB, last=True)

            for i in range(KD):
                act.wait_ge(sem("F_fold"), at("F_fold", i + 1 if i == 0 else 2))
                for q in range(4):
                    act.activation(w_ug[:, 1 - i, q * 512:(q + 1) * 512], PS[:, 4 * i + q, :], ACT.Copy,
                                   scale=signs16[:, i:i + 1]).then_inc(sem("F_fu"), 1)
            for i in range(4):
                act.wait_ge(sem("F_xt"), at("F_xt", 2 * i + 2))
                act.activation(xT[:, :, i * 2 * P:(i + 1) * 2 * P].rearrange("p k (b t) -> p b k t", b=2),
                               bank(4 + i, 2, KD, P), ACT.Copy).then_inc(sem("F_xT"), 1)
            with act.Fori(0, NC_) as c:
                nc.scalar.preload_act_table(ACT.Silu)
                for f in range(NF):
                    n = NF * c + f
                    act.wait_ge(sem("F_g"), at("F_g", n + 1))
                    act.wait_ge(sem("F_hid"), at("F_hid", n - 1))
                    act.activation(sgate[:, f % 2, :], PS[:, 2 + f % 2, :], ACT.Silu, scale=ffn_cols[:, f:f + 1])\
                       .then_inc(sem("F_sg"), 1)
                nc.scalar.preload_act_table_set("natural_log_exp_and_others")
                act.wait_ge(sem("F_st"), at("F_st", 9 * c + 9))
                act.activation(rstd4, mv4[:, :, 1], ACT.Ln, bias=eps_ln[:, 0:1]).then_inc(sem("F_rs"), 1)
                act.wait_ge(sem("F_rs"), at("F_rs", 2 * c + 1))
                act.activation(rstd4, rstd4, ACT.Exp, scale=-0.5).then_inc(sem("F_rs"), 1)

        @block.gpsimd
        def _(pool):
            start_counts(pool, "pool")
            pool.memset(X[:, NB, :], 0.0).then_inc(sem("zero"), 1)
            pool.wait_ge(sem("zero"), 1)
            pool.wait_ge(sem("d_x"), 16)

            def fetch_x(st, b, ready):
                if ready is not None:
                    pool.wait_ge(sem(ready), at(ready, b + 1))
                pool.wait_ge(sem(f"{st}_xt"), at(f"{st}_xt", b))
                pool.wait_ge(sem(f"{st}_xb"), at(f"{st}_xb", b))
                pool.tensor_copy(x_now, X[:, b, :]).then_inc(sem(f"{st}_xb"), 1)

            for st, ready in (("A", None), ("B", "A_ln")):
                if ready is not None:
                    pool.wait_ge(sem("A_xt"), at("A_xt", NB + 1))
                    pool.wait_ge(sem("A_xb"), at("A_xb", NB + 1))
                with pool.Fori(0, NB) as b:
                    fetch_x(st, b, ready)
                fetch_x(st, NB, None)

            def weights_lo(e, slot, second):
                raw, hi, lo = (w2_e, w2_hi_f, w2_lo) if second else (w1_e, w1_hi_f, w1_lo)
                pool.wait_ge(sem("C_wh"), at("C_wh", 2 * e + 1 + second))
                pool.tensor_tensor(lo[slot], raw[slot], hi[slot], ALU.subtract).then_inc(sem("C_wl"), 1)

            def experts(pair, last=False):
                for j in range(4):
                    for m in range(2):
                        pool.wait_ge(sem("C_ah"), at("C_ah", 8 * pair + 2 * j + m + 1))
                        pool.tensor_tensor(act_lo[:, j % 2, m, :], act_out[:, m, :], act_hi_f[:, j % 2, m, :],
                                           ALU.subtract).then_inc(sem("C_al"), 1)
                    if not (last and j > 1):
                        weights_lo(2 * pair + 1 + j // 2, (1 + j // 2) % 2, j % 2 == 1)

            for i in range(4):
                pool.wait_ge(sem("C_th"), at("C_th", i + 1))
                cols = slice(i * 2 * P, (i + 1) * 2 * P)
                pool.tensor_tensor(tT_lo[:, :, cols], tT[:, :, cols], tT_hi_f[:, :, cols], ALU.subtract)\
                    .then_inc(sem("C_tl"), 1)
            weights_lo(0, 0, False)
            weights_lo(0, 0, True)
            with pool.Fori(0, NE // 2 - 1) as pair:
                experts(pair)
            experts(NE // 2 - 1, last=True)

            with pool.Fori(0, NC_) as c:
                pool.wait_ge(sem("D_dtu"), at("D_dtu", 2 * c + 1))
                for s in range(NS):
                    for m in range(MD):
                        n = (NS * c + s) * MD + m
                        if m == 0:
                            pool.wait_ge(sem("D_b"), at("D_b", NS * c + s + 1))
                        pool.wait_ge(sem("D_h"), at("D_h", n - 3))
                        pool.tensor_tensor(drive[:, m, :], dtu[:, m, :], b_rep[s % 3], ALU.mult)\
                            .then_inc(sem("D_dbu"), 1)

            trig = lambda t, i: t[:, 32 + i * 512:32 + (i + 1) * 512].rearrange("p (b f) -> p b f", b=NB)
            halves = lambda t: t.rearrange("p (i f) -> p i f", i=2)

            def rotation(dst, i, b, row):
                for kind, (table, w) in enumerate(((cosines, qk_w), (sines, qk_signed))):
                    ins = pool.tensor_tensor(halves(dst[:, kind, :]),
                                             trig(table, i)[:, b, :].unsqueeze(1).broadcast_to([P, 2, 64]),
                                             halves(w[:, row, :]), ALU.mult)
                return ins

            pool.wait_ge(sem("signed"), 1)
            with pool.Fori(0, NB) as b:
                pool.wait_ge(sem("D_ln"), at("D_ln", NB))
                pool.wait_ge(sem("K_xt"), at("K_xt", b))
                pool.wait_ge(sem("K_xb"), at("K_xb", b))
                pool.tensor_copy(x_now1, X[:, b, :]).then_inc(sem("K_xb"), 1)
                pool.wait_ge(sem("K_u"), at("K_u", 2 * b))
                pool.wait_ge(sem("K_tab"), at("K_tab", b))
                pool.sem_inc(sem("pool_go"), 1)
                for i in range(2):
                    ins = rotation(rope_kt[:, i, :, :], i, b, 1)
                ins.then_inc(sem("K_tab"), 1)

            def fetch_x1(b, ready=True):
                pool.wait_ge(sem("E_xt"), at("E_xt", b))
                pool.wait_ge(sem("E_xb"), at("E_xb", b))
                pool.tensor_copy(x_now1, X[:, b, :]).then_inc(sem("E_xb"), 1)

            def move_x(b):
                pool.wait_ge(sem("E_xa"), at("E_xa", b + 1))
                pool.wait_ge(sem("E_q"), at("E_q", NG * b))
                pool.sem_inc(sem("pool_go"), 1)
                pool.tensor_copy(xs1.rearrange("p k t -> p (k t)"), xs_next).then_inc(sem("E_xsp"), 1)

            def square_q(n, slot):
                pool.wait_ge(sem("E_qabs"), at("E_qabs", n + 1))
                pool.wait_ge(sem("E_ss"), at("E_ss", n))
                pool.wait_ge(sem("E_sq"), at("E_sq", n))
                pool.tensor_tensor(q_sq, q_tok1[:, slot, :], q_tok1[:, slot, :], ALU.mult).then_inc(sem("E_sq"), 1)

            def tables_q(b):
                pool.wait_ge(sem("E_u"), at("E_u", NG * b))
                pool.wait_ge(sem("E_tab"), at("E_tab", b))
                pool.sem_inc(sem("pool_go"), 1)
                rotation(rope_qt, 1, b % NB if isinstance(b, int) else b, 0).then_inc(sem("E_tab"), 1)

            def butterflies(b):
                cols = bass.ds(b * 256, 256)
                pool.tensor_tensor(ctxT_flat[:, cols], w_ug[:, 0, cols], w_ug[:, 1, cols], ALU.add)\
                    .then_inc(sem("fly_step"), 1)
                pool.wait_ge(sem("fly_step"), 4 * b + 1)
                pool.sem_inc(sem("pool_go"), 1)
                pool.tensor_tensor(w_ug[:, 0, cols], w_ug[:, 0, cols], w_ug[:, 1, cols], ALU.subtract)
                wd = w_down[:, :, bass.ds(b * 32, 32)]
                buf = [wd, fly[:, 0, :, :], fly[:, 1, :, :], wd]
                for step in range(3):
                    src, dst = buf[step], buf[step + 1]
                    if step > 0:
                        pool.wait_ge(sem("fly_step"), 4 * b + 1 + step)
                        pool.sem_inc(sem("pool_go"), 1)
                    stride = 1 << step
                    for block_ in range(NF // (2 * stride)):
                        lo = slice(2 * stride * block_, 2 * stride * block_ + stride)
                        hi = slice(2 * stride * block_ + stride, 2 * stride * (block_ + 1))
                        pool.tensor_tensor(dst[:, lo, :], src[:, lo, :], src[:, hi, :], ALU.add)
                        ins = pool.tensor_tensor(dst[:, hi, :], src[:, lo, :], src[:, hi, :], ALU.subtract)
                    ins.then_inc(sem("fly_step"), 1)
                pool.wait_ge(sem("fly_step"), 4 * b + 4)
                pool.sem_inc(sem("E_fly"), 1)

            def sequence1(b):
                square_q(NG * b + 1, 1)
                fetch_x1(b + 1)
                square_q(NG * b + 2, 0)
                move_x(b + 1)
                square_q(NG * b + 3, 1)
                tables_q(b + 1)
                square_q(NG * b + 4, 0)
                butterflies(b)

            pool.wait_ge(sem("K_xs"), at("K_xs", NB))
            pool.wait_ge(sem("K_u"), at("K_u", 2 * NB))
            pool.wait_ge(sem("K_cs"), at("K_cs", NB))
            pool.wait_ge(sem("K_xb"), at("K_xb", NB))
            pool.wait_ge(sem("K_tab"), at("K_tab", NB))
            pool.wait_ge(sem("K_kt"), at("K_kt", 2 * NB))
            pool.wait_ge(sem("d_ffn"), 32)
            fetch_x1(0)
            tables_q(0)
            move_x(0)
            square_q(0, 0)
            with pool.Fori(0, NB - 1) as b:
                sequence1(b)
            square_q(NG * (NB - 1) + 1, 1)
            fetch_x1(NB)
            square_q(NG * (NB - 1) + 2, 0)
            move_x(NB)
            square_q(NG * (NB - 1) + 3, 1)
            tables_q(NB)
            square_q(NG * NB, 0)
            butterflies(NB - 1)

        @block.vector
        def _(dve):
            start_counts(dve, "dve")
            steps = [0]

            def link(ins):
                steps[0] += 1
                ins.then_inc(sem("dve_step"), 1)
                dve.wait_ge(sem("dve_step"), steps[0])

            tt, ts = dve.tensor_tensor, dve.tensor_scalar
            dve.memset(eps_ln, LN_EPS).then_inc(sem("eps"), 1)
            dve.memset(one, 1.0).then_inc(sem("eps"), 1)
            dve.memset(eps_rms, RMS_EPS).then_inc(sem("eps"), 1)
            for v in val:
                dve.memset(v[:, :, RK:RK + 1], 1.0).then_inc(sem("ones"), 1)

            def residual4(st, c, bank0):
                xc = X[:, bass.ds(4 * c, 4), :]
                dve.wait_ge(sem(f"{st}_o"), at(f"{st}_o", c + 1))
                tt(z4, xc, PS[:, bank0:bank0 + 2, :].rearrange("p a (b d) -> p (a b) d", b=2), ALU.add)\
                    .then_inc(sem(f"{st}_m"), 1)
                dve.wait_ge(sem(f"{st}_m"), at(f"{st}_m", c + 1))
                for t in range(4):
                    dve.bn_stats(stats4[:, t, :], z4[:, t, :]).then_inc(sem(f"{st}_st"), 1)
                dve.wait_ge(sem(f"{st}_st"), at(f"{st}_st", 9 * c + 4))
                dve.memset(spare, 0.0).then_inc(sem(f"{st}_st"), 1)
                for t in range(4):
                    dve.bn_aggr(mv4[:, t, :], stats4[:, t, :]).then_inc(sem(f"{st}_st"), 1)
                dve.wait_ge(sem(f"{st}_st"), at(f"{st}_st", 9 * c + 9))
                dve.wait_ge(sem(f"{st}_rs"), at(f"{st}_rs", 2 * c + 2))
                for t in range(4):
                    ts(X[:, 4 * c + t, :], z4[:, t, :], mv4[:, t, 0:1], rstd4[:, t:t + 1], ALU.subtract, ALU.mult)\
                        .then_inc(sem(f"{st}_ln"), 1)

            dve.wait_ge(sem("d_ids"), 32)
            dve.wait_ge(sem("d_const"), 16 * N_CONST)
            link(dve.tensor_copy(float_ids[:, :, :], int_ids[:, :, :]))
            for i in range(2):
                dst = angles[:, 32 + i * 512:32 + (i + 1) * 512].rearrange("p (b f) -> p b f", b=NB)
                ins = tt(dst, float_ids[:, i, :].unsqueeze(2).broadcast_to([P, NB, 64]),
                         inv_freq.unsqueeze(1).broadcast_to([P, NB, 64]), ALU.mult)
            link(ins)
            link(ts(sines[:, :], angles[:, :], 1 / (2 * PI), ROUND, ALU.mult, ALU.add))
            link(ts(sines[:, :], sines[:, :], -ROUND, None, ALU.add))
            for part in (TWO_PI_HI, TWO_PI_MID, TWO_PI_LO):
                link(dve.scalar_tensor_tensor(angles[:, :], sines[:, :], -part, angles[:, :], ALU.mult, ALU.add))
            link(ts(cosines[:, :], angles[:, :], PI / 2, -2 * PI, ALU.is_gt, ALU.mult))
            link(dve.scalar_tensor_tensor(cosines[:, :], angles[:, :], PI / 2, cosines[:, :], ALU.add, ALU.add))
            link(ts(cosines[:, :], cosines[:, :], PI_SAFE, -PI_SAFE, ALU.min, ALU.max))
            ts(sines[:, :], angles[:, :], PI_SAFE, -PI_SAFE, ALU.min, ALU.max).then_inc(sem("ang"), 1)
            dve.wait_ge(sem("trig"), 2)
            for i in range(2):
                dve.tensor_copy(rope_0[:, 0, 32 * i:32 * i + 32], cosines[:, 0:32])
            dve.tensor_copy(rope_0[:, 1, 0:32], sines[:, 0:32])
            link(ts(rope_0[:, 1, 32:64], sines[:, 0:32], -1.0, None, ALU.mult))
            dve.memset(eps_q, RMS_EPS * DH).then_inc(sem("eps"), 1)

            def keys_values(st):
                s = st.s
                raw = PS[:, 0:2, :].rearrange("p c (a d) -> p (c a) d", a=4)
                dve.wait_ge(s("kvp"), at(st.name + "_kvp", 1))
                if st.x:
                    dve.tensor_copy(st.val[:, :, 0:RK], raw[:, :, 0:RK]).then_inc(s("kvr"), 1)
                    dve.wait_ge(sem("A_kvt"), at("A_kvt", 1))
                else:
                    for b in range(NB):
                        dve.bn_stats(stats8[:, b, :], raw[:, b, 0:RK]).then_inc(s("v"), 1)
                    dve.wait_ge(s("v"), at(st.name + "_v", NB))
                    for b in range(NB):
                        dve.bn_aggr(mv8[:, b, :], stats8[:, b, :]).then_inc(s("v"), 1)
                    dve.wait_ge(s("v"), at(st.name + "_v", 2 * NB))
                    wide = [P, NB, RK]
                    v = st.val[:, :, 0:RK]
                    link(tt(v, raw[:, :, 0:RK], mv8[:, :, 0:1].broadcast_to(wide), ALU.subtract))
                    dve.wait_ge(s("kvrs"), at(st.name + "_kvrs", 1))
                    link(tt(v, v, rstd8.unsqueeze(2).broadcast_to(wide), ALU.mult))
                    link(tt(v, v, gamma.unsqueeze(1).broadcast_to(wide), ALU.mult))
                    tt(v, v, beta.unsqueeze(1).broadcast_to(wide), ALU.add).then_inc(s("kvn"), 1)
                    dve.wait_ge(s("kvp"), at(st.name + "_kvp", 1))
                    dve.memset(stats6, 0.0).then_inc(s("kvr"), 1)
                wide = [P, NB, RR]
                u = place(area_2, 10640, NB, RR)
                w = place(area_2, 11152, NB, RR)
                tt(u, raw[:, :, RK:], st.rope[:, 0, :].unsqueeze(1).broadcast_to(wide), ALU.mult)
                link(tt(w, raw[:, :, RK:], st.rope[:, 1, :].unsqueeze(1).broadcast_to(wide), ALU.mult))
                v4 = lambda t: t.rearrange("p b (i f) -> p b i f", i=2)
                tt(v4(k_tok[:, :, RK:]), v4(u), v4(w)[:, :, ::-1, :], ALU.add).then_inc(s("kvr"), 1)

            def attend(st):
                s = st.s
                cc = st.rope[:, 0, :].unsqueeze(1).broadcast_to([P, HG, RR])
                sn = st.rope[:, 1, :].unsqueeze(1).broadcast_to([P, HG, RR])

                def rotate(n, slot):
                    q = place_q(slot)[:, :, RK:]
                    u = rope_u[:, slot % 2, :].rearrange("p (h d) -> p h d", h=HG)
                    w = rope_v[:, slot % 2, :].rearrange("p (h d) -> p h d", h=HG)
                    dve.wait_ge(s("qabs"), at(st.name + "_qabs", n + 1))
                    tt(u, q, cc, ALU.mult)
                    tt(w, q, sn, ALU.mult).then_inc(s("u"), 1)
                    dve.wait_ge(s("u"), at(st.name + "_u", n + 1))
                    v4 = lambda t: t.rearrange("p h (i f) -> p h i f", i=2)
                    tt(v4(place_q(slot)[:, :, RK:]), v4(u), v4(w)[:, :, ::-1, :], ALU.add).then_inc(s("rope"), 1)

                def maximum(n, b, g):
                    dve.wait_ge(s("sc"), at(st.name + "_sc", n + 1))
                    dve.wait_ge(s("exp"), at(st.name + "_exp", n - 1))
                    src = bank(2 + g % 2, HG, P)
                    if st.x:
                        m = masked[:, g % 2, :].rearrange("p (h k) -> p h k", h=HG)
                        tt(m, src, band[:, b, :].unsqueeze(1).broadcast_to([P, HG, P]), ALU.add).then_inc(s("sm"), 1)
                        dve.wait_ge(s("sm"), at(st.name + "_sm", 2 * n + 1))
                        src = m
                    dve.tensor_reduce(negmax[:, g % 2, :], src, AX_X, ALU.max, negate=True).then_inc(s("sm"), 1)
                    dve.wait_ge(s("sm"), at(st.name + "_sm", 2 * n + 2 if st.x else n + 1))
                    ts(negmax[:, g % 2, :], negmax[:, g % 2, :], st.scale, None, ALU.mult).then_inc(s("max"), 1)

                def copy_p(n):
                    dve.wait_ge(s("tp"), at(st.name + "_tp", n + 1))
                    dve.wait_ge(s("pv"), at(st.name + "_pv", n))
                    dve.tensor_copy(probT, PS[:, 4, :]).then_inc(s("pt"), 1)

                def normalise(n):
                    dve.wait_ge(s("pv"), at(st.name + "_pv", n + 1))
                    dve.wait_ge(s("to"), at(st.name + "_to", n))
                    o = bank(5, HG, RK + 1)
                    dve.reciprocal(rinv[:, 0, :], o[:, :, RK]).then_inc(s("band"), 1)
                    dve.wait_ge(s("band"), at(st.name + "_band", n + 1))
                    tt(o_norm.rearrange("p (h d) -> p h d", h=HG), o[:, :, 0:RK],
                       rinv[:, 0, :].unsqueeze(2).broadcast_to([P, HG, RK]), ALU.mult).then_inc(s("on"), 1)

                def residual(b):
                    dve.wait_ge(s("y"), at(st.name + "_y", b + 1))
                    tt(z, X[:, b, :], PS[:, 7, 0:D], ALU.add).then_inc(s("lna"), 1)
                    dve.wait_ge(s("lna"), at(st.name + "_lna", b + 1))
                    dve.bn_stats(stats6, z).then_inc(s("v"), 1)
                    dve.wait_ge(s("v"), at(st.name + "_v", V_BASE[st.name] + 2 * b + 1))
                    dve.memset(spare, 0.0)
                    dve.bn_aggr(mv, stats6).then_inc(s("v"), 1)

                def layernorm(b):
                    dve.wait_ge(s("v"), at(st.name + "_v", V_BASE[st.name] + 2 * b + 2))
                    dve.wait_ge(s("rs"), at(st.name + "_rs", 2 * b + 2))
                    ts(X[:, b, :], z, mv[:, 0:1], rstd[:, 0:1], ALU.subtract, ALU.mult).then_inc(s("ln"), 1)

                def sequence(b, first=False, last=False):
                    for g in range(NG):
                        n = NG * b + g
                        if not (first and g < 2) and not (last and g > 1):
                            normalise(n - 2)
                        if not last:
                            rotate(n + 1, g + 1)
                            maximum(n, b, g)
                        if not (first and g < 1) and not (last and g > 0):
                            copy_p(n - 1)
                        if g == 2 and not first:
                            residual(b - 1)
                        if g == 3 and not first:
                            layernorm(b - 1)

                rotate(0, 0)
                sequence(0, first=True)
                with dve.Fori(1, NB) as b:
                    sequence(b)
                sequence(NB, last=True)

            keys_values(stages[0])
            keys_values(stages[1])
            for b in range(NB):
                bb = band[:, b, :]
                link(ts(bb, key_ids, float_ids[:, 2, b:b + 1], -1e30, ALU.is_gt, ALU.mult))
                link(ts(z[:, 0:P], key_ids, float_ids[:, 2, b:b + 1], -8.0, ALU.subtract, ALU.is_lt))
                link(dve.scalar_tensor_tensor(bb, z[:, 0:P], -1e30, bb, ALU.mult, ALU.add))
            dve.wait_ge(sem("B_kvt"), at("B_kvt", 1))
            attend(stages[0])
            attend(stages[1])

            dve.wait_ge(sem("d_rows"), 64)
            ts(qk_signed[:, :, 0:64], qk_w[:, :, 0:64], 1.0, None, ALU.mult)
            ts(signs16, ffn_cols[:, 16:18], 1.0 / 16, None, ALU.mult)
            ts(qk_signed[:, :, 64:], qk_w[:, :, 64:], -1.0, None, ALU.mult).then_inc(sem("signed"), 1)

            dve.wait_ge(sem("C_r"), at("C_r", 3))
            for b in range(NB):
                dve.scalar_tensor_tensor(t_tok[:, b, :], X[:, b, :], ssq8[:, b:b + 1], norm_w, ALU.mult, ALU.mult)\
                   .then_inc(sem("C_t"), 1)
            dve.wait_ge(sem("d_moe"), 48)
            ts(b2_bias, b1[:, :, 2:4], 1.0, None, ALU.add)
            dve.memset(logits[:, :, NE:], -3e38)
            dve.wait_ge(sem("C_lg"), at("C_lg", 1))
            link(tt(logits[:, :, 0:NE], bank(4, NB, NE), gate_b.unsqueeze(1).broadcast_to([P, NB, NE]), ALU.add))
            for b in range(NB):
                ins = dve.max(top8[:, b, :], logits[:, b, 0:NE])
            link(ins)
            tt(expl, logits[:, :, 0:NE], top8[:, :, 0:1].broadcast_to([P, NB, NE]), ALU.subtract)\
                .then_inc(sem("C_lgs"), 1)
            link(dve.memset(top8[:, :, TOPK:], -3e38))
            for b in range(NB):
                ins = dve.match_replace(picked[:, b, :], top8[:, b, :], logits[:, b, :], 3e38)
            link(ins)
            link(ts(picked, picked, 3e38, None, ALU.is_equal))
            dve.wait_ge(sem("C_e"), at("C_e", 1))
            link(tt(expl, expl, picked[:, :, 0:NE], ALU.mult))
            link(dve.tensor_reduce(gsum, expl, AX_X, ALU.add))
            link(dve.reciprocal(gsum, gsum))
            tt(gates, expl, gsum.unsqueeze(2).broadcast_to([P, NB, NE]), ALU.mult).then_inc(sem("C_g"), 1)

            def half_hidden(k, m, e):
                n = 2 * k + m
                dve.wait_ge(sem("C_ha"), at("C_ha", n + 1))
                dve.wait_ge(sem("C_gl"), at("C_gl", n - 1))
                ts(act_lin[:, m, :], PS[:, 2 * m, :], b1[:, e, m:m + 1], 7.0, ALU.add, ALU.min)\
                    .then_inc(sem("C_lin"), 1)
                dve.wait_ge(sem("C_hb"), at("C_hb", n + 1))
                dve.wait_ge(sem("C_act"), at("C_act", n - 1))
                ts(act_up[:, m, :], PS[:, 2 * m + 1, :], b2_bias[:, e, m:m + 1], -6.0, ALU.add, ALU.max)\
                    .then_inc(sem("C_up"), 1)

            def activate(k, m, c):
                n = 2 * k + m
                dve.wait_ge(sem("C_gl"), at("C_gl", n + 1))
                dve.wait_ge(sem("C_up"), at("C_up", n + 1))
                dve.wait_ge(sem("C_al"), at("C_al", n - 1))
                dve.scalar_tensor_tensor(act_out[:, m, :], act_up[:, m, :], 8.0, act_gl[:, m, :], ALU.min, ALU.mult)\
                   .then_inc(sem("C_act"), 1)

            def accumulate(k, c, e):
                dve.wait_ge(sem("C_y"), at("C_y", k + 1))
                dve.wait_ge(sem("C_acc"), at("C_acc", k - 1))
                for t in range(4):
                    b = 4 * c + t
                    ins = dve.scalar_tensor_tensor(X[:, b, :], bank(4 + 2 * c + t // 2, 2, D)[:, t % 2, :],
                                                   gates[:, b, bass.ds(e, 1)], X[:, b, :], ALU.mult, ALU.add)
                ins.then_inc(sem("C_acc"), 1)

            def experts(pair, first=False, last=False):
                for j in range(4):
                    k = 4 * pair + j
                    if not last:
                        for m in range(2):
                            half_hidden(k, m, 2 * pair + j // 2)
                        for m in range(2):
                            activate(k, m, j % 2)
                    if first and j == 0:
                        dve.wait_ge(sem("C_gb"), at("C_gb", 1))
                        for b in range(NB):
                            ins = dve.scalar_tensor_tensor(X[:, b, :], X[:, b, :], 2.0, bank(4 + b // 2, 2, D)[:, b % 2, :],
                                                           ALU.mult, ALU.add)
                        ins.then_inc(sem("C_x"), 1)
                        dve.wait_ge(sem("C_x"), at("C_x", 1))
                    elif not (last and j > 0):
                        accumulate(k - 1, (j - 1) % 2, 2 * pair + (0 if j >= 1 else -1) + (1 if j > 2 else 0))

            experts(0, first=True)
            with dve.Fori(1, NE // 2) as pair:
                experts(pair)
            experts(NE // 2, last=True)
            dve.wait_ge(sem("C_acc"), at("C_acc", 2 * NE))
            for b in range(NB):
                dve.bn_stats(stats8[:, b, :], X[:, b, :]).then_inc(sem("C_v2"), 1)
            dve.wait_ge(sem("C_v2"), at("C_v2", NB))
            for b in range(NB):
                dve.bn_aggr(mv8[:, b, :], stats8[:, b, :]).then_inc(sem("C_v2"), 1)
            dve.wait_ge(sem("C_rs"), at("C_rs", 2))
            dve.wait_ge(sem("C_v2"), at("C_v2", 2 * NB))
            for b in range(NB):
                ts(X[:, b, :], X[:, b, :], mv8[:, b, 0:1], rstd8[:, b:b + 1], ALU.subtract, ALU.mult)\
                    .then_inc(sem("C_ln"), 1)

            dve.wait_ge(sem("d_ssm"), 16)
            dve.wait_ge(sem("A_log"), 1)
            link(ts(ssm_cols[:, :, 6:22], ssm_cols[:, :, 6:22], -1.0, None, ALU.mult))
            with dve.Fori(0, NC_) as c:
                tok = lambda t, m: t[:, m, :].rearrange("p (b t) -> p b t", b=4)
                for m in range(MD):
                    n = MD * c + m
                    xp, u4 = bank(m, 4, P), tok(u_c, m)
                    dve.wait_ge(sem("D_c1"), at("D_c1", n + 1))
                    dve.scalar_tensor_tensor(u4[:, :, 1:], xp[:, :, 0:P - 1], ssm_cols[:, m, 0:1], u4[:, :, 1:],
                                             ALU.mult, ALU.add).then_inc(sem("D_cv"), 1)
                    dve.wait_ge(sem("D_cv"), at("D_cv", 2 * n + 1))
                    dve.scalar_tensor_tensor(u4[:, :, 0:P - 1], xp[:, :, 1:], ssm_cols[:, m, 2:3], u4[:, :, 0:P - 1],
                                             ALU.mult, ALU.add).then_inc(sem("D_cv"), 1)
                dve.wait_ge(sem("D_dtp"), at("D_dtp", c + 1))
                for m in range(MD):
                    ins = ts(dt[:, m, :], PS[:, m, :], ssm_cols[:, m, 4:5], None, ALU.add)
                ins.then_inc(sem("D_v"), 1)
                dve.wait_ge(sem("D_v"), at("D_v", c + 1))
                dve.wait_ge(sem("D_sp"), at("D_sp", 3 * c + 3))
                dve.scalar_tensor_tensor(dt, dt, 0.0, sp_tmp, ALU.max, ALU.add).then_inc(sem("D_dt"), 1)
                dve.wait_ge(sem("D_dt"), at("D_dt", c + 1))
                tt(dtu, dt, u_c, ALU.mult).then_inc(sem("D_dtu"), 1)
                dve.wait_ge(sem("D_dtu"), at("D_dtu", 2 * c + 1))
                dve.memset(dt.rearrange("p m (b t) -> p m b t", b=4)[:, :, :, 0], 1e37).then_inc(sem("D_dtu"), 1)

                def step_state(s, m):
                    n = (NS * c + s) * MD + m
                    dve.wait_ge(sem("D_da"), at("D_da", n + 1))
                    dve.wait_ge(sem("D_dbu"), at("D_dbu", n + 1))
                    dve.wait_ge(sem("D_hc"), at("D_hc", n - 3))
                    dve.tensor_tensor_scan(state[:, m, :], decay[:, m, :], drive[:, m, :], 0.0,
                                           ALU.mult, ALU.add).then_inc(sem("D_h"), 1)

                def read_state(s, m):
                    n = (NS * c + s) * MD + m
                    dve.wait_ge(sem("D_h"), at("D_h", n + 1))
                    dve.wait_ge(sem("D_y"), at("D_y", n - 3))
                    if m == 0:
                        dve.wait_ge(sem("D_rep"), at("D_rep", NS * c + s + 1))
                    tt(read_out[:, m, :], state[:, m, :], PS[:, 6 + s % 2, :], ALU.mult).then_inc(sem("D_hc"), 1)

                step_state(0, 0)
                for i in range(1, NS * MD):
                    step_state(i // MD, i % MD)
                    read_state((i - 1) // MD, (i - 1) % MD)
                read_state(NS - 1, MD - 1)
                dve.wait_ge(sem("D_y"), at("D_y", (c + 1) * NS * MD))
                for m in range(MD):
                    ins = dve.scalar_tensor_tensor(yg[:, m, :], u_c[:, m, :], ssm_cols[:, m, 5:6], PS[:, m, :],
                                                   ALU.mult, ALU.add)
                ins.then_inc(sem("D_rd"), 1)
                dve.wait_ge(sem("D_rd"), at("D_rd", c + 1))
                tt(yg, yg, sz, ALU.mult).then_inc(sem("D_yg"), 1)
                residual4("D", c, 0)

            dve.wait_ge(sem("D_ln"), at("D_ln", NB))
            heads = lambda t: t.rearrange("p (h d) -> p h d", h=HG)
            swapped = lambda t: t.rearrange("p (h i f) -> p h i f", h=HG, i=2)

            def keys_dve(b):
                for half in range(2):
                    n = 2 * b + half
                    if half == 0:
                        dve.wait_ge(sem("K_tab"), at("K_tab", b + 1))
                    dve.wait_ge(sem("K_sq"), at("K_sq", n + 1))
                    dve.wait_ge(sem("K_kx"), at("K_kx", n))
                    tab = rope_kt[:, half, :, :]
                    tt(heads(rope_u1), bank(half, HG, DH), tab[:, 0, :].unsqueeze(1).broadcast_to([P, HG, DH]), ALU.mult)
                    tt(heads(rope_v1), bank(half, HG, DH), tab[:, 1, :].unsqueeze(1).broadcast_to([P, HG, DH]), ALU.mult)\
                        .then_inc(sem("K_u"), 1)
                    dve.wait_ge(sem("K_rs"), at("K_rs", 2 * n - 2))
                    dve.tensor_reduce(sumsq[:, half, :], heads(squares[:, half, :]), AX_X, ALU.add)\
                       .then_inc(sem("K_ss"), 1)
                    dve.wait_ge(sem("K_u"), at("K_u", n + 1))
                    dve.wait_ge(sem("K_kt"), at("K_kt", n - 1))
                    dve.wait_ge(sem("K_kr"), at("K_kr", n - 1))
                    tt(swapped(k_tok1[:, half, :]), swapped(rope_u1), swapped(rope_v1)[:, :, ::-1, :], ALU.add)\
                        .then_inc(sem("K_kx"), 1)
                for half in range(2):
                    n = 2 * b + half
                    dve.wait_ge(sem("K_kx"), at("K_kx", n + 1))
                    dve.wait_ge(sem("K_rs"), at("K_rs", 2 * n + 2))
                    tt(heads(k_tok1[:, half, :]), heads(k_tok1[:, half, :]),
                       rms[:, half, :].unsqueeze(2).broadcast_to([P, HG, DH]), ALU.mult).then_inc(sem("K_kr"), 1)

            with dve.Fori(0, NB) as b:
                keys_dve(b)

            def rotate1(n, slot):
                if slot == 0:
                    dve.wait_ge(sem("E_tab"), at("E_tab", n_seq[0] + 1))
                dve.wait_ge(sem("E_qabs"), at("E_qabs", n + 1))
                dve.wait_ge(sem("E_rope"), at("E_rope", n))
                tt(heads(rope_u1), heads(q_tok1[:, slot, :]), rope_qt[:, 0, :].unsqueeze(1).broadcast_to([P, HG, DH]), ALU.mult)
                tt(heads(rope_v1), heads(q_tok1[:, slot, :]), rope_qt[:, 1, :].unsqueeze(1).broadcast_to([P, HG, DH]), ALU.mult)\
                    .then_inc(sem("E_u"), 1)
                dve.wait_ge(sem("E_sq"), at("E_sq", n + 1))
                dve.wait_ge(sem("E_rq"), at("E_rq", 2 * n - 2))
                dve.tensor_reduce(sumsq[:, slot, :], heads(q_sq), AX_X, ALU.add).then_inc(sem("E_ss"), 1)
                dve.wait_ge(sem("E_u"), at("E_u", n + 1))
                tt(swapped(q_tok1[:, slot, :]), swapped(rope_u1), swapped(rope_v1)[:, :, ::-1, :], ALU.add)\
                    .then_inc(sem("E_rope"), 1)

            def maximum1(n, slot):
                dve.wait_ge(sem("E_sc"), at("E_sc", n + 1))
                dve.wait_ge(sem("E_exp"), at("E_exp", n - 1))
                dve.tensor_reduce(negmax[:, slot, :], PS[:, 2:4, :].rearrange("p a (j k) -> p (a j) k", j=2), AX_X, ALU.max,
                                  negate=True).then_inc(sem("E_nm"), 1)
                dve.wait_ge(sem("E_nm"), at("E_nm", n + 1))
                dve.wait_ge(sem("E_rq"), at("E_rq", 2 * n + 2))
                tt(negmax[:, slot, :], negmax[:, slot, :], rms[:, slot, :], ALU.mult).then_inc(sem("E_max"), 1)

            def copy_p1(n):
                dve.wait_ge(sem("E_tp"), at("E_tp", n + 1))
                dve.wait_ge(sem("E_pv"), at("E_pv", n))
                dve.tensor_copy(probT1, PS[:, 4:6, :]).then_inc(sem("E_pt"), 1)

            def normalise1(n, slot):
                dve.wait_ge(sem("E_pv"), at("E_pv", n + 1))
                dve.wait_ge(sem("E_to"), at("E_to", n))
                dve.reciprocal(rinv[:, 0, :], prob_sum[:, slot, :]).then_inc(sem("E_rc"), 1)
                dve.wait_ge(sem("E_rc"), at("E_rc", n + 1))
                tt(heads(o_norm1), bank(6, HG, DH), rinv[:, 0, :].unsqueeze(2).broadcast_to([P, HG, DH]), ALU.mult)\
                    .then_inc(sem("E_on"), 1)

            def residual1(b):
                dve.wait_ge(sem("E_y"), at("E_y", b + 1))
                tt(z1, X[:, b, :], PS[:, 7, 0:D], ALU.add).then_inc(sem("E_lna"), 1)
                dve.wait_ge(sem("E_lna"), at("E_lna", b + 1))
                dve.bn_stats(stats6, z1).then_inc(sem("E_v"), 1)
                dve.wait_ge(sem("E_v"), at("E_v", 2 * b + 1))
                dve.memset(spare, 0.0)
                dve.bn_aggr(mv, stats6).then_inc(sem("E_v"), 1)

            def layernorm1(b):
                dve.wait_ge(sem("E_v"), at("E_v", 2 * b + 2))
                dve.wait_ge(sem("E_rs"), at("E_rs", 2 * b + 2))
                ts(X[:, b, :], z1, mv[:, 0:1], rstd[:, 0:1], ALU.subtract, ALU.mult).then_inc(sem("E_ln"), 1)

            n_seq = [0]

            def sequence1(b, first=False, last=False):
                for g in range(NG):
                    n = NG * b + g
                    n_seq[0] = b
                    if not (first and g < 2) and not (last and g > 1):
                        normalise1(n - 2, g % 2)
                    if not last:
                        n_seq[0] = b + (g + 1) // NG
                        rotate1(n + 1, (g + 1) % 2)
                        maximum1(n, g % 2)
                    if not (first and g < 1) and not (last and g > 0):
                        copy_p1(n - 1)
                    if g == 2 and not first:
                        residual1(b - 1)
                    if g == 3 and not first:
                        layernorm1(b - 1)

            dve.wait_ge(sem("K_kt"), at("K_kt", 2 * NB))
            rotate1(0, 0)
            sequence1(0, first=True)
            with dve.Fori(1, NB) as b:
                sequence1(b)
            sequence1(NB, last=True)

            dve.wait_ge(sem("F_fd"), at("F_fd", 1))
            for f in range(NF):
                ins = ts(w_down[:, f, :], PS[:, f // 2, (f % 2) * D:(f % 2 + 1) * D], ffn_cols[:, 18 + f:19 + f], 1.0 / 32,
                         ALU.mult, ALU.mult)
            ins.then_inc(sem("F_fe"), 1)
            dve.wait_ge(sem("F_fe"), at("F_fe", 1))
            tt(w_down, w_down, wsd.unsqueeze(1).broadcast_to([P, NF, D]), ALU.mult).then_inc(sem("F_fe"), 1)
            with dve.Fori(0, NC_) as c:
                for f in range(NF):
                    n = NF * c + f
                    dve.wait_ge(sem("F_up"), at("F_up", n + 1))
                    dve.wait_ge(sem("F_sg"), at("F_sg", n + 1))
                    if f == 0:
                        dve.wait_ge(sem("F_o"), at("F_o", c))
                    dve.scalar_tensor_tensor(hid[:, f, :], PS[:, f % 2, :], ffn_cols[:, 8 + f:9 + f], sgate[:, f % 2, :],
                                             ALU.mult, ALU.mult).then_inc(sem("F_hid"), 1)
                residual4("F", c, 4)



def layouts(v):
    import numpy as np

    def rows(w, k=P):
        return w.reshape(-1, k, w.shape[-1]).transpose(1, 0, 2)

    def halves(w):
        return np.concatenate([w[..., 0::2], w[..., 1::2]], axis=-1)

    x, c = v["x"], v["ctx_2048"]
    o = {"x": x.transpose(1, 0, 2), "xT": rows(x.reshape(NT, D).T), "ctxT": rows(c.reshape(NT, D).T)}
    o["ids"] = np.stack([v["pos_BxS2"].T, v["itok_BxS_4096_4607"].T, v["itok_BxS_0_1023"].T], axis=1)
    o["freqs"] = v["L0_attn_freqs_cis"][0:P]
    wq = v["L0_attn_Wq"].reshape(D, NH, DH + RR)
    o["a_wqnT"] = wq[:, :, 0:DH].transpose(2, 1, 0)
    o["a_wqr"] = halves(wq[:, :, DH:]).reshape(KD, P, NH, RR).transpose(1, 0, 2, 3)
    kva = v["L0_attn_Wkv_a"]
    o["a_wkva"] = rows(np.concatenate([kva[:, 0:RK], halves(kva[:, RK:])], axis=1))
    kvb = v["L0_attn_Wkv_b"].reshape(RK, NH, 2 * DH)
    o["a_wkbT"] = kvb[:, :, 0:DH].transpose(2, 1, 0)
    o["a_wvbT"] = kvb[:, :, DH:].transpose(2, 1, 0)
    o["a_wout"] = v["L0_attn_Wout"].reshape(NH, DH, D).transpose(1, 0, 2)
    o["gamma"], o["beta"] = v["L0_attn_kv_gamma"], v["L0_attn_kv_beta"]
    o["b_wdq"], o["b_wkvc"], o["b_wkr"] = rows(v["L0_xattn_W_dq"]), rows(v["L0_xattn_W_kvc"]), v["L0_xattn_W_kr"]
    o["b_wuqT"] = v["L0_xattn_W_uq"].reshape(QC, NH, DH).transpose(2, 1, 0)
    o["b_wukT"] = v["L0_xattn_W_uk"].reshape(RK, NH, DH).transpose(2, 1, 0)
    o["b_wuvT"] = v["L0_xattn_W_uv"].reshape(RK, NH, DH).transpose(2, 1, 0)
    o["b_wqr"] = v["L0_xattn_W_qr"].reshape(QC, NH, RR)
    o["b_wo"] = v["L0_xattn_W_o"].reshape(NH, DH, D).transpose(1, 0, 2)
    w1 = v["L0_ffn_w1"]
    w1 = np.concatenate([w1[:, 0::2], w1[:, 1::2]], axis=1)
    o["w1"] = w1.transpose(0, 2, 1).reshape(NE, KD, P, 512).transpose(0, 2, 1, 3)
    b1 = v["L0_ffn_b1"]
    o["b1"] = np.concatenate([b1[:, 0::2], b1[:, 1::2]], axis=1).reshape(NE, 4, P).transpose(2, 0, 1)
    o["w2"] = v["L0_ffn_w2"].transpose(0, 2, 1).reshape(NE, KD, P, D).transpose(0, 2, 1, 3)
    o["b2"], o["gate_w"] = v["L0_ffn_b2"], rows(v["L0_ffn_gate_w"].T)
    o["w_in"], o["w_x"], o["w_dt"] = rows(v["L1_attn_W_in"]), rows(v["L1_attn_W_x"]), v["L1_attn_W_dt"]
    o["w_ssm"] = rows(v["L1_attn_W_out"])
    col = lambda w: w.reshape(MD, P, -1)
    cols = [col(v["L1_attn_conv_w"]), col(v["L1_attn_conv_b"]), col(v["L1_attn_b_dt"]), col(v["L1_attn_D"]),
            col(v["L1_attn_A_log"]), np.zeros((MD, P, 2), np.float32)]
    o["ssm_cols"] = np.concatenate(cols, axis=2).transpose(1, 0, 2)
    o["e_wq"], o["e_wk"], o["e_wv"] = (rows(v[f"L1_xattn_W{n}"].T) for n in "qkv")
    o["e_wo"] = v["L1_xattn_Wo"].T.reshape(NH, DH, D).transpose(1, 0, 2)
    o["q_norm"], o["k_norm"] = v["L1_xattn_q_norm_w"], v["L1_xattn_k_norm_w"]
    o["w_ug"] = rows(np.concatenate([v["L1_ffn_W_up"], v["L1_ffn_W_gate"]], axis=0).T)
    o["w_down"] = rows(v["L1_ffn_W_down"].T)
    ws = v["L1_ffn_Wscale_ug"].reshape(2, NF, P)
    cols = [ws[1].T, ws[0].T, v["L1_ffn_SU_ug"].reshape(KD, P).T, v["L1_ffn_SU_dp"].reshape(NF, P).T]
    o["ffn_cols"], o["ws_down"] = np.concatenate(cols, axis=1), v["L1_ffn_Wscale_dp"]
    o["norm_w"], o["gate_b"] = v["L0_ffn_norm_w"], v["L0_ffn_gate_b"]
    h = np.array([[1.0]])
    while h.shape[0] < P:
        h = np.block([[h, h], [h, -h]])
    o["consts"] = np.concatenate([np.eye(P), h, np.tile(np.arange(P), (P, 1))], axis=1).astype(np.float32)
    f32 = np.float32
    inv = (f32(1.0) / f32(10000.0) ** (np.arange(RR // 2, dtype=f32) / f32(RR // 2))).astype(f32)
    ang = (np.arange(P, dtype=f32)[:, None] * inv).astype(np.float64)
    cs, sn = np.cos(ang), np.sin(ang)
    o["rope_x"] = np.stack([np.concatenate([cs, cs], 1), np.concatenate([sn, -sn], 1)], axis=1).astype(f32)
    inv = (f32(1.0) / f32(10000.0) ** (np.arange(0, DH, 2, dtype=f32) / f32(DH))).astype(f32)
    o["inv_freq"] = np.tile(inv, (P, 1))
    return {k: np.ascontiguousarray(w) for k, w in o.items()}


def kernel(**inputs):
    import numpy as np
    import concourse.bacc as bacc
    from concourse.bass_utils import run_bass_kernel_spmd

    arrays = layouts({k: np.asarray(v) for k, v in inputs.items()})
    nc = bacc.Bacc("TRN2", target_bir_lowering=False, num_devices=1)
    aps = {k: nc.dram_tensor(k, w.shape, mybir.dt.from_np(w.dtype), kind="ExternalInput").ap()
           for k, w in arrays.items()}
    out = nc.dram_tensor("out", (P, NB, D), F32, kind="ExternalOutput").ap()
    build(nc, aps, out)
    r = run_bass_kernel_spmd(nc, [arrays], core_ids=[0])
    return np.ascontiguousarray(r.results[0]["out"].transpose(1, 0, 2))
```

```python
from contextlib import ExitStack

import concourse.bass as bass
from concourse import mybir

F32 = mybir.dt.float32
F32R = mybir.dt.float32r
I32 = mybir.dt.int32
ALU = mybir.AluOpType
ACT = mybir.ActivationFunctionType
AX_X = mybir.AxisListType.X

P = 128
NB = 8
D = 256
KD = D // P
NT = NB * P
NH = 16
HG = 4
NG = NH // HG
RK = 64
RR = 64
DH = 128
QC = 96
NE = 16
TOPK = 4
DI = 512
MD = DI // P
NS = 16
DTR = 128
KVH = 4
FF = 1024
NF = FF // P
LN_EPS = 1e-5
RMS_EPS = 1e-6
CHUNK = 512
NC_ = NT // CHUNK
BC_AFTER = 2
CREDIT = 6

PI = 3.14159265358979
TWO_PI_HI = 6.28125
TWO_PI_MID = 0.0019350051879882812
TWO_PI_LO = 2 * PI - TWO_PI_HI - TWO_PI_MID
ROUND = 12582912.0
PI_SAFE = 3.1415925


GROUPS = NB * NG
ATTEND = dict(xt=NB + 1, q=GROUPS + 1, tq=GROUPS, sc=GROUPS, tp=GROUPS, pv=GROUPS, to=GROUPS, y=GROUPS, xs=NB + 1,
              qabs=GROUPS + 1, qt=GROUPS, exp=GROUPS, ot=GROUPS, rs=2 * NB, u=GROUPS + 1, rope=GROUPS + 1, max=GROUPS,
              pt=GROUPS, on=GROUPS, ln=NB, lna=NB, xb=NB + 1, band=GROUPS)
EVENTS = {
    "A": dict(ATTEND, xl=NB + 1, v=4 * NB, sm=GROUPS, kvp=1, kvt=1, kvr=2, kvc=2, kve=1),
    "B": dict(ATTEND, v=2 * NB, sm=2 * GROUPS, kvp=1, kvt=1, kvr=2, kvc=2, kve=1),
    "C": dict(y=2 * NE, rs=2, ln=NB),
    "K": dict(xt=NB, xs=NB, rs=4 * NB, u=2 * NB, xb=NB, q=2 * NB, pv=2 * NB, tab=NB, ss=2 * NB),
    "E": dict(xt=NB + 1, rs=2 * NB, ln=NB),
    "D": dict(xt=NB, xT=4, ln=NB, m=2 * NC_, st=10 * NC_, rs=2 * NC_, o=2 * NC_),
}
ORDER = "ABCDKEF"


def physical(name):
    st, _, n = name.partition("_")
    if st in ORDER:
        for first in ORDER[:ORDER.index(st)]:
            if n in EVENTS[first]:
                return f"{first}_{n}"
    return name


def at(name, n):
    st, _, short = name.partition("_")
    return n + CREDIT + sum(EVENTS[x].get(short, 0) for x in ORDER[:ORDER.index(st)])


def build(nc, a, out):
    ctx = ExitStack()
    with ctx:
        sems = {}

        def sem(name):
            name = physical(name)
            if name not in sems:
                sems[name] = ctx.enter_context(nc.semaphore(name))
            return sems[name]

        def sb(name, shape, dt=F32):
            return ctx.enter_context(nc.sbuf_tensor(f"{name}_sb", shape, dt))

        X = sb("X", [P, NB + 1, D])
        consts = sb("consts", [P, 3 * P])
        ident, hadamard, key_ids = consts[:, 0:P], consts[:, P:2 * P], consts[:, 2 * P:3 * P]
        small = sb("small", [P, 2256])
        angles = sb("angles", [P, 32 + 2 * NB * 64])
        cosines = sb("cosines", [P, 32 + 2 * NB * 64])
        sines = sb("sines", [P, 32 + 2 * NB * 64])
        AREA_0, AREA_G, AREA_1, AREA_2 = 10240, 16640, 24320, 28800

        def parts(start, n):
            with ExitStack() as here:
                if start > 0:
                    here.enter_context(nc.sbuf_tensor(f"before_{start}_sb", [P, start], F32))
                return here.enter_context(nc.sbuf_tensor(f"parts_{start}_sb", [P, n], F32R))[:, :]

        at_tT, at_w1, at_w2, at_act = AREA_2 + 2048, AREA_1, AREA_2 + 10880, AREA_2 + 7168
        tT_hi_parts, tT_lo_parts = parts(at_tT, KD * NT), parts(AREA_0 + 3360, KD * NT)
        expert_parts = [parts(start, KD * 2 * (512 + D)) for start in (at_w1, at_w2)]
        act_hi_parts, act_lo_parts = parts(at_act, 4 * CHUNK), parts(AREA_G + 4352, 4 * CHUNK)
        at_ug, at_down_lo, at_hid, at_down_hi, at_xT = AREA_G, AREA_1 + 512, 0, 2 * NF * CHUNK, AREA_2 + 4224
        ug_parts = parts(at_ug, 2 * KD * 2 * FF)
        down_hi_parts, down_lo_parts = parts(at_down_hi, NF * D), parts(at_down_lo, NF * D)
        hid_parts, xT_parts = parts(at_hid, 2 * NF * CHUNK), parts(at_xT, 2 * KD * NT)
        wq_hi_parts, xs_parts = parts(AREA_0, KD * NH * DH), parts(AREA_2 + 13200, 2 * KD * P)
        bc_parts = parts(AREA_2 + 10240, CHUNK)
        area = sb("area", [P, 42760])
        select = sb("select", [2 * 2 * NS, 2 * NS], F32R)
        area_f, area_0 = area[:, 0:10240], area[:, 10240:16640]
        area_g, area_1, area_2 = area[:, 16640:24320], area[:, 24320:28800], area[:, 28800:42760]
        PS = ctx.enter_context(nc.psum_tensor("PS", [P, 8, 512], F32))

        def place(area, start, *shape):
            n = 1
            for k in shape:
                n *= k
            v = area[:, start:start + n]
            if len(shape) == 2:
                v = v.rearrange("p (a b) -> p a b", a=shape[0])
            if len(shape) == 3:
                v = v.rearrange("p (a b c) -> p a b c", a=shape[0], b=shape[1])
            return v

        def bank(i, *shape):
            v = PS[:, i, :]
            n = 1
            for k in shape:
                n *= k
            v = PS[:, i, 0:n]
            if len(shape) == 2:
                v = v.rearrange("p (a b) -> p a b", a=shape[0])
            if len(shape) == 3:
                v = v.rearrange("p (a b c) -> p a b c", a=shape[0], b=shape[1])
            return v

        used = [0]

        def little(*shape):
            n = 1
            for k in shape:
                n *= k
            v = place(small, used[0], *shape)
            used[0] += n
            assert used[0] <= 2256
            return v

        gamma, beta = little(64), little(64)
        norm_w, gate_b = little(D), little(NE)
        qk_w = little(2, 128)
        inv_freq = little(64)
        rope_x = little(2, 64)
        rope_0 = little(2, 64)
        eps_ln, eps_rms = little(1), little(1)
        negmax = little(2, HG)
        rinv = little(2, HG)
        stats6, mv, rstd = little(6), little(2), little(1)
        stats8, mv8, rstd8 = little(NB, 6), little(NB, 2), little(NB)
        spare = little(1)
        b1 = little(NE, 4)
        gates = little(NB, NE)
        b2_bias = little(NE, 2)
        stats4, mv4, rstd4 = little(4, 6), little(4, 2), little(4)
        one = little(1)
        qk_signed = little(2, 128)
        sumsq, rms = little(2, HG), little(2, HG)
        prob_sum = little(2, HG)
        ffn_cols = little(2 * NF + KD + NF)
        wsd = little(D)
        signs16, eps_q = little(KD), little(1)
        ssm_cols = little(MD, 24)

        int_ids = ctx.enter_context(nc.sbuf_tensor("int_ids", [P, 3, NB], I32))
        float_ids = sb("float_ids", [P, 3, NB])

        wq_nopeT = place(area_f, 0, NH, D)
        wk_upT = place(area_f, 4096, NH, RK)
        wv_upT = place(area_f, 5120, NH, RK)
        w_out = place(area_f, 6144, NH, D)
        exact = lambda t: t.bitcast(F32)
        wq0_hi, wq0_hi_f = place(wq_hi_parts, 0, KD, NH, DH), place(exact(wq_hi_parts), 0, KD, NH, DH)
        wq0_lo = place(hid_parts, 0, KD, NH, DH)
        wq_rope = [place(area_2, 5376, NH, RR), place(area_2, 12176, NH, RR)]
        xs_hi, xs_hi_f, xs_lo = place(xs_parts, 0, KD, P), place(exact(xs_parts), 0, KD, P), place(xs_parts, KD * P, KD, P)
        wkv0 = place(area_0, 4096, KD, DH)
        wo0 = place(area_0, 4352, NH // 2, D)
        wuqT = place(area_g, 0, NH, QC)
        wukT = place(area_g, 1536, NH, RK)
        wuvT = place(area_g, 2560, NH, RK)
        w_ox = place(area_g, 3584, NH, D)
        wqx = place(area_1, 0, NH, DH)
        wdq = place(area_1, 2048, KD, QC)
        wkvc = place(area_1, 2240, KD, RK)
        wkr = place(area_1, 2368, RR)
        wox = place(area_1, 2432, NH // 2, D)
        xs = place(area_2, 0, KD, P)
        q_tok = place(area_2, 256, 2, HG * DH)
        qT = place(area_2, 1280, 2, HG * P)
        prob = place(area_2, 2304, 2, HG * P)
        masked = place(area_2, 3328, 2, HG * P)
        probT = place(area_2, 4352, HG * P)
        o_norm = place(area_2, 4864, 2 * HG * RK // 2)
        oT = place(area_2, 5376, NH // 2, P)
        keyT = [place(area_2, 6400, NB, P), place(area_2, 7424, NB, P)]
        val = [place(area_2, 8448, NB, RK + 1), place(area_2, 8968, NB, RK + 1)]
        qcT = place(area_2, 9488, P)
        band = place(area_2, 9616, NB, P)
        rope_u = place(area_2, 10640, 2, HG * RR)
        rope_v = place(area_2, 11152, 2, HG * RR)
        x_now = place(area_2, 11920, D)
        k_tok = place(area_2, 256, NB, DH)
        z = place(area_2, 11664, D)
        x0T = place(area_2, 1280, KD, NT)
        ctxT_flat = sb("ctxT", [P, KD * NT])
        ctxT = place(ctxT_flat, 0, KD, NT)

        kv_cT = place(area_2, 4352, NT)

        def place_q(slot):
            return q_tok[:, slot % 2, :].rearrange("p (h d) -> p h d", h=HG)

        V_BASE = {"A": 2 * NB, "B": 0}

        w1_e = [place(area_0, 1536 * i, KD, 512) for i in range(2)]
        w2_e = [place(area_0, 1536 * i + 1024, KD, D) for i in range(2)]
        gate_wT = place(area_0, 3072, KD, NE)
        b2_all = place(area_0, 3104, D)
        tT = place(area_2, 0, KD, NT)
        t_tok = place(area_2, 2048, NB, D)
        tT_hi, tT_hi_f = place(tT_hi_parts, 0, KD, NT), place(exact(tT_hi_parts), 0, KD, NT)
        tT_lo = place(tT_lo_parts, 0, KD, NT)
        w1_hi, w1_lo = ([place(t, start, KD, 512) for t in expert_parts] for start in (0, 1024))
        w2_hi, w2_lo = ([place(t, start, KD, D) for t in expert_parts] for start in (2048, 2560))
        w1_hi_f = [place(exact(t), 0, KD, 512) for t in expert_parts]
        w2_hi_f = [place(exact(t), 2048, KD, D) for t in expert_parts]
        act_out = place(area_1, 3072, 2, CHUNK)
        squares0 = place(area_g, 4352, NB, D)
        act_hi, act_hi_f = place(act_hi_parts, 0, 2, 2, CHUNK), place(exact(act_hi_parts), 0, 2, 2, CHUNK)
        act_lo = place(act_lo_parts, 0, 2, 2, CHUNK)
        act_lin = place(area_2, 4096, 2, CHUNK)
        act_up = place(area_2, 5120, 2, CHUNK)
        act_gl = place(area_2, 6144, 2, CHUNK)
        logits = place(area_2, 9216, NB, NE + TOPK)
        top8 = place(area_2, 9376, NB, 8)
        picked = place(area_2, 9440, NB, NE + TOPK)
        expl = place(area_2, 9600, NB, NE)
        gatesT = place(area_2, 9728, NT)
        gsum = place(area_2, 10752, NB)
        ssq8 = place(area_2, 10760, NB)
        w_in = place(area_g, 0, KD, 2 * DI)
        w_x = place(area_g, 2048, MD, DTR + 4 * NS)
        w_dt = place(area_g, 2816, DI)
        w_ssm = place(area_g, 3328, MD, D)
        sz = place(area_g, 4352, MD, CHUNK)
        xT = place(area_2, 0, KD, NT)
        u_c = place(area_2, 2048, MD, CHUNK)
        dt = place(area_2, 4096, MD, CHUNK)
        dtu = place(area_2, 6144, MD, CHUNK)
        yg = place(area_2, 8192, MD, CHUNK)
        sp_tmp = place(area_2, 8192, MD, CHUNK)
        bc, bc_f = bc_parts, exact(bc_parts)
        dt_in = place(area_2, 10752, CHUNK)
        decay = place(area_2, 11264, 4, CHUNK)
        z4 = place(area_1, 0, 4, D)
        drive = place(area_1, 0, 4, CHUNK)
        state = place(area_1, 2048, 4, CHUNK)
        read_out = place(area_2, 8192, 4, CHUNK)
        b_rep = [place(area_g, 6400, CHUNK), place(area_g, 6912, CHUNK), place(area_2, 13312, CHUNK)]
        wq1 = place(area_f, 0, KD, NH * DH)
        wk1 = place(area_f, 4096, KD, KVH * DH)
        wv1 = place(area_f, 5120, KD, KVH * DH)
        wo1 = place(area_f, 6144, NH, D)
        keyT1 = area[:, 16640:16640 + 8192].rearrange("p (b g k) -> p b g k", b=NB, g=KVH)
        val1 = area[:, 24832:24832 + 8192].rearrange("p (b h n) -> p b h n", b=NB, h=2)
        area_e = area[:, 33024:42760]
        xs1 = place(area_e, 0, KD, P)
        x_now1 = place(area_e, 256, D)
        q_tok1 = place(area_e, 512, 2, HG * DH)
        k_tok1 = q_tok1
        rope_u1, rope_v1 = place(area_e, 1536, HG * DH), place(area_e, 2048, HG * DH)
        qT1 = place(area_e, 2560, 2, HG * P)
        probs1 = place(area_e, 3584, 2, HG * 2 * P)
        probT1 = place(area_e, 5632, 2, HG * P)
        squares = probT1
        o_norm1 = place(area_e, 6656, HG * DH)
        oT1 = place(area_e, 7168, NH, P)
        cs1 = place(area_e, 7168, KD, P)
        xs_next = place(area_0, 2 * 2 * FF + NF * D, KD * P)
        q_sq = place(area_e, 9216, HG * DH)
        rope_kt = place(angles, 0, 2, 2, DH)
        rope_qt = place(angles, 512, 2, DH)
        z1 = place(angles, 768, D)
        fly = place(angles, 0, 2, NF, FF // P * 4)
        w_ug = place(area_0, 0, KD, 2 * FF)
        w_down = place(area_0, 2 * 2 * FF, NF, D)
        sgate = place(area_2, 2048, 2, CHUNK)
        hid = place(area_2, 3072, 2, CHUNK)
        z4_last = place(area_2, 8448, 4, D)
        ug_hi, ug_lo = place(ug_parts, 0, KD, 2 * FF), place(ug_parts, KD * 2 * FF, KD, 2 * FF)
        ug_hi_f = place(exact(ug_parts), 0, KD, 2 * FF)
        down_hi, down_hi_f = place(down_hi_parts, 0, NF, D), place(exact(down_hi_parts), 0, NF, D)
        down_lo = place(down_lo_parts, 0, NF, D)
        hid_hi, hid_hi_f = place(hid_parts, 0, NF, CHUNK), place(exact(hid_parts), 0, NF, CHUNK)
        hid_lo = place(hid_parts, NF * CHUNK, NF, CHUNK)
        xT_hi, xT_hi_f = place(xT_parts, 0, KD, NT), place(exact(xT_parts), 0, KD, NT)
        xT_lo = place(xT_parts, KD * NT, KD, NT)
        block = ctx.enter_context(nc.Block())

        L0_OWNED = {
            "pe": "xt q tq sc tp pv to y qc kvp kvt",
            "act": "xs qabs qt exp ot qcs rs kvrs kvc kve",
            "dve": "rope u max on pt ln lna kvn kvr sm v band",
            "pool": "xb",
        }
        OWNED = {
            "A": dict(L0_OWNED, pool="xb xl"),
            "B": L0_OWNED,
            "C": {"pe": "tt lg gt gb ha hb y", "act": "r tT gT gl e rs th wh ah", "pool": "wl al",
                  "dve": "tl t up lin act acc lgs g x ln v2"},
            "D": {"pe": "xt xp zp bc dtp rep rb sum o", "act": "xT c1 uc sz ev sp b da rs",
                  "dve": "cv tv dt dtu rd h hc yg ln m st", "pool": "dbu"},
            "K": {"pe": "xt q pv kt", "act": "xs cs sq vc rs tc", "dve": "u ss kx kr", "pool": "xb tab"},
            "E": {"pe": "xt q tq sc tp pv to y", "act": "xa qabs qt exp ot rs rq",
                  "dve": "u rope ss nm max pt rc on lna v ln", "pool": "xb tab sq fly xsp"},
            "F": {"pe": "fold fd xt g up o", "act": "fu xT sg rs xh dh hh", "dve": "fe hid m st ln fl",
                  "pool": "xl dl hl"},
        }

        def start_counts(eng, who):
            for st in OWNED:
                for n in OWNED[st].get(who, "").split():
                    if physical(f"{st}_{n}") != f"{st}_{n}":
                        continue
                    eng.sem_inc(sem(f"{st}_{n}"), CREDIT)

        N_CONST = 7
        FOLDS = 4 + 4 + 2 + 4

        @block.sync
        def _(sp):
            def load(dst, src, s):
                sp.dma_start(dst, src).then_inc(sem(s), 16)

            load(x0T, a["xT"], "d_kv")
            load(wkv0, a["a_wkva"], "d_kv")
            load(consts[:, :], a["consts"], "d_const")
            load(rope_x, a["rope_x"], "d_const")
            load(inv_freq, a["inv_freq"], "d_const")
            load(gamma, a["gamma"].partition_broadcast(P), "d_const")
            load(beta, a["beta"].partition_broadcast(P), "d_const")
            load(norm_w, a["norm_w"].partition_broadcast(P), "d_const")
            load(gate_b, a["gate_b"].partition_broadcast(P), "d_const")
            load(int_ids[:, :, :], a["ids"], "d_ids")
            load(angles[:, 0:32], a["freqs"], "d_ids")
            load(X[:, 0:NB, :], a["x"], "d_x")
            load(wq_nopeT, a["a_wqnT"], "d_foldq")
            load(wk_upT, a["a_wkbT"], "d_foldq")
            for k in range(KD):
                load(wq_rope[k], a["a_wqr"][:, k], "d_wq0")
            load(wv_upT, a["a_wvbT"], "d_foldo")
            load(w_out, a["a_wout"], "d_foldo")
            load(ctxT[:, :, :], a["ctxT"], "d_ctx")
            load(wdq, a["b_wdq"], "d_ctx")
            load(wkvc, a["b_wkvc"], "d_ctx")
            load(wkr[0:RK, :], a["b_wkr"], "d_ctx")
            load(wuqT, a["b_wuqT"], "d_foldbq")
            load(wukT, a["b_wukT"], "d_foldbq")
            load(wqx[0:QC, :, RK:DH], a["b_wqr"], "d_wqx")
            load(wuvT, a["b_wuvT"], "d_foldbo")
            load(w_ox, a["b_wo"], "d_foldbo")
            load(b1, a["b1"], "d_moe")
            load(ssm_cols, a["ssm_cols"], "d_ssm")
            sp.wait_ge(sem("A_q"), at("A_q", NG * NB + 1))
            load(gate_wT, a["gate_w"], "d_moe")
            load(b2_all[0:NE, :], a["b2"], "d_moe")
            for i in range(2):
                load(w1_e[i], a["w1"][i], f"d_expert{i}")
                load(w2_e[i], a["w2"][i], f"d_expert{i}")
            load(w_in, a["w_in"], "d_ssm")
            load(w_x, a["w_x"], "d_ssm")
            load(w_dt, a["w_dt"], "d_ssm")
            load(w_ssm, a["w_ssm"], "d_ssm")
            sp.wait_ge(sem("fold_mm"), FOLDS)
            load(wq1, a["e_wq"], "d_e")
            load(wk1, a["e_wk"], "d_e")
            load(wv1, a["e_wv"], "d_e")
            load(wo1, a["e_wo"], "d_e")
            load(qk_w[:, 0, :], a["q_norm"].partition_broadcast(P), "d_rows")
            load(qk_w[:, 1, :], a["k_norm"].partition_broadcast(P), "d_rows")
            load(ffn_cols, a["ffn_cols"], "d_rows")
            load(wsd, a["ws_down"].partition_broadcast(P), "d_rows")
            with sp.Fori(1, NE // 2) as pair:
                for i in range(2):
                    sp.wait_ge(sem("C_wl"), at("C_wl", 4 * pair + 2 * i - 2))
                    load(w1_e[i], a["w1"][2 * pair + i], f"d_expert{i}")
                    load(w2_e[i], a["w2"][2 * pair + i], f"d_expert{i}")
            sp.wait_ge(sem("C_y"), at("C_y", 2 * NE))
            load(w_ug, a["w_ug"], "d_ffn")
            load(w_down, a["w_down"], "d_ffn")
            for half in range(2):
                sp.wait_ge(sem("F_ln"), at("F_ln", 4 * half + 4))
                sp.dma_start(out[:, 4 * half:4 * half + 4, :], X[:, 4 * half:4 * half + 4, :]).then_inc(sem("d_out"), 16)
            sp.wait_ge(sem("d_out"), 32)


        class Stage:

            def __init__(self, name, i, scale):
                self.name, self.i, self.scale = name, i, scale
                self.x = i == 1
                self.keyT, self.val = keyT[i], val[i]
                self.wo = wox if self.x else wo0
                self.rope = rope_x if self.x else rope_0

            def s(self, n):
                return sem(f"{self.name}_{n}")

        stages = [Stage("A", 0, float((DH + RR) ** -0.5)), Stage("B", 1, float((DH + RR) ** -0.5))]

        @block.tensor
        def _(pe):
            start_counts(pe, "pe")
            mm = nc.tensor.matmul
            tr = nc.tensor.transpose

            def keys_values(st):
                if st.x:
                    pe.wait_ge(sem("d_ctx"), 64)
                    pe.wait_ge(sem("A_kvr"), at("A_kvr", 2))
                    for c in range(NC_):
                        for k in range(KD):
                            ins = mm(PS[0:RK, 4 + c, :], wkvc[:, k, :], ctxT[:, k, c * CHUNK:(c + 1) * CHUNK],
                                     start=k == 0, stop=k == KD - 1)
                    ins.then_inc(sem("kvcT"), 1)
                    for b in range(NB):
                        for k in range(KD):
                            mm(bank(b // 4, 4, DH)[:, b % 4, 0:RK], ctxT[:, k, b * P:(b + 1) * P], wkvc[:, k, :],
                               start=k == 0, stop=k == KD - 1)
                    pe.wait_ge(st.s("kvc"), at(st.name + "_kvc", 1))
                    for b in range(NB):
                        ins = mm(bank(b // 4, 4, DH)[:, b % 4, RK:DH], kv_cT[0:RK, b * P:(b + 1) * P], wkr[0:RK, :],
                                 start=True, stop=True)
                    ins.then_inc(st.s("kvp"), 1)
                else:
                    pe.wait_ge(sem("d_kv"), 32)
                    for b in range(NB):
                        for k in range(KD):
                            ins = mm(bank(b // 4, 4, DH)[:, b % 4, :], x0T[:, k, b * P:(b + 1) * P], wkv0[:, k, :],
                                     start=k == 0, stop=k == KD - 1)
                    ins.then_inc(st.s("kvp"), 1)

            def turn_keys0(st):
                pe.wait_ge(st.s("kvr"), at(st.name + "_kvr", 2))
                pe.wait_ge(st.s("kve"), at(st.name + "_kve", 1))
                for b in range(NB):
                    ins = tr(bank(2 + b // 4, 4, P)[:, b % 4, :], k_tok[:, b, :], ident)
                ins.then_inc(st.s("kvt"), 1)

            def fold_bank(n):
                if n >= 4:
                    pe.wait_ge(sem("fold_ev"), n - 3)
                    if n < 8:
                        pe.wait_ge(sem("fold_lo"), n - 3)
                return 4 + n % 4

            def fold_queries(st, n):
                up_q, up_k = (wuqT, wukT) if st.x else (wq_nopeT, wk_upT)
                pe.wait_ge(sem("d_foldbq" if st.x else "d_foldq"), 32)
                for r0, nr in ([(0, QC)] if st.x else [(0, P), (P, P)]):
                    for hh in range(2):
                        to = fold_bank(n)
                        for h in range(8):
                            ins = mm(bank(to, 8, RK)[0:nr, h, :], up_q[:, 8 * hh + h, r0:r0 + nr],
                                     up_k[:, 8 * hh + h, :], start=True, stop=True)
                        ins.then_inc(sem("fold_mm"), 1)
                        n += 1
                return n

            def fold_output(st, n):
                up_v, w_o = (wuvT, w_ox) if st.x else (wv_upT, w_out)
                pe.wait_ge(sem("d_foldbo" if st.x else "d_foldo"), 32)
                for jj in range(NH // 4):
                    to = fold_bank(n)
                    for j in range(2):
                        for h in range(2):
                            ins = mm(bank(to, 2, D)[RK * h:RK * h + RK, j, :], up_v[:, 4 * jj + 2 * j + h, :],
                                     w_o[:, 4 * jj + 2 * j + h, :], start=True, stop=True)
                    ins.then_inc(sem("fold_mm"), 1)
                    n += 1
                return n

            def attend(st):
                s = st.s

                def turn_x(b):
                    pe.wait_ge(s("xb"), at(st.name + "_xb", b + 1))
                    pe.wait_ge(s("xs"), at(st.name + "_xs", b))
                    if st.x:
                        pe.wait_ge(s("qcs"), at(st.name + "_qcs", b))
                    for k in range(KD):
                        ins = tr(PS[:, 6, k * P:(k + 1) * P], x_now[:, k * P:(k + 1) * P], ident)
                    ins.then_inc(s("xt"), 1)

                def compress(b):
                    pe.wait_ge(s("xs"), at(st.name + "_xs", b + 1))
                    for k in range(KD):
                        ins = mm(PS[0:QC, 6, 256:256 + P], wdq[:, k, :], xs[:, k, :], start=k == 0, stop=k == KD - 1)
                    ins.then_inc(s("qc"), 1)

                def queries(n, b, g):
                    if g == 0:
                        pe.wait_ge(s("qcs" if st.x else "xl"), at(st.name + "_" + ("qcs" if st.x else "xl"), b + 1))
                    pe.wait_ge(s("qabs"), at(st.name + "_qabs", n))
                    if st.x:
                        ins = mm(bank(0, HG, DH), qcT[0:QC, :], wqx[0:QC, HG * g:HG * g + HG, :], start=True, stop=True)
                    else:
                        for k in range(KD):
                            for i, (x, w) in enumerate(((xs_hi, wq0_hi), (xs_hi, wq0_lo), (xs_lo, wq0_hi))):
                                ins = mm(bank(0, HG, DH), x[:, k, :], w[:, k, HG * g:HG * g + HG, :],
                                         start=k == 0 and i == 0, stop=k == KD - 1 and i == 2)
                    ins.then_inc(s("q"), 1)

                def turn_q(n, g):
                    pe.wait_ge(s("rope"), at(st.name + "_rope", n + 1))
                    pe.wait_ge(s("ot"), at(st.name + "_ot", n - 2))
                    for j in range(HG):
                        ins = tr(bank(1, HG, P)[:, j, :], q_tok[:, g % 2, j * DH:(j + 1) * DH], ident)
                    ins.then_inc(s("tq"), 1)

                def scores(n, b, g):
                    pe.wait_ge(s("qt"), at(st.name + "_qt", n + 1))
                    pe.wait_ge(s("max"), at(st.name + "_max", n - 1))
                    if not st.x:
                        pe.wait_ge(s("exp"), at(st.name + "_exp", n - 1))
                    for j in range(HG):
                        ins = mm(bank(2 + g % 2, HG, P)[:, j, :], qT[:, g % 2, j * P:(j + 1) * P], st.keyT[:, b, :],
                                 start=True, stop=True)
                    ins.then_inc(s("sc"), 1)

                def turn_p(n, g):
                    pe.wait_ge(s("exp"), at(st.name + "_exp", n + 1))
                    pe.wait_ge(s("pt"), at(st.name + "_pt", n))
                    for j in range(HG):
                        ins = tr(bank(4, HG, P)[:, j, :], prob[:, g % 2, j * P:(j + 1) * P], ident)
                    ins.then_inc(s("tp"), 1)

                def mix(n, b):
                    pe.wait_ge(s("pt"), at(st.name + "_pt", n + 1))
                    pe.wait_ge(s("on"), at(st.name + "_on", n))
                    for j in range(HG):
                        ins = mm(bank(5, HG, RK + 1)[:, j, :], probT[:, j * P:(j + 1) * P], st.val[:, b, :],
                                 start=True, stop=True)
                    ins.then_inc(s("pv"), 1)

                def turn_o(n):
                    pe.wait_ge(s("on"), at(st.name + "_on", n + 1))
                    for j in range(HG // 2):
                        ins = tr(PS[:, 1, j * P:(j + 1) * P], o_norm[:, j * P:(j + 1) * P], ident)
                    ins.then_inc(s("to"), 1)

                def project(n, b, g):
                    pe.wait_ge(s("ot"), at(st.name + "_ot", n + 1))
                    if g == 0:
                        pe.wait_ge(s("lna"), at(st.name + "_lna", b))
                    for c in (2 * g, 2 * g + 1):
                        ins = mm(PS[:, 7, 0:D], oT[:, c, :], st.wo[:, c, :], start=c == 0, stop=c == NH // 2 - 1)
                    ins.then_inc(s("y"), 1)

                def sequence(b, first=False, last=False):
                    for g in range(NG):
                        n = NG * b + g
                        if not last:
                            turn_q(n, g)
                            queries(n + 1, b + (g + 1) // NG, (g + 1) % NG)
                        if not (first and g < 3) and not (last and g > 2):
                            project(n - 3, b if g == 3 else b - 1, (g - 3) % NG)
                        if not (first and g < 2) and not (last and g > 1):
                            mix(n - 2, b if g >= 2 else b - 1)
                        if not last:
                            scores(n, b, g)
                            if g == 2 and st.x:
                                compress(b + 1)
                        if not (first and g < 2) and not (last and g > 1):
                            pe.wait_ge(s("qt"), at(st.name + "_qt", GROUPS if last else n + 1))
                            pe.wait_ge(s("ot"), at(st.name + "_ot", n - 2))
                            turn_o(n - 2)
                        if not (first and g < 1) and not (last and g > 0):
                            turn_p(n - 1, g + 1)
                        if g == 1 and not last:
                            turn_x(b + 1)

                pe.wait_ge(s("kvc"), at(st.name + "_kvc", 2))
                turn_x(0)
                if st.x:
                    compress(0)
                queries(0, 0, 0)
                sequence(0, first=True)
                with pe.Fori(1, NB) as b:
                    sequence(b)
                sequence(NB, last=True)

            keys_values(stages[0])
            pe.wait_ge(sem("d_const"), 16 * N_CONST)
            n = fold_queries(stages[0], 0)
            turn_keys0(stages[0])
            n = fold_output(stages[0], n)
            pe.wait_ge(sem("fold_ev"), n)
            keys_values(stages[1])
            n = fold_queries(stages[1], n)
            pe.wait_ge(sem("A_kvc"), at("A_kvc", 2))
            turn_keys0(stages[1])
            n = fold_output(stages[1], n)
            pe.wait_ge(sem("fold_ev"), n)
            pe.wait_ge(sem("wq_lo"), 2)
            pe.wait_ge(sem("d_wqx"), 16)
            pe.wait_ge(sem("B_kvc"), at("B_kvc", 2))
            attend(stages[0])
            for n, count in (("lna", NB), ("ot", NB * NG), ("on", NB * NG), ("pt", NB * NG), ("exp", NB * NG),
                             ("qt", NB * NG), ("qabs", NB * NG + 1), ("xs", NB + 1)):
                pe.wait_ge(sem("A_" + n), at("A_" + n, count))
            attend(stages[1])

            def gates_pe():
                pe.wait_ge(sem("C_g"), at("C_g", 1))
                for b in range(NB):
                    ins = tr(PS[0:NE, 5 + b // 4, (b % 4) * P:(b % 4 + 1) * P], gates[:, b, :], ident)
                ins.then_inc(sem("C_gt"), 1)
                pe.wait_ge(sem("C_gT"), at("C_gT", 1))
                for b in range(NB):
                    ins = mm(bank(4 + b // 2, 2, D)[:, b % 2, :], gatesT[0:NE, b * P:(b + 1) * P], b2_all[0:NE, :],
                             start=True, stop=True)
                ins.then_inc(sem("C_gb"), 1)

            def hidden(k, j):
                slot, c = j // 2, j % 2
                for m in range(2):
                    for part, name in ((0, "ha"), (1, "hb")):
                        read = "C_lin" if part == 0 else "C_up"
                        pe.wait_ge(sem(read), at(read, 2 * k + m - 1))
                        cols, toks = slice((2 * part + m) * P, (2 * part + m + 1) * P), slice(c * CHUNK, (c + 1) * CHUNK)
                        for kk in range(KD):
                            for i, (w, t) in enumerate(((w1_hi, tT_hi), (w1_hi, tT_lo), (w1_lo, tT_hi))):
                                ins = mm(PS[:, 2 * m + part, :], w[slot][:, kk, cols], t[:, kk, toks],
                                         start=kk == 0 and i == 0, stop=kk == KD - 1 and i == 2)
                        ins.then_inc(sem("C_" + name), 1)

            def outputs(k, j):
                slot, c = j // 2, j % 2
                pe.wait_ge(sem("C_al"), at("C_al", 2 * k + 2))
                if j % 2 == 0:
                    pe.wait_ge(sem("C_wl"), at("C_wl", k + 2))
                pe.wait_ge(sem("C_acc"), at("C_acc", k - 1))
                for t in range(4):
                    for m in range(2):
                        for i, (x, w) in enumerate(((act_hi, w2_hi), (act_hi, w2_lo), (act_lo, w2_hi))):
                            ins = mm(bank(4 + 2 * c + t // 2, 2, D)[:, t % 2, :], x[:, c, m, t * P:(t + 1) * P],
                                     w[slot][:, m, :], start=m == 0 and i == 0, stop=m == 1 and i == 2)
                ins.then_inc(sem("C_y"), 1)

            def experts(pair, first=False, last=False):
                for j in range(4):
                    k = 4 * pair + j
                    if not last:
                        if j % 2 == 0:
                            pe.wait_ge(sem("C_wl"), at("C_wl", k + 1))
                        hidden(k, j)
                    if first and j == 0:
                        gates_pe()
                        pe.wait_ge(sem("C_x"), at("C_x", 1))
                    elif not (last and j > 0):
                        outputs(k - 1, (j - 1) % 4)

            for n, count in (("lna", NB), ("ot", NB * NG), ("on", NB * NG), ("pt", NB * NG), ("exp", NB * NG),
                             ("qt", NB * NG), ("qabs", NB * NG + 1), ("xs", NB + 1), ("qcs", NB + 1)):
                pe.wait_ge(sem("B_" + n), at("B_" + n, count))
            for b in range(NB):
                pe.wait_ge(sem("C_t"), at("C_t", b + 1))
                for k in range(KD):
                    ins = tr(PS[:, b // 2, ((b % 2) * KD + k) * P:((b % 2) * KD + k + 1) * P],
                             t_tok[:, b, k * P:(k + 1) * P], ident)
                ins.then_inc(sem("C_tt"), 1)
            pe.wait_ge(sem("d_moe"), 48)
            for b in range(NB):
                if b % 2 == 0:
                    pe.wait_ge(sem("C_tT"), at("C_tT", b // 2 + 1))
                for k in range(KD):
                    ins = mm(bank(4, NB, NE)[:, b, :], tT[:, k, b * P:(b + 1) * P], gate_wT[:, k, :],
                             start=k == 0, stop=k == KD - 1)
            ins.then_inc(sem("C_lg"), 1)
            pe.wait_ge(sem("C_tl"), at("C_tl", 4))
            experts(0, first=True)
            with pe.Fori(1, NE // 2) as pair:
                experts(pair)
            experts(NE // 2, last=True)

            pe.wait_ge(sem("C_lin"), at("C_lin", 4 * NE))
            pe.wait_ge(sem("C_acc"), at("C_acc", 2 * NE))
            for b in range(NB):
                pe.wait_ge(sem("C_ln"), at("C_ln", b + 1))
                for k in range(KD):
                    ins = tr(PS[:, b // 2, ((b % 2) * KD + k) * P:((b % 2) * KD + k + 1) * P],
                             X[:, b, k * P:(k + 1) * P], ident)
                ins.then_inc(sem("D_xt"), 1)
            pe.wait_ge(sem("D_xT"), at("D_xT", 4))
            pe.wait_ge(sem("d_ssm"), 80)
            with pe.Fori(0, NC_) as c:
                pe.wait_ge(sem("D_rd"), at("D_rd", MD * c))
                for m in range(MD):
                    for k in range(KD):
                        ins = mm(PS[:, m, :], w_in[:, k, m * P:(m + 1) * P], xT[:, k, bass.ds(c * CHUNK, CHUNK)],
                                 start=k == 0, stop=k == KD - 1)
                    ins.then_inc(sem("D_xp"), 1)
                pe.wait_ge(sem("D_m"), at("D_m", 2 * c))
                for m in range(MD):
                    for k in range(KD):
                        ins = mm(PS[:, 4 + m, :], w_in[:, k, DI + m * P:DI + (m + 1) * P],
                                 xT[:, k, bass.ds(c * CHUNK, CHUNK)], start=k == 0, stop=k == KD - 1)
                    ins.then_inc(sem("D_zp"), 1)
                for k in range(MD):
                    pe.wait_ge(sem("D_uc"), at("D_uc", MD * c + k + 1))
                    ins = mm(PS[:, 0, :], w_x[:, k, 0:DTR], u_c[:, k, :], start=k == 0, stop=k == MD - 1)
                ins.then_inc(sem("D_bc"), 1)
                pe.wait_ge(sem("D_ev"), at("D_ev", 2 * c + 1))
                for m in range(MD):
                    mm(PS[:, m, :], w_dt[:, m * P:(m + 1) * P], dt_in, start=True, stop=True).then_inc(sem("D_dtp"), 1)
                pe.wait_ge(sem("D_sz"), at("D_sz", c + 1))
                for k in range(MD):
                    ins = mm(PS[0:4 * NS, 6, :], w_x[:, k, DTR:], u_c[:, k, :], start=k == 0, stop=k == MD - 1)
                ins.then_inc(sem("D_bc"), 1)

                def replicate(row, to):
                    return mm(PS[:, to, :], select[:, row:row + 1].broadcast_to([4 * NS, P]), bc[0:4 * NS, :],
                              start=True, stop=True)

                def replicate_b(s):
                    if s < NS:
                        pe.wait_ge(sem("D_b"), at("D_b", NS * c + s - 1))
                        replicate(s, 4 + s % 2).then_inc(sem("D_rb"), 1)

                def replicate_c(s):
                    if s < NS:
                        pe.wait_ge(sem("D_hc"), at("D_hc", (NS * c + s - 1) * MD))
                        replicate(NS + s, 6 + s % 2).then_inc(sem("D_rep"), 1)

                pe.wait_ge(sem("D_dt"), at("D_dt", (MD + 1) * c + BC_AFTER + 2))
                replicate_b(0)
                replicate_c(0)
                replicate_b(1)
                for s in range(NS):
                    for m in range(MD):
                        if m == 0:
                            replicate_b(s + 2)
                            replicate_c(s + 1)
                        pe.wait_ge(sem("D_hc"), at("D_hc", (NS * c + s) * MD + m + 1))
                        if s == 0:
                            pe.wait_ge(sem("D_tv"), at("D_tv", MD * c + m + 1))
                        mm(PS[:, m, :], ident, read_out[:, m, :], start=s == 0, stop=s == NS - 1)\
                            .then_inc(sem("D_sum"), 1)
                pe.wait_ge(sem("D_yg"), at("D_yg", MD * c + MD))
                for t in range(4):
                    for k in range(MD):
                        ins = mm(bank(6 + t // 2, 2, D)[:, t % 2, :], yg[:, k, t * P:(t + 1) * P], w_ssm[:, k, :],
                                 start=k == 0, stop=k == MD - 1)
                    if t % 2 == 1:
                        ins.then_inc(sem("D_o"), 1)

            def turn_tokens(b):
                pe.wait_ge(sem("K_xb"), at("K_xb", b + 1))
                pe.wait_ge(sem("K_xs"), at("K_xs", b))
                for k in range(KD):
                    ins = tr(PS[:, 6, k * P:(k + 1) * P], x_now1[:, k * P:(k + 1) * P], ident)
                ins.then_inc(sem("K_xt"), 1)

            def project_keys(b):
                for half in range(2):
                    n = 2 * b + half
                    src = xs1 if half else cs1
                    pe.wait_ge(sem("K_xs" if half else "K_cs"), at("K_xs" if half else "K_cs", b + 1))
                    pe.wait_ge(sem("K_u"), at("K_u", n - 1))
                    for k in range(KD):
                        ins = mm(PS[:, half, :], src[:, k, :], wk1[:, k, :], start=k == 0, stop=k == KD - 1)
                    ins.then_inc(sem("K_q"), 1)
                    pe.wait_ge(sem("K_vc"), at("K_vc", n - 1))
                    for k in range(KD):
                        ins = mm(PS[:, 2 + half, :], src[:, k, :], wv1[:, k, :], start=k == 0, stop=k == KD - 1)
                    ins.then_inc(sem("K_pv"), 1)

            def turn_keys(b):
                for half in range(2):
                    n = 2 * b + half
                    pe.wait_ge(sem("K_kr"), at("K_kr", n + 1))
                    pe.wait_ge(sem("K_tc"), at("K_tc", n - 1))
                    for g in range(KVH):
                        ins = tr(bank(4 + half, KVH, P)[:, g, :], k_tok1[:, half, g * DH:(g + 1) * DH], ident)
                    ins.then_inc(sem("K_kt"), 1)

            pe.wait_ge(sem("D_m"), at("D_m", 2 * NC_))
            pe.wait_ge(sem("d_e"), 64)
            turn_tokens(0)
            project_keys(0)
            turn_tokens(1)
            with pe.Fori(1, NB - 1) as b:
                project_keys(b)
                turn_tokens(b + 1)
                turn_keys(b - 1)
            project_keys(NB - 1)
            turn_keys(NB - 2)
            turn_keys(NB - 1)

            def turn_x1(b, n=0):
                pe.wait_ge(sem("E_xb"), at("E_xb", b + 1))
                pe.wait_ge(sem("E_xa"), at("E_xa", b))
                pe.wait_ge(sem("E_qabs"), at("E_qabs", n))
                for k in range(KD):
                    ins = tr(PS[:, 0, k * P:(k + 1) * P], x_now1[:, k * P:(k + 1) * P], ident)
                ins.then_inc(sem("E_xt"), 1)

            def queries1(n, b, g):
                if g == 0:
                    pe.wait_ge(sem("E_xsp"), at("E_xsp", b + 1))
                pe.wait_ge(sem("E_qabs"), at("E_qabs", n))
                for k in range(KD):
                    ins = mm(PS[:, 0, :], xs1[:, k, :], wq1[:, k, g * 512:(g + 1) * 512], start=k == 0, stop=k == KD - 1)
                ins.then_inc(sem("E_q"), 1)

            def turn_q1(n, g):
                pe.wait_ge(sem("E_rope"), at("E_rope", n + 1))
                pe.wait_ge(sem("E_ot"), at("E_ot", n - 2))
                for j in range(HG):
                    ins = tr(bank(1, HG, P)[:, j, :], q_tok1[:, g % 2, j * DH:(j + 1) * DH], ident)
                ins.then_inc(sem("E_tq"), 1)

            def mix1(n, b, g):
                pe.wait_ge(sem("E_pt"), at("E_pt", n + 1))
                pe.wait_ge(sem("E_on"), at("E_on", n))
                for j in range(HG):
                    for half in range(2):
                        ins = mm(bank(6, HG, DH)[:, j, :], probT1[:, half, j * P:(j + 1) * P],
                                 val1[:, b, half, g * DH:(g + 1) * DH], start=half == 0, stop=half == 1)
                ins.then_inc(sem("E_pv"), 1)

            def scores1(n, b, g):
                pe.wait_ge(sem("E_qt"), at("E_qt", n + 1))
                pe.wait_ge(sem("E_nm"), at("E_nm", n))
                pe.wait_ge(sem("E_exp"), at("E_exp", n))
                for j in range(HG):
                    ins = mm(PS[:, 2 + j // 2, (j % 2) * 256:(j % 2 + 1) * 256], qT1[:, g % 2, j * P:(j + 1) * P],
                             keyT1[:, b, g, :], start=True, stop=True)
                ins.then_inc(sem("E_sc"), 1)

            def turn_o1(n):
                pe.wait_ge(sem("E_on"), at("E_on", n + 1))
                pe.wait_ge(sem("E_qt"), at("E_qt", n + 3))
                for j in range(HG):
                    ins = tr(bank(1, HG, P)[:, j, :], o_norm1[:, j * DH:(j + 1) * DH], ident)
                ins.then_inc(sem("E_to"), 1)

            def turn_p1(n, g):
                pe.wait_ge(sem("E_exp"), at("E_exp", n + 1))
                pe.wait_ge(sem("E_pt"), at("E_pt", n))
                for half in range(2):
                    for j in range(HG):
                        ins = tr(bank(4 + half, HG, P)[:, j, :],
                                 probs1[:, g % 2, j * 256 + half * P:j * 256 + (half + 1) * P], ident)
                ins.then_inc(sem("E_tp"), 1)

            def project1(n, b, g):
                pe.wait_ge(sem("E_ot"), at("E_ot", n + 1))
                if g == 0:
                    pe.wait_ge(sem("E_lna"), at("E_lna", b))
                for h in range(HG * g, HG * g + HG):
                    ins = mm(PS[:, 7, 0:D], oT1[:, h, :], wo1[:, h, :], start=h == 0, stop=h == NH - 1)
                ins.then_inc(sem("E_y"), 1)

            def sequence1(b, first=False, last=False):
                for g in range(NG):
                    n = NG * b + g
                    if not last:
                        turn_q1(n, g)
                        if g == 2:
                            pe.wait_ge(sem("E_xa"), at("E_xa", b + 2))
                        queries1(n + 1, b + (g + 1) // NG, (g + 1) % NG)
                    if not (first and g < 3) and not (last and g > 2):
                        project1(n - 3, b if g == 3 else b - 1, (g - 3) % NG)
                    if not (first and g < 2) and not (last and g > 1):
                        mix1(n - 2, b if g >= 2 else b - 1, (g - 2) % NG)
                    if not last:
                        scores1(n, b, g)
                    if not (first and g < 2) and not (last and g > 1):
                        if last:
                            pe.wait_ge(sem("E_ot"), at("E_ot", n - 2))
                            pe.wait_ge(sem("E_on"), at("E_on", n - 1))
                            for j in range(HG):
                                ins = tr(bank(1, HG, P)[:, j, :], o_norm1[:, j * DH:(j + 1) * DH], ident)
                            ins.then_inc(sem("E_to"), 1)
                        else:
                            turn_o1(n - 2)
                    if not (first and g < 1) and not (last and g > 0):
                        turn_p1(n - 1, (g - 1) % NG)
                    if g == 1 and not last:
                        turn_x1(b + 1, n + 2)

            pe.wait_ge(sem("K_tc"), at("K_tc", 2 * NB))
            pe.wait_ge(sem("K_vc"), at("K_vc", 2 * NB))
            turn_x1(0)
            queries1(0, 0, 0)
            sequence1(0, first=True)
            with pe.Fori(1, NB) as b:
                sequence1(b)
            sequence1(NB, last=True)

            for n, count in (("lna", NB), ("ot", NB * NG), ("on", NB * NG), ("pt", NB * NG), ("exp", NB * NG),
                             ("qabs", NB * NG + 1), ("xa", NB + 1), ("fly", NB)):
                pe.wait_ge(sem("E_" + n), at("E_" + n, count))
            for i in range(KD):
                src = ctxT_flat if i == 0 else w_ug[:, 0, :]
                for q in range(4):
                    ins = mm(PS[:, 4 * i + q, :], hadamard, src[:, q * 512:(q + 1) * 512], start=True, stop=True)
                ins.then_inc(sem("F_fold"), 1)
            pe.wait_ge(sem("F_fl"), at("F_fl", 4))
            wd_flat = w_down.rearrange("p f d -> p (f d)")
            for q in range(4):
                ins = mm(PS[:, q, :], hadamard, wd_flat[:, q * 512:(q + 1) * 512], start=True, stop=True)
            ins.then_inc(sem("F_fd"), 1)
            pe.wait_ge(sem("F_fl"), at("F_fl", 8))
            for b in range(NB):
                pe.wait_ge(sem("E_ln"), at("E_ln", b + 1))
                for k in range(KD):
                    ins = tr(PS[:, 4 + b // 2, ((b % 2) * KD + k) * P:((b % 2) * KD + k + 1) * P],
                             X[:, b, k * P:(k + 1) * P], ident)
                ins.then_inc(sem("F_xt"), 1)
            pe.wait_ge(sem("F_xl"), at("F_xl", 4))
            pe.wait_ge(sem("F_fl"), at("F_fl", 8))
            pe.wait_ge(sem("F_fe"), at("F_fe", 1))
            with pe.Fori(0, NC_) as c:
                for f in range(NF):
                    n = NF * c + f
                    for part, name in ((1, "g"), (0, "up")):
                        pe.wait_ge(sem("F_sg" if part else "F_hid"), at("F_sg" if part else "F_hid", n - 1))
                        for k in range(KD):
                            for i, (w, x) in enumerate(((ug_hi, xT_hi), (ug_hi, xT_lo), (ug_lo, xT_hi))):
                                ins = mm(PS[:, 2 * part + f % 2, :], w[:, 1 - k, part * FF + f * P:part * FF + (f + 1) * P],
                                         x[:, k, bass.ds(c * CHUNK, CHUNK)], start=k == 0 and i == 0,
                                         stop=k == KD - 1 and i == 2)
                        ins.then_inc(sem("F_" + name), 1)
                pe.wait_ge(sem("F_dl"), at("F_dl", 1))
                pe.wait_ge(sem("F_m"), at("F_m", 2 * c))
                for t in range(4):
                    for f in range(NF):
                        if t == 0:
                            pe.wait_ge(sem("F_hl"), at("F_hl", NF * c + f + 1))
                        for i, (x, w) in enumerate(((hid_hi, down_hi), (hid_hi, down_lo), (hid_lo, down_hi))):
                            ins = mm(bank(4 + t // 2, 2, D)[:, t % 2, :], x[:, f, t * P:(t + 1) * P], w[:, f, :],
                                     start=f == 0 and i == 0, stop=f == NF - 1 and i == 2)
                    if t % 2 == 1:
                        ins.then_inc(sem("F_o"), 1)

        @block.scalar
        def _(act):
            start_counts(act, "act")
            nc.scalar.preload_act_table_set("natural_log_exp_and_others")

            def keys_values(st):
                s = st.s
                if st.x:
                    act.wait_ge(sem("kvcT"), 1)
                    act.activation(kv_cT[0:RK, :], PS[0:RK, 4:6, :], ACT.Copy).then_inc(s("kvc"), 1)
                    act.wait_ge(s("kvr"), at(st.name + "_kvr", 2))
                    act.activation(k_tok[:, :, 0:RK], PS[:, 0:2, :].rearrange("p c (a d) -> p (c a) d", a=4)[:, :, 0:RK],
                                   ACT.Copy).then_inc(s("kve"), 1)
                else:
                    act.wait_ge(s("v"), at(st.name + "_v", 2 * NB))
                    act.activation(rstd8, mv8[:, :, 1], ACT.Ln, bias=eps_ln[:, 0:1]).then_inc(s("kvc"), 1)
                    act.wait_ge(s("kvc"), at(st.name + "_kvc", 1))
                    act.activation(rstd8, rstd8, ACT.Exp, scale=-0.5).then_inc(s("kvrs"), 1)
                    act.wait_ge(s("kvn"), at(st.name + "_kvn", 1))
                    act.activation(k_tok[:, :, 0:RK], st.val[:, :, 0:RK], ACT.Copy).then_inc(s("kve"), 1)

            def copy_keys0(st):
                s = st.s
                act.wait_ge(s("kvt"), at(st.name + "_kvt", 1))
                act.activation(st.keyT.rearrange("p b k -> p (b k)"), PS[:, 2:4, :].rearrange("p c k -> p (c k)"),
                               ACT.Copy).then_inc(s("kvc"), 1)

            def fold_queries(st, n):
                for i, nr in enumerate([QC] if st.x else [P, P]):
                    for hh in range(2):
                        act.wait_ge(sem("fold_mm"), n + 1)
                        dst = wqx[0:QC, 8 * hh:8 * hh + 8, 0:RK] if st.x else wq0_hi[:, i, 8 * hh:8 * hh + 8, 0:RK]
                        act.activation(dst, bank(4 + n % 4, 8, RK)[0:nr], ACT.Copy).then_inc(sem("fold_ev"), 1)
                        n += 1
                if not st.x:
                    act.wait_ge(sem("d_wq0"), 32)
                    for k in range(KD):
                        act.activation(wq0_hi[:, k, :, RK:], wq_rope[k], ACT.Copy).then_inc(sem("wq_hi"), 1)
                return n

            def fold_output(st, n):
                for jj in range(NH // 4):
                    act.wait_ge(sem("fold_mm"), n + 1)
                    act.activation(st.wo[:, 2 * jj:2 * jj + 2, :], bank(4 + n % 4, 2, D), ACT.Copy)\
                       .then_inc(sem("fold_ev"), 1)
                    n += 1
                return n

            def attend(st):
                s = st.s

                def copy_x(b):
                    act.wait_ge(s("xt"), at(st.name + "_xt", b + 1))
                    act.wait_ge(s("qc" if st.x else "q"), at(st.name + "_" + ("qc" if st.x else "q"), b if st.x else NG * b))
                    src = PS[:, 6, 0:256].rearrange("p (k t) -> p k t", k=KD)
                    ins = act.activation(xs, src, ACT.Copy)
                    if not st.x:
                        ins = act.activation(xs_hi, src, ACT.Copy)
                    ins.then_inc(s("xs"), 1)

                def copy_compressed(b):
                    act.wait_ge(s("qc"), at(st.name + "_qc", b + 1))
                    act.wait_ge(s("q"), at(st.name + "_q", NG * b))
                    act.activation(qcT[0:QC, :], PS[0:QC, 6, 256:256 + P], ACT.Copy).then_inc(s("qcs"), 1)

                def copy_queries(n, slot):
                    act.wait_ge(s("q"), at(st.name + "_q", n + 1))
                    act.wait_ge(s("tq"), at(st.name + "_tq", n - 1))
                    act.activation(q_tok[:, slot % 2, :], PS[:, 0, :], ACT.Copy).then_inc(s("qabs"), 1)

                def copy_q(n, g):
                    act.wait_ge(s("tq"), at(st.name + "_tq", n + 1))
                    act.wait_ge(s("sc"), at(st.name + "_sc", n - 1))
                    act.activation(qT[:, g % 2, :], PS[:, 1, :], ACT.Copy).then_inc(s("qt"), 1)

                def softmax(n, g):
                    act.wait_ge(s("max"), at(st.name + "_max", n + 1))
                    act.wait_ge(s("tp"), at(st.name + "_tp", n - 1))
                    src = masked[:, g % 2, :] if st.x else PS[:, 2 + g % 2, :]
                    for j in range(HG):
                        ins = act.activation(prob[:, g % 2, j * P:(j + 1) * P], src[:, j * P:(j + 1) * P], ACT.Exp,
                                             bias=negmax[:, g % 2, j:j + 1], scale=st.scale)
                    ins.then_inc(s("exp"), 1)

                def copy_o(n, g):
                    act.wait_ge(s("to"), at(st.name + "_to", n + 1))
                    act.wait_ge(s("y"), at(st.name + "_y", n - 3))
                    act.activation(oT[:, 2 * g:2 * g + 2, :], PS[:, 1, 0:256].rearrange("p (a t) -> p a t", a=2),
                                   ACT.Copy).then_inc(s("ot"), 1)

                def copy_p(n):
                    act.wait_ge(s("tp"), at(st.name + "_tp", n + 1))
                    act.wait_ge(s("pv"), at(st.name + "_pv", n))
                    act.activation(probT, PS[:, 4, :], ACT.Copy).then_inc(s("pt"), 1)

                def inv_std(b):
                    act.wait_ge(s("v"), at(st.name + "_v", V_BASE[st.name] + 2 * b + 2))
                    act.wait_ge(s("ln"), at(st.name + "_ln", b))
                    act.activation(rstd, mv[:, 1:2], ACT.Ln, bias=eps_ln[:, 0:1]).then_inc(s("rs"), 1)
                    act.wait_ge(s("rs"), at(st.name + "_rs", 2 * b + 1))
                    act.activation(rstd, rstd, ACT.Exp, scale=-0.5).then_inc(s("rs"), 1)

                def sequence(b, first=False, last=False):
                    for g in range(NG):
                        n = NG * b + g
                        if not last:
                            copy_q(n, g)
                        if not (first and g < 1) and not (last and g > 0):
                            softmax(n - 1, (g - 1) % NG)
                        if not last:
                            if g == 2 and st.x:
                                copy_x(b + 1)
                            copy_queries(n + 1, g + 1)
                            if g == 2:
                                (copy_compressed if st.x else copy_x)(b + 1)
                        if not (first and g < 2) and not (last and g > 1):
                            copy_o(n - 2, (g - 2) % NG)
                        if st.x and not (first and g < 1) and not (last and g > 0):
                            copy_p(n - 1)
                        if g == 3 and last and st.x:
                            squares_of(range(NB - 1))
                        if g == 3 and not first:
                            inv_std(b - 1)

                copy_x(0)
                if st.x:
                    copy_compressed(0)
                copy_queries(0, 0)
                sequence(0, first=True)
                with act.Fori(1, NB) as b:
                    sequence(b)
                sequence(NB, last=True)

            def squares_of(sequences):
                for b in sequences:
                    act.wait_ge(sem("B_ln"), at("B_ln", b + 1))
                    ins = act.activation(squares0[:, b, :], X[:, b, :], ACT.Square, accum_out=ssq8[:, b:b + 1])
                return ins

            act.wait_ge(sem("eps"), 3)
            act.wait_ge(sem("ang"), 1)
            act.activation(sines[:, :], sines[:, :], ACT.Sin).then_inc(sem("trig"), 1)
            act.activation(cosines[:, :], cosines[:, :], ACT.Sin).then_inc(sem("trig"), 1)
            nc.scalar.preload_act_table_set("natural_log_exp_and_others")
            n = 0
            for st in stages:
                keys_values(st)
                n = fold_queries(st, n)
                copy_keys0(st)
                n = fold_output(st, n)
            act.wait_ge(sem("d_ssm"), 16)
            act.activation(ssm_cols[:, :, 6:22], ssm_cols[:, :, 6:22], ACT.Exp).then_inc(sem("A_log"), 1)
            attend(stages[0])
            attend(stages[1])

            def weights_hi(e, slot, second):
                act.wait_ge(sem(f"d_expert{slot}"), 16 * e + 32 - 16 * slot)
                if second:
                    act.wait_ge(sem("C_y"), at("C_y", 2 * e - 2))
                    act.activation(w2_hi[slot], w2_e[slot], ACT.Copy).then_inc(sem("C_wh"), 1)
                else:
                    act.wait_ge(sem("C_hb"), at("C_hb", 4 * e - 4))
                    act.activation(w1_hi[slot], w1_e[slot], ACT.Copy).then_inc(sem("C_wh"), 1)

            squares_of([NB - 1]).then_inc(sem("C_r"), 1)
            act.wait_ge(sem("C_r"), at("C_r", 1))
            act.activation(ssq8, ssq8, ACT.Ln, scale=1.0 / D, bias=eps_ln[:, 0:1]).then_inc(sem("C_r"), 1)
            act.wait_ge(sem("C_r"), at("C_r", 2))
            act.activation(ssq8, ssq8, ACT.Exp, scale=-0.5).then_inc(sem("C_r"), 1)
            weights_hi(0, 0, False)
            for i in range(4):
                act.wait_ge(sem("C_tt"), at("C_tt", 2 * i + 2))
                act.activation(tT[:, :, i * 2 * P:(i + 1) * 2 * P].rearrange("p k (b t) -> p b k t", b=2),
                               bank(i, 2, KD, P), ACT.Copy).then_inc(sem("C_tT"), 1)
            for i in range(4):
                act.wait_ge(sem("C_tT"), at("C_tT", i + 1))
                act.wait_ge(sem("C_tt"), at("C_tt", NB))
                cols = slice(i * 2 * P, (i + 1) * 2 * P)
                act.activation(tT_hi[:, :, cols], tT[:, :, cols], ACT.Copy).then_inc(sem("C_th"), 1)
            weights_hi(0, 0, True)
            act.wait_ge(sem("C_lgs"), at("C_lgs", 1))
            act.activation(expl, expl, ACT.Exp).then_inc(sem("C_e"), 1)
            act.wait_ge(sem("C_gt"), at("C_gt", 1))
            act.activation(gatesT[0:NE, :], PS[0:NE, 5:7, :].rearrange("p a b -> p (a b)"), ACT.Copy)\
               .then_inc(sem("C_gT"), 1)
            nc.scalar.preload_act_table(ACT.Gelu_apprx_sigmoid)

            def experts(pair, last=False):
                for j in range(4):
                    for m in range(2):
                        n = 8 * pair + 2 * j + m
                        act.wait_ge(sem("C_lin"), at("C_lin", n + 1))
                        act.wait_ge(sem("C_act"), at("C_act", n - 1))
                        act.activation(act_gl[:, m, :], act_lin[:, m, :], ACT.Gelu_apprx_sigmoid)\
                           .then_inc(sem("C_gl"), 1)
                    for m in range(2):
                        n = 8 * pair + 2 * j + m
                        act.wait_ge(sem("C_act"), at("C_act", n + 1))
                        act.wait_ge(sem("C_y"), at("C_y", 4 * pair + j - 1))
                        act.activation(act_hi[:, j % 2, m, :], act_out[:, m, :], ACT.Copy).then_inc(sem("C_ah"), 1)
                    if not (last and j > 1):
                        weights_hi(2 * pair + 1 + j // 2, (1 + j // 2) % 2, j % 2 == 1)

            with act.Fori(0, NE // 2 - 1) as pair:
                experts(pair)
            experts(NE // 2 - 1, last=True)
            nc.scalar.preload_act_table_set("natural_log_exp_and_others")

            def inv_std8():
                act.wait_ge(sem("C_v2"), at("C_v2", 2 * NB))
                act.activation(rstd8, mv8[:, :, 1], ACT.Ln, bias=eps_ln[:, 0:1]).then_inc(sem("C_rs"), 1)
                act.wait_ge(sem("C_rs"), at("C_rs", 1))
                act.activation(rstd8, rstd8, ACT.Exp, scale=-0.5).then_inc(sem("C_rs"), 1)

            inv_std8()

            for i in range(4):
                act.wait_ge(sem("D_xt"), at("D_xt", 2 * i + 2))
                act.activation(xT[:, :, i * 2 * P:(i + 1) * 2 * P].rearrange("p k (b t) -> p b k t", b=2),
                               bank(i, 2, KD, P), ACT.Copy).then_inc(sem("D_xT"), 1)
            with act.Fori(0, NC_) as c:
                nc.scalar.preload_act_table(ACT.Silu)
                for m in range(MD):
                    act.wait_ge(sem("D_xp"), at("D_xp", MD * c + m + 1))
                    act.activation(u_c[:, m, :], PS[:, m, :], ACT.Identity, bias=ssm_cols[:, m, 3:4],
                                   scale=ssm_cols[:, m, 1:2]).then_inc(sem("D_c1"), 1)
                for m in range(MD):
                    act.wait_ge(sem("D_cv"), at("D_cv", 2 * (MD * c + m) + 2))
                    act.activation(u_c[:, m, :], u_c[:, m, :], ACT.Silu).then_inc(sem("D_uc"), 1)
                for m in range(MD):
                    act.wait_ge(sem("D_zp"), at("D_zp", MD * c + m + 1))
                    ins = act.activation(sz[:, m, :], PS[:, 4 + m, :], ACT.Silu)
                ins.then_inc(sem("D_sz"), 1)
                act.wait_ge(sem("D_bc"), at("D_bc", 2 * c + 1))
                act.activation(dt_in, PS[:, 0, :], ACT.Copy).then_inc(sem("D_ev"), 1)
                nc.scalar.preload_act_table_set("natural_log_exp_and_others")
                for m in range(MD):
                    n = MD * c + m
                    act.wait_ge(sem("D_tv"), at("D_tv", n + 1))
                    act.activation(sp_tmp[:, m, :], dt[:, m, :], ACT.Abs).then_inc(sem("D_sp"), 1)
                    act.wait_ge(sem("D_sp"), at("D_sp", 3 * n + 1))
                    act.activation(sp_tmp[:, m, :], sp_tmp[:, m, :], ACT.Exp, scale=-1.0).then_inc(sem("D_sp"), 1)
                    act.wait_ge(sem("D_sp"), at("D_sp", 3 * n + 2))
                    act.activation(sp_tmp[:, m, :], sp_tmp[:, m, :], ACT.Ln, bias=one[:, 0:1]).then_inc(sem("D_sp"), 1)
                    if m == BC_AFTER:
                        act.wait_ge(sem("D_bc"), at("D_bc", 2 * c + 2))
                        act.activation(bc[0:4 * NS, :], PS[0:4 * NS, 6, :], ACT.Copy).then_inc(sem("D_ev"), 1)

                def copy_b(s):
                    act.wait_ge(sem("D_rb"), at("D_rb", NS * c + s + 1))
                    if s > 1:
                        act.wait_ge(sem("D_dbu"), at("D_dbu", (NS * c + s - 2) * MD))
                    act.activation(b_rep[s % 3], PS[:, 4 + s % 2, :], ACT.Copy).then_inc(sem("D_b"), 1)

                copy_b(0)
                for s in range(NS):
                    for m in range(MD):
                        n = (NS * c + s) * MD + m
                        act.wait_ge(sem("D_h"), at("D_h", n - 3))
                        if s == 0:
                            act.wait_ge(sem("D_dtu"), at("D_dtu", 2 * (MD * c + m) + 2))
                        act.activation(decay[:, m, :], dt[:, m, :], ACT.Exp, scale=ssm_cols[:, m, 6 + s:7 + s])\
                           .then_inc(sem("D_da"), 1)
                        if m == 0 and s < NS - 1:
                            copy_b(s + 1)
                act.wait_ge(sem("D_st"), at("D_st", 10 * c + 10))
                act.activation(rstd4, mv4[:, :, 1], ACT.Ln, bias=eps_ln[:, 0:1]).then_inc(sem("D_rs"), 1)
                act.wait_ge(sem("D_rs"), at("D_rs", 2 * c + 1))
                act.activation(rstd4, rstd4, ACT.Exp, scale=-0.5).then_inc(sem("D_rs"), 1)

            def fetch_context(b):
                act.wait_ge(sem("K_pv"), at("K_pv", 2 * b - 1))
                act.activation(cs1, ctxT[:, :, bass.ds(b * P, P)], ACT.Copy).then_inc(sem("K_cs"), 1)

            def copy_tokens(b):
                act.wait_ge(sem("K_xt"), at("K_xt", b + 1))
                act.wait_ge(sem("K_pv"), at("K_pv", 2 * b))
                act.activation(xs1, PS[:, 6, 0:256].rearrange("p (k t) -> p k t", k=KD), ACT.Copy)\
                   .then_inc(sem("K_xs"), 1)

            def keys_act(b, more=True):
                for half in range(2):
                    n = 2 * b + half
                    act.wait_ge(sem("K_q"), at("K_q", n + 1))
                    act.wait_ge(sem("K_ss"), at("K_ss", n - 1))
                    act.activation(squares[:, half, :], PS[:, half, :], ACT.Square).then_inc(sem("K_sq"), 1)
                    act.wait_ge(sem("K_pv"), at("K_pv", n + 1))
                    act.activation(val1[:, b, half, :], PS[:, 2 + half, :], ACT.Copy).then_inc(sem("K_vc"), 1)
                    if more:
                        (copy_tokens if half else fetch_context)(b + 1)
                for half in range(2):
                    n = 2 * b + half
                    act.wait_ge(sem("K_ss"), at("K_ss", n + 1))
                    act.wait_ge(sem("K_kr"), at("K_kr", n - 1))
                    act.activation(rms[:, half, :], sumsq[:, half, :], ACT.Ln, scale=1.0 / DH, bias=eps_rms[:, 0:1])\
                       .then_inc(sem("K_rs"), 1)
                    act.wait_ge(sem("K_rs"), at("K_rs", 2 * n + 1))
                    act.activation(rms[:, half, :], rms[:, half, :], ACT.Exp, scale=-0.5).then_inc(sem("K_rs"), 1)

            def copy_keys(b):
                for half in range(2):
                    act.wait_ge(sem("K_kt"), at("K_kt", 2 * b + half + 1))
                    act.activation(keyT1[:, b, :, half * P:(half + 1) * P], bank(4 + half, KVH, P), ACT.Copy)\
                       .then_inc(sem("K_tc"), 1)

            act.wait_ge(sem("eps"), 4)
            act.wait_ge(sem("signed"), 1)
            nc.scalar.preload_act_table_set("natural_log_exp_and_others")
            act.wait_ge(sem("D_ln"), at("D_ln", NB))
            fetch_context(0)
            copy_tokens(0)
            keys_act(0)
            with act.Fori(1, NB - 1) as b:
                keys_act(b)
                copy_keys(b - 1)
            keys_act(NB - 1, more=False)
            copy_keys(NB - 2)
            copy_keys(NB - 1)

            def copy_x1(b):
                act.wait_ge(sem("E_xt"), at("E_xt", b + 1))
                act.wait_ge(sem("E_xsp"), at("E_xsp", b))
                act.activation(xs_next, PS[:, 0, 0:256], ACT.Copy).then_inc(sem("E_xa"), 1)

            def copy_queries1(n, slot):
                act.wait_ge(sem("E_q"), at("E_q", n + 1))
                act.wait_ge(sem("E_tq"), at("E_tq", n - 1))
                act.activation(q_tok1[:, slot, :], PS[:, 0, :], ACT.Copy).then_inc(sem("E_qabs"), 1)

            def inv_rms(n, slot):
                act.wait_ge(sem("E_ss"), at("E_ss", n + 1))
                act.wait_ge(sem("E_exp"), at("E_exp", n - 1))
                act.wait_ge(sem("E_max"), at("E_max", n - 1))
                act.activation(rms[:, slot, :], sumsq[:, slot, :], ACT.Ln, bias=eps_q[:, 0:1]).then_inc(sem("E_rq"), 1)
                act.wait_ge(sem("E_rq"), at("E_rq", 2 * n + 1))
                act.activation(rms[:, slot, :], rms[:, slot, :], ACT.Exp, scale=-0.5).then_inc(sem("E_rq"), 1)

            def copy_q1(n, g):
                act.wait_ge(sem("E_tq"), at("E_tq", n + 1))
                act.wait_ge(sem("E_sc"), at("E_sc", n - 1))
                act.activation(qT1[:, g % 2, :], PS[:, 1, :], ACT.Copy).then_inc(sem("E_qt"), 1)

            def softmax1(n, slot):
                act.wait_ge(sem("E_max"), at("E_max", n + 1))
                act.wait_ge(sem("E_tp"), at("E_tp", n - 1))
                act.wait_ge(sem("E_on"), at("E_on", n - 1))
                for j in range(HG):
                    ins = act.activation(probs1[:, slot, j * 256:(j + 1) * 256],
                                         PS[:, 2 + j // 2, (j % 2) * 256:(j % 2 + 1) * 256], ACT.Exp,
                                         bias=negmax[:, slot, j:j + 1], scale=rms[:, slot, j:j + 1],
                                         accum_out=prob_sum[:, slot, j:j + 1])
                ins.then_inc(sem("E_exp"), 1)

            def copy_o1(n, g):
                act.wait_ge(sem("E_to"), at("E_to", n + 1))
                act.wait_ge(sem("E_y"), at("E_y", n - 3))
                act.activation(oT1[:, HG * g:HG * g + HG, :], bank(1, HG, P), ACT.Copy).then_inc(sem("E_ot"), 1)

            def inv_std1(b):
                act.wait_ge(sem("E_v"), at("E_v", 2 * b + 2))
                act.wait_ge(sem("E_ln"), at("E_ln", b))
                act.activation(rstd, mv[:, 1:2], ACT.Ln, bias=eps_ln[:, 0:1]).then_inc(sem("E_rs"), 1)
                act.wait_ge(sem("E_rs"), at("E_rs", 2 * b + 1))
                act.activation(rstd, rstd, ACT.Exp, scale=-0.5).then_inc(sem("E_rs"), 1)

            def sequence1(b, first=False, last=False):
                for g in range(NG):
                    n = NG * b + g
                    if not last:
                        if g == 2:
                            copy_x1(b + 1)
                        copy_q1(n, g)
                    if not (first and g < 1) and not (last and g > 0):
                        softmax1(n - 1, (g - 1) % 2)
                    if not last:
                        copy_queries1(n + 1, (g + 1) % 2)
                    if not (first and g < 2) and not (last and g > 1):
                        copy_o1(n - 2, (g - 2) % NG)
                    if not last:
                        inv_rms(n + 1, (g + 1) % 2)
                    if g == 3 and not first:
                        inv_std1(b - 1)

            copy_x1(0)
            copy_queries1(0, 0)
            inv_rms(0, 0)
            sequence1(0, first=True)
            with act.Fori(1, NB) as b:
                sequence1(b)
            sequence1(NB, last=True)

            for i in range(KD):
                act.wait_ge(sem("F_fold"), at("F_fold", i + 1 if i == 0 else 2))
                for q in range(4):
                    act.activation(ug_hi[:, 1 - i, q * 512:(q + 1) * 512], PS[:, 4 * i + q, :], ACT.Copy,
                                   scale=signs16[:, i:i + 1]).then_inc(sem("F_fu"), 1)
            for i in range(4):
                act.wait_ge(sem("F_xt"), at("F_xt", 2 * i + 2))
                act.activation(xT[:, :, i * 2 * P:(i + 1) * 2 * P].rearrange("p k (b t) -> p b k t", b=2),
                               bank(4 + i, 2, KD, P), ACT.Copy).then_inc(sem("F_xT"), 1)
                act.wait_ge(sem("F_xT"), at("F_xT", i + 1))
                cols = slice(i * 2 * P, (i + 1) * 2 * P)
                act.activation(xT_hi[:, :, cols], xT[:, :, cols], ACT.Copy).then_inc(sem("F_xh"), 1)
            act.wait_ge(sem("F_fe"), at("F_fe", 2))
            act.activation(down_hi, w_down, ACT.Copy).then_inc(sem("F_dh"), 1)

            def hidden_hi(c, f):
                act.wait_ge(sem("F_hid"), at("F_hid", NF * c + f + 1))
                act.wait_ge(sem("F_o"), at("F_o", 2 * c))
                act.activation(hid_hi[:, f, :], hid[:, f % 2, :], ACT.Copy).then_inc(sem("F_hh"), 1)

            with act.Fori(0, NC_) as c:
                nc.scalar.preload_act_table(ACT.Silu)
                for f in range(NF):
                    n = NF * c + f
                    act.wait_ge(sem("F_g"), at("F_g", n + 1))
                    act.wait_ge(sem("F_hid"), at("F_hid", n - 1))
                    act.activation(sgate[:, f % 2, :], PS[:, 2 + f % 2, :], ACT.Silu, scale=ffn_cols[:, f:f + 1])\
                       .then_inc(sem("F_sg"), 1)
                    if f > 0:
                        hidden_hi(c, f - 1)
                hidden_hi(c, NF - 1)
                nc.scalar.preload_act_table_set("natural_log_exp_and_others")
                act.wait_ge(sem("F_st"), at("F_st", 10 * c + 10))
                act.activation(rstd4, mv4[:, :, 1], ACT.Ln, bias=eps_ln[:, 0:1]).then_inc(sem("F_rs"), 1)
                act.wait_ge(sem("F_rs"), at("F_rs", 2 * c + 1))
                act.activation(rstd4, rstd4, ACT.Exp, scale=-0.5).then_inc(sem("F_rs"), 1)

        @block.gpsimd
        def _(pool):
            start_counts(pool, "pool")
            pool.memset(X[:, NB, :], 0.0).then_inc(sem("zero"), 1)
            pool.wait_ge(sem("zero"), 1)
            pool.wait_ge(sem("d_x"), 16)

            def fetch_x(st, b, ready):
                if ready is not None:
                    pool.wait_ge(sem(ready), at(ready, b + 1))
                pool.wait_ge(sem(f"{st}_xt"), at(f"{st}_xt", b))
                pool.wait_ge(sem(f"{st}_xb"), at(f"{st}_xb", b))
                pool.tensor_copy(x_now, X[:, b, :]).then_inc(sem(f"{st}_xb"), 1)

            def tokens_lo(b):
                pool.wait_ge(sem("A_xs"), at("A_xs", b + 1))
                pool.tensor_tensor(xs_lo, xs, xs_hi_f, ALU.subtract).then_inc(sem("A_xl"), 1)

            pool.wait_ge(sem("wq_hi"), 2)
            pool.wait_ge(sem("fold_mm"), 4)
            for k in range(KD):
                pool.tensor_tensor(wq0_lo[:, k, :, RK:], wq_rope[k], wq0_hi_f[:, k, :, RK:], ALU.subtract)\
                    .then_inc(sem("wq_lo"), 1)
            with pool.Fori(0, NB) as b:
                fetch_x("A", b, None)
                tokens_lo(b)
            fetch_x("A", NB, None)
            tokens_lo(NB)
            pool.wait_ge(sem("A_xt"), at("A_xt", NB + 1))
            pool.wait_ge(sem("A_xb"), at("A_xb", NB + 1))
            with pool.Fori(0, NB) as b:
                fetch_x("B", b, "A_ln")
            fetch_x("B", NB, None)

            def weights_lo(e, slot, second):
                raw, hi, lo = (w2_e, w2_hi_f, w2_lo) if second else (w1_e, w1_hi_f, w1_lo)
                pool.wait_ge(sem("C_wh"), at("C_wh", 2 * e + 1 + second))
                pool.tensor_tensor(lo[slot], raw[slot], hi[slot], ALU.subtract).then_inc(sem("C_wl"), 1)

            def experts(pair, last=False):
                for j in range(4):
                    for m in range(2):
                        pool.wait_ge(sem("C_ah"), at("C_ah", 8 * pair + 2 * j + m + 1))
                        pool.tensor_tensor(act_lo[:, j % 2, m, :], act_out[:, m, :], act_hi_f[:, j % 2, m, :],
                                           ALU.subtract).then_inc(sem("C_al"), 1)
                    if not (last and j > 1):
                        weights_lo(2 * pair + 1 + j // 2, (1 + j // 2) % 2, j % 2 == 1)

            weights_lo(0, 0, False)
            weights_lo(0, 0, True)
            with pool.Fori(0, NE // 2 - 1) as pair:
                experts(pair)
            experts(NE // 2 - 1, last=True)

            with pool.Fori(0, NC_) as c:
                for s in range(NS):
                    for m in range(MD):
                        n = (NS * c + s) * MD + m
                        if m == 0:
                            pool.wait_ge(sem("D_b"), at("D_b", NS * c + s + 1))
                        if s == 0:
                            pool.wait_ge(sem("D_dtu"), at("D_dtu", 2 * (MD * c + m) + 1))
                        pool.wait_ge(sem("D_h"), at("D_h", n - 3))
                        pool.tensor_tensor(drive[:, m, :], dtu[:, m, :], b_rep[s % 3], ALU.mult)\
                            .then_inc(sem("D_dbu"), 1)

            trig = lambda t, i: t[:, 32 + i * 512:32 + (i + 1) * 512].rearrange("p (b f) -> p b f", b=NB)
            halves = lambda t: t.rearrange("p (i f) -> p i f", i=2)

            def rotation(dst, i, b, row):
                for kind, (table, w) in enumerate(((cosines, qk_w), (sines, qk_signed))):
                    ins = pool.tensor_tensor(halves(dst[:, kind, :]),
                                             trig(table, i)[:, b, :].unsqueeze(1).broadcast_to([P, 2, 64]),
                                             halves(w[:, row, :]), ALU.mult)
                return ins

            pool.wait_ge(sem("signed"), 1)
            with pool.Fori(0, NB) as b:
                pool.wait_ge(sem("D_ln"), at("D_ln", NB))
                pool.wait_ge(sem("K_xt"), at("K_xt", b))
                pool.wait_ge(sem("K_xb"), at("K_xb", b))
                pool.tensor_copy(x_now1, X[:, b, :]).then_inc(sem("K_xb"), 1)
                pool.wait_ge(sem("K_u"), at("K_u", 2 * b))
                pool.wait_ge(sem("K_tab"), at("K_tab", b))
                pool.sem_inc(sem("pool_go"), 1)
                for i in range(2):
                    ins = rotation(rope_kt[:, i, :, :], i, b, 1)
                ins.then_inc(sem("K_tab"), 1)

            def fetch_x1(b, ready=True):
                pool.wait_ge(sem("E_xt"), at("E_xt", b))
                pool.wait_ge(sem("E_xb"), at("E_xb", b))
                pool.tensor_copy(x_now1, X[:, b, :]).then_inc(sem("E_xb"), 1)

            def move_x(b):
                pool.wait_ge(sem("E_xa"), at("E_xa", b + 1))
                pool.wait_ge(sem("E_q"), at("E_q", NG * b))
                pool.sem_inc(sem("pool_go"), 1)
                pool.tensor_copy(xs1.rearrange("p k t -> p (k t)"), xs_next).then_inc(sem("E_xsp"), 1)

            def square_q(n, slot):
                pool.wait_ge(sem("E_qabs"), at("E_qabs", n + 1))
                pool.wait_ge(sem("E_ss"), at("E_ss", n))
                pool.wait_ge(sem("E_sq"), at("E_sq", n))
                pool.tensor_tensor(q_sq, q_tok1[:, slot, :], q_tok1[:, slot, :], ALU.mult).then_inc(sem("E_sq"), 1)

            def tables_q(b):
                pool.wait_ge(sem("E_u"), at("E_u", NG * b))
                pool.wait_ge(sem("E_tab"), at("E_tab", b))
                pool.sem_inc(sem("pool_go"), 1)
                rotation(rope_qt, 1, b % NB if isinstance(b, int) else b, 0).then_inc(sem("E_tab"), 1)

            def butterflies(b):
                cols = bass.ds(b * 256, 256)
                pool.tensor_tensor(ctxT_flat[:, cols], w_ug[:, 0, cols], w_ug[:, 1, cols], ALU.add)\
                    .then_inc(sem("fly_step"), 1)
                pool.wait_ge(sem("fly_step"), 4 * b + 1)
                pool.sem_inc(sem("pool_go"), 1)
                pool.tensor_tensor(w_ug[:, 0, cols], w_ug[:, 0, cols], w_ug[:, 1, cols], ALU.subtract)
                wd = w_down[:, :, bass.ds(b * 32, 32)]
                buf = [wd, fly[:, 0, :, :], fly[:, 1, :, :], wd]
                for step in range(3):
                    src, dst = buf[step], buf[step + 1]
                    if step > 0:
                        pool.wait_ge(sem("fly_step"), 4 * b + 1 + step)
                        pool.sem_inc(sem("pool_go"), 1)
                    stride = 1 << step
                    for block_ in range(NF // (2 * stride)):
                        lo = slice(2 * stride * block_, 2 * stride * block_ + stride)
                        hi = slice(2 * stride * block_ + stride, 2 * stride * (block_ + 1))
                        pool.tensor_tensor(dst[:, lo, :], src[:, lo, :], src[:, hi, :], ALU.add)
                        ins = pool.tensor_tensor(dst[:, hi, :], src[:, lo, :], src[:, hi, :], ALU.subtract)
                    ins.then_inc(sem("fly_step"), 1)
                pool.wait_ge(sem("fly_step"), 4 * b + 4)
                pool.sem_inc(sem("E_fly"), 1)

            def sequence1(b):
                square_q(NG * b + 1, 1)
                fetch_x1(b + 1)
                square_q(NG * b + 2, 0)
                move_x(b + 1)
                square_q(NG * b + 3, 1)
                tables_q(b + 1)
                square_q(NG * b + 4, 0)
                butterflies(b)

            pool.wait_ge(sem("K_xs"), at("K_xs", NB))
            pool.wait_ge(sem("K_u"), at("K_u", 2 * NB))
            pool.wait_ge(sem("K_cs"), at("K_cs", NB))
            pool.wait_ge(sem("K_xb"), at("K_xb", NB))
            pool.wait_ge(sem("K_tab"), at("K_tab", NB))
            pool.wait_ge(sem("K_kt"), at("K_kt", 2 * NB))
            pool.wait_ge(sem("d_ffn"), 32)
            fetch_x1(0)
            tables_q(0)
            move_x(0)
            square_q(0, 0)
            with pool.Fori(0, NB - 1) as b:
                sequence1(b)
            square_q(NG * (NB - 1) + 1, 1)
            fetch_x1(NB)
            square_q(NG * (NB - 1) + 2, 0)
            move_x(NB)
            square_q(NG * (NB - 1) + 3, 1)
            tables_q(NB)
            square_q(NG * NB, 0)
            butterflies(NB - 1)

            for i in range(4):
                pool.wait_ge(sem("F_xh"), at("F_xh", i + 1))
                cols = slice(i * 2 * P, (i + 1) * 2 * P)
                pool.tensor_tensor(xT_lo[:, :, cols], xT[:, :, cols], xT_hi_f[:, :, cols], ALU.subtract)\
                    .then_inc(sem("F_xl"), 1)
            pool.wait_ge(sem("F_dh"), at("F_dh", 1))
            pool.tensor_tensor(down_lo, w_down, down_hi_f, ALU.subtract).then_inc(sem("F_dl"), 1)
            with pool.Fori(0, NC_) as c:
                for f in range(NF):
                    pool.wait_ge(sem("F_hh"), at("F_hh", NF * c + f + 1))
                    pool.tensor_tensor(hid_lo[:, f, :], hid[:, f % 2, :], hid_hi_f[:, f, :], ALU.subtract)\
                        .then_inc(sem("F_hl"), 1)

        @block.vector
        def _(dve):
            start_counts(dve, "dve")
            steps = [0]

            def link(ins):
                steps[0] += 1
                ins.then_inc(sem("dve_step"), 1)
                dve.wait_ge(sem("dve_step"), steps[0])

            tt, ts = dve.tensor_tensor, dve.tensor_scalar
            dve.memset(eps_ln, LN_EPS).then_inc(sem("eps"), 1)
            dve.memset(one, 1.0).then_inc(sem("eps"), 1)
            dve.memset(eps_rms, RMS_EPS).then_inc(sem("eps"), 1)
            for v in val:
                dve.memset(v[:, :, RK:RK + 1], 1.0).then_inc(sem("ones"), 1)

            def residual4(st, c, bank0, sums):
                for half in range(2):
                    n = 2 * c + half
                    dve.wait_ge(sem(f"{st}_o"), at(f"{st}_o", n + 1))
                    tt(sums[:, 2 * half:2 * half + 2, :], X[:, bass.ds(4 * c + 2 * half, 2), :], bank(bank0 + half, 2, D),
                       ALU.add).then_inc(sem(f"{st}_m"), 1)
                    dve.wait_ge(sem(f"{st}_m"), at(f"{st}_m", n + 1))
                    for t in (2 * half, 2 * half + 1):
                        dve.bn_stats(stats4[:, t, :], sums[:, t, :]).then_inc(sem(f"{st}_st"), 1)
                    dve.wait_ge(sem(f"{st}_st"), at(f"{st}_st", 5 * n + 2))
                    dve.memset(spare, 0.0).then_inc(sem(f"{st}_st"), 1)
                    for t in (2 * half, 2 * half + 1):
                        dve.bn_aggr(mv4[:, t, :], stats4[:, t, :]).then_inc(sem(f"{st}_st"), 1)
                dve.wait_ge(sem(f"{st}_st"), at(f"{st}_st", 10 * c + 10))
                dve.wait_ge(sem(f"{st}_rs"), at(f"{st}_rs", 2 * c + 2))
                for t in range(4):
                    ts(X[:, 4 * c + t, :], sums[:, t, :], mv4[:, t, 0:1], rstd4[:, t:t + 1], ALU.subtract, ALU.mult)\
                        .then_inc(sem(f"{st}_ln"), 1)

            dve.wait_ge(sem("d_ids"), 32)
            dve.wait_ge(sem("d_const"), 16 * N_CONST)
            link(dve.tensor_copy(float_ids[:, :, :], int_ids[:, :, :]))
            for i in range(2):
                dst = angles[:, 32 + i * 512:32 + (i + 1) * 512].rearrange("p (b f) -> p b f", b=NB)
                ins = tt(dst, float_ids[:, i, :].unsqueeze(2).broadcast_to([P, NB, 64]),
                         inv_freq.unsqueeze(1).broadcast_to([P, NB, 64]), ALU.mult)
            link(ins)
            link(ts(sines[:, :], angles[:, :], 1 / (2 * PI), ROUND, ALU.mult, ALU.add))
            link(ts(sines[:, :], sines[:, :], -ROUND, None, ALU.add))
            for part in (TWO_PI_HI, TWO_PI_MID, TWO_PI_LO):
                link(dve.scalar_tensor_tensor(angles[:, :], sines[:, :], -part, angles[:, :], ALU.mult, ALU.add))
            link(ts(cosines[:, :], angles[:, :], PI / 2, -2 * PI, ALU.is_gt, ALU.mult))
            link(dve.scalar_tensor_tensor(cosines[:, :], angles[:, :], PI / 2, cosines[:, :], ALU.add, ALU.add))
            link(ts(cosines[:, :], cosines[:, :], PI_SAFE, -PI_SAFE, ALU.min, ALU.max))
            ts(sines[:, :], angles[:, :], PI_SAFE, -PI_SAFE, ALU.min, ALU.max).then_inc(sem("ang"), 1)
            dve.wait_ge(sem("trig"), 2)
            for i in range(2):
                dve.tensor_copy(rope_0[:, 0, 32 * i:32 * i + 32], cosines[:, 0:32])
            dve.tensor_copy(rope_0[:, 1, 0:32], sines[:, 0:32])
            link(ts(rope_0[:, 1, 32:64], sines[:, 0:32], -1.0, None, ALU.mult))
            dve.memset(eps_q, RMS_EPS * DH).then_inc(sem("eps"), 1)

            def keys_values(st):
                s = st.s
                raw = PS[:, 0:2, :].rearrange("p c (a d) -> p (c a) d", a=4)
                dve.wait_ge(s("kvp"), at(st.name + "_kvp", 1))
                if st.x:
                    dve.tensor_copy(st.val[:, :, 0:RK], raw[:, :, 0:RK]).then_inc(s("kvr"), 1)
                    dve.wait_ge(sem("A_kvt"), at("A_kvt", 1))
                else:
                    for b in range(NB):
                        dve.bn_stats(stats8[:, b, :], raw[:, b, 0:RK]).then_inc(s("v"), 1)
                    dve.wait_ge(s("v"), at(st.name + "_v", NB))
                    for b in range(NB):
                        dve.bn_aggr(mv8[:, b, :], stats8[:, b, :]).then_inc(s("v"), 1)
                    dve.wait_ge(s("v"), at(st.name + "_v", 2 * NB))
                    wide = [P, NB, RK]
                    v = st.val[:, :, 0:RK]
                    link(tt(v, raw[:, :, 0:RK], mv8[:, :, 0:1].broadcast_to(wide), ALU.subtract))
                    dve.wait_ge(s("kvrs"), at(st.name + "_kvrs", 1))
                    link(tt(v, v, rstd8.unsqueeze(2).broadcast_to(wide), ALU.mult))
                    link(tt(v, v, gamma.unsqueeze(1).broadcast_to(wide), ALU.mult))
                    tt(v, v, beta.unsqueeze(1).broadcast_to(wide), ALU.add).then_inc(s("kvn"), 1)
                    dve.wait_ge(s("kvp"), at(st.name + "_kvp", 1))
                    dve.memset(stats6, 0.0).then_inc(s("kvr"), 1)
                wide = [P, NB, RR]
                u = place(area_2, 10640, NB, RR)
                w = place(area_2, 11152, NB, RR)
                tt(u, raw[:, :, RK:], st.rope[:, 0, :].unsqueeze(1).broadcast_to(wide), ALU.mult)
                link(tt(w, raw[:, :, RK:], st.rope[:, 1, :].unsqueeze(1).broadcast_to(wide), ALU.mult))
                v4 = lambda t: t.rearrange("p b (i f) -> p b i f", i=2)
                tt(v4(k_tok[:, :, RK:]), v4(u), v4(w)[:, :, ::-1, :], ALU.add).then_inc(s("kvr"), 1)

            def attend(st):
                s = st.s
                cc = st.rope[:, 0, :].unsqueeze(1).broadcast_to([P, HG, RR])
                sn = st.rope[:, 1, :].unsqueeze(1).broadcast_to([P, HG, RR])

                def rotate(n, slot):
                    q = place_q(slot)[:, :, RK:]
                    u = rope_u[:, slot % 2, :].rearrange("p (h d) -> p h d", h=HG)
                    w = rope_v[:, slot % 2, :].rearrange("p (h d) -> p h d", h=HG)
                    dve.wait_ge(s("qabs"), at(st.name + "_qabs", n + 1))
                    tt(u, q, cc, ALU.mult)
                    tt(w, q, sn, ALU.mult).then_inc(s("u"), 1)
                    dve.wait_ge(s("u"), at(st.name + "_u", n + 1))
                    v4 = lambda t: t.rearrange("p h (i f) -> p h i f", i=2)
                    tt(v4(place_q(slot)[:, :, RK:]), v4(u), v4(w)[:, :, ::-1, :], ALU.add).then_inc(s("rope"), 1)

                def maximum(n, b, g):
                    dve.wait_ge(s("sc"), at(st.name + "_sc", n + 1))
                    dve.wait_ge(s("exp"), at(st.name + "_exp", n - 1))
                    src = bank(2 + g % 2, HG, P)
                    if st.x:
                        m = masked[:, g % 2, :].rearrange("p (h k) -> p h k", h=HG)
                        tt(m, src, band[:, b, :].unsqueeze(1).broadcast_to([P, HG, P]), ALU.add).then_inc(s("sm"), 1)
                        dve.wait_ge(s("sm"), at(st.name + "_sm", 2 * n + 1))
                        src = m
                    dve.tensor_reduce(negmax[:, g % 2, :], src, AX_X, ALU.max, negate=True).then_inc(s("sm"), 1)
                    dve.wait_ge(s("sm"), at(st.name + "_sm", 2 * n + 2 if st.x else n + 1))
                    ts(negmax[:, g % 2, :], negmax[:, g % 2, :], st.scale, None, ALU.mult).then_inc(s("max"), 1)

                def copy_p(n):
                    dve.wait_ge(s("tp"), at(st.name + "_tp", n + 1))
                    dve.wait_ge(s("pv"), at(st.name + "_pv", n))
                    dve.tensor_copy(probT, PS[:, 4, :]).then_inc(s("pt"), 1)

                def normalise(n):
                    dve.wait_ge(s("pv"), at(st.name + "_pv", n + 1))
                    dve.wait_ge(s("to"), at(st.name + "_to", n))
                    o = bank(5, HG, RK + 1)
                    dve.reciprocal(rinv[:, 0, :], o[:, :, RK]).then_inc(s("band"), 1)
                    dve.wait_ge(s("band"), at(st.name + "_band", n + 1))
                    tt(o_norm.rearrange("p (h d) -> p h d", h=HG), o[:, :, 0:RK],
                       rinv[:, 0, :].unsqueeze(2).broadcast_to([P, HG, RK]), ALU.mult).then_inc(s("on"), 1)

                def residual(b):
                    dve.wait_ge(s("y"), at(st.name + "_y", NG * b + NG))
                    tt(z, X[:, b, :], PS[:, 7, 0:D], ALU.add).then_inc(s("lna"), 1)
                    dve.wait_ge(s("lna"), at(st.name + "_lna", b + 1))
                    dve.bn_stats(stats6, z).then_inc(s("v"), 1)
                    dve.wait_ge(s("v"), at(st.name + "_v", V_BASE[st.name] + 2 * b + 1))
                    dve.memset(spare, 0.0)
                    dve.bn_aggr(mv, stats6).then_inc(s("v"), 1)

                def layernorm(b):
                    dve.wait_ge(s("v"), at(st.name + "_v", V_BASE[st.name] + 2 * b + 2))
                    dve.wait_ge(s("rs"), at(st.name + "_rs", 2 * b + 2))
                    ts(X[:, b, :], z, mv[:, 0:1], rstd[:, 0:1], ALU.subtract, ALU.mult).then_inc(s("ln"), 1)

                def sequence(b, first=False, last=False):
                    for g in range(NG):
                        n = NG * b + g
                        if not (first and g < 2) and not (last and g > 1):
                            normalise(n - 2)
                        if not last:
                            rotate(n + 1, g + 1)
                            maximum(n, b, g)
                        if not st.x and not (first and g < 1) and not (last and g > 0):
                            copy_p(n - 1)
                        if g == 2 and not first:
                            residual(b - 1)
                        if g == 3 and not first:
                            layernorm(b - 1)

                rotate(0, 0)
                sequence(0, first=True)
                with dve.Fori(1, NB) as b:
                    sequence(b)
                sequence(NB, last=True)

            keys_values(stages[0])
            dve.wait_ge(sem("fold_mm"), 4)
            for n in range(4):
                dve.wait_ge(sem("fold_ev"), n + 1)
                heads8 = slice(8 * (n % 2), 8 * (n % 2) + 8)
                tt(wq0_lo[:, n // 2, heads8, 0:RK], bank(4 + n, 8, RK), wq0_hi_f[:, n // 2, heads8, 0:RK], ALU.subtract)\
                    .then_inc(sem("fold_lo"), 1)
            keys_values(stages[1])
            for b in range(NB):
                bb = band[:, b, :]
                link(ts(bb, key_ids, float_ids[:, 2, b:b + 1], -1e30, ALU.is_gt, ALU.mult))
                link(ts(z[:, 0:P], key_ids, float_ids[:, 2, b:b + 1], -8.0, ALU.subtract, ALU.is_lt))
                link(dve.scalar_tensor_tensor(bb, z[:, 0:P], -1e30, bb, ALU.mult, ALU.add))
            dve.wait_ge(sem("B_kvt"), at("B_kvt", 1))
            attend(stages[0])
            attend(stages[1])

            dve.wait_ge(sem("d_rows"), 64)
            ts(qk_signed[:, :, 0:64], qk_w[:, :, 0:64], 1.0, None, ALU.mult)
            ts(signs16, ffn_cols[:, 16:18], 1.0 / 16, None, ALU.mult)
            ts(qk_signed[:, :, 64:], qk_w[:, :, 64:], -1.0, None, ALU.mult).then_inc(sem("signed"), 1)

            dve.wait_ge(sem("C_r"), at("C_r", 3))
            for b in range(NB):
                dve.scalar_tensor_tensor(t_tok[:, b, :], X[:, b, :], ssq8[:, b:b + 1], norm_w, ALU.mult, ALU.mult)\
                   .then_inc(sem("C_t"), 1)
            dve.wait_ge(sem("d_moe"), 48)
            ts(b2_bias, b1[:, :, 2:4], 1.0, None, ALU.add)
            dve.memset(logits[:, :, NE:], -3e38)
            for i in range(4):
                dve.wait_ge(sem("C_th"), at("C_th", i + 1))
                cols = slice(i * 2 * P, (i + 1) * 2 * P)
                tt(tT_lo[:, :, cols], tT[:, :, cols], tT_hi_f[:, :, cols], ALU.subtract).then_inc(sem("C_tl"), 1)
            dve.wait_ge(sem("C_lg"), at("C_lg", 1))
            link(tt(logits[:, :, 0:NE], bank(4, NB, NE), gate_b.unsqueeze(1).broadcast_to([P, NB, NE]), ALU.add))
            for b in range(NB):
                ins = dve.max(top8[:, b, :], logits[:, b, 0:NE])
            link(ins)
            tt(expl, logits[:, :, 0:NE], top8[:, :, 0:1].broadcast_to([P, NB, NE]), ALU.subtract)\
                .then_inc(sem("C_lgs"), 1)
            link(dve.memset(top8[:, :, TOPK:], -3e38))
            for b in range(NB):
                ins = dve.match_replace(picked[:, b, :], top8[:, b, :], logits[:, b, :], 3e38)
            link(ins)
            link(ts(picked, picked, 3e38, None, ALU.is_equal))
            dve.wait_ge(sem("C_e"), at("C_e", 1))
            link(tt(expl, expl, picked[:, :, 0:NE], ALU.mult))
            link(dve.tensor_reduce(gsum, expl, AX_X, ALU.add))
            link(dve.reciprocal(gsum, gsum))
            tt(gates, expl, gsum.unsqueeze(2).broadcast_to([P, NB, NE]), ALU.mult).then_inc(sem("C_g"), 1)

            def half_hidden(k, m, e):
                n = 2 * k + m
                dve.wait_ge(sem("C_ha"), at("C_ha", n + 1))
                dve.wait_ge(sem("C_gl"), at("C_gl", n - 1))
                ts(act_lin[:, m, :], PS[:, 2 * m, :], b1[:, e, m:m + 1], 7.0, ALU.add, ALU.min)\
                    .then_inc(sem("C_lin"), 1)
                dve.wait_ge(sem("C_hb"), at("C_hb", n + 1))
                dve.wait_ge(sem("C_act"), at("C_act", n - 1))
                ts(act_up[:, m, :], PS[:, 2 * m + 1, :], b2_bias[:, e, m:m + 1], -6.0, ALU.add, ALU.max)\
                    .then_inc(sem("C_up"), 1)

            def activate(k, m, c):
                n = 2 * k + m
                dve.wait_ge(sem("C_gl"), at("C_gl", n + 1))
                dve.wait_ge(sem("C_up"), at("C_up", n + 1))
                dve.wait_ge(sem("C_al"), at("C_al", n - 1))
                dve.scalar_tensor_tensor(act_out[:, m, :], act_up[:, m, :], 8.0, act_gl[:, m, :], ALU.min, ALU.mult)\
                   .then_inc(sem("C_act"), 1)

            def accumulate(k, c, e):
                dve.wait_ge(sem("C_y"), at("C_y", k + 1))
                dve.wait_ge(sem("C_acc"), at("C_acc", k - 1))
                for t in range(4):
                    b = 4 * c + t
                    ins = dve.scalar_tensor_tensor(X[:, b, :], bank(4 + 2 * c + t // 2, 2, D)[:, t % 2, :],
                                                   gates[:, b, bass.ds(e, 1)], X[:, b, :], ALU.mult, ALU.add)
                ins.then_inc(sem("C_acc"), 1)

            def experts(pair, first=False, last=False):
                for j in range(4):
                    k = 4 * pair + j
                    if not last:
                        for m in range(2):
                            half_hidden(k, m, 2 * pair + j // 2)
                        for m in range(2):
                            activate(k, m, j % 2)
                    if first and j == 0:
                        dve.wait_ge(sem("C_gb"), at("C_gb", 1))
                        for b in range(NB):
                            ins = dve.scalar_tensor_tensor(X[:, b, :], X[:, b, :], 2.0, bank(4 + b // 2, 2, D)[:, b % 2, :],
                                                           ALU.mult, ALU.add)
                        ins.then_inc(sem("C_x"), 1)
                        dve.wait_ge(sem("C_x"), at("C_x", 1))
                    elif not (last and j > 0):
                        accumulate(k - 1, (j - 1) % 2, 2 * pair + (0 if j >= 1 else -1) + (1 if j > 2 else 0))

            experts(0, first=True)
            with dve.Fori(1, NE // 2) as pair:
                experts(pair)
            experts(NE // 2, last=True)
            dve.wait_ge(sem("C_acc"), at("C_acc", 2 * NE))
            for b in range(NB):
                dve.bn_stats(stats8[:, b, :], X[:, b, :]).then_inc(sem("C_v2"), 1)
            dve.wait_ge(sem("C_v2"), at("C_v2", NB))
            for b in range(NB):
                dve.bn_aggr(mv8[:, b, :], stats8[:, b, :]).then_inc(sem("C_v2"), 1)
            dve.wait_ge(sem("C_rs"), at("C_rs", 2))
            dve.wait_ge(sem("C_v2"), at("C_v2", 2 * NB))
            for b in range(NB):
                ts(X[:, b, :], X[:, b, :], mv8[:, b, 0:1], rstd8[:, b:b + 1], ALU.subtract, ALU.mult)\
                    .then_inc(sem("C_ln"), 1)

            tt(select[:, :], ident[0:4 * NS, 0:2 * NS], ident[0:4 * NS, 2 * NS:4 * NS], ALU.add)
            dve.wait_ge(sem("d_ssm"), 16)
            dve.wait_ge(sem("A_log"), 1)
            link(ts(ssm_cols[:, :, 6:22], ssm_cols[:, :, 6:22], -1.0, None, ALU.mult))
            with dve.Fori(0, NC_) as c:
                tok = lambda t, m: t[:, m, :].rearrange("p (b t) -> p b t", b=4)
                for m in range(MD):
                    n = MD * c + m
                    xp, u4 = bank(m, 4, P), tok(u_c, m)
                    dve.wait_ge(sem("D_c1"), at("D_c1", n + 1))
                    dve.scalar_tensor_tensor(u4[:, :, 1:], xp[:, :, 0:P - 1], ssm_cols[:, m, 0:1], u4[:, :, 1:],
                                             ALU.mult, ALU.add).then_inc(sem("D_cv"), 1)
                    dve.wait_ge(sem("D_cv"), at("D_cv", 2 * n + 1))
                    dve.scalar_tensor_tensor(u4[:, :, 0:P - 1], xp[:, :, 1:], ssm_cols[:, m, 2:3], u4[:, :, 0:P - 1],
                                             ALU.mult, ALU.add).then_inc(sem("D_cv"), 1)
                for m in range(MD):
                    dve.wait_ge(sem("D_dtp"), at("D_dtp", MD * c + m + 1))
                    ts(dt[:, m, :], PS[:, m, :], ssm_cols[:, m, 4:5], None, ALU.add).then_inc(sem("D_tv"), 1)
                for m in range(MD):
                    n = MD * c + m
                    dve.wait_ge(sem("D_sp"), at("D_sp", 3 * n + 3))
                    dve.scalar_tensor_tensor(dt[:, m, :], dt[:, m, :], 0.0, sp_tmp[:, m, :], ALU.max, ALU.add)\
                       .then_inc(sem("D_dt"), 1)
                    dve.wait_ge(sem("D_dt"), at("D_dt", (MD + 1) * c + m + 1 + (m > BC_AFTER)))
                    tt(dtu[:, m, :], dt[:, m, :], u_c[:, m, :], ALU.mult).then_inc(sem("D_dtu"), 1)
                    dve.wait_ge(sem("D_dtu"), at("D_dtu", 2 * n + 1))
                    dve.memset(dt[:, m, :].rearrange("p (b t) -> p b t", b=4)[:, :, 0], 1e37).then_inc(sem("D_dtu"), 1)
                    if m == BC_AFTER:
                        dve.wait_ge(sem("D_ev"), at("D_ev", 2 * c + 2))
                        low = slice(2 * NS, 4 * NS)
                        tt(bc[low, :], PS[low, 6, :], bc_f[low, :], ALU.subtract).then_inc(sem("D_dt"), 1)

                def step_state(s, m):
                    n = (NS * c + s) * MD + m
                    dve.wait_ge(sem("D_da"), at("D_da", n + 1))
                    dve.wait_ge(sem("D_dbu"), at("D_dbu", n + 1))
                    dve.wait_ge(sem("D_hc"), at("D_hc", n - 3))
                    dve.tensor_tensor_scan(state[:, m, :], decay[:, m, :], drive[:, m, :], 0.0,
                                           ALU.mult, ALU.add).then_inc(sem("D_h"), 1)

                def read_state(s, m):
                    n = (NS * c + s) * MD + m
                    dve.wait_ge(sem("D_h"), at("D_h", n + 1))
                    dve.wait_ge(sem("D_sum"), at("D_sum", n - 3))
                    if m == 0:
                        dve.wait_ge(sem("D_rep"), at("D_rep", NS * c + s + 1))
                    tt(read_out[:, m, :], state[:, m, :], PS[:, 6 + s % 2, :], ALU.mult).then_inc(sem("D_hc"), 1)

                step_state(0, 0)
                for i in range(1, NS * MD):
                    step_state(i // MD, i % MD)
                    read_state((i - 1) // MD, (i - 1) % MD)
                read_state(NS - 1, MD - 1)
                dve.wait_ge(sem("D_sum"), at("D_sum", (c + 1) * NS * MD))
                for m in range(MD):
                    dve.scalar_tensor_tensor(yg[:, m, :], u_c[:, m, :], ssm_cols[:, m, 5:6], PS[:, m, :],
                                             ALU.mult, ALU.add).then_inc(sem("D_rd"), 1)
                for m in range(MD):
                    dve.wait_ge(sem("D_rd"), at("D_rd", MD * c + m + 1))
                    tt(yg[:, m, :], yg[:, m, :], sz[:, m, :], ALU.mult).then_inc(sem("D_yg"), 1)
                residual4("D", c, 6, z4)

            dve.wait_ge(sem("D_ln"), at("D_ln", NB))
            heads = lambda t: t.rearrange("p (h d) -> p h d", h=HG)
            swapped = lambda t: t.rearrange("p (h i f) -> p h i f", h=HG, i=2)

            def keys_dve(b):
                for half in range(2):
                    n = 2 * b + half
                    if half == 0:
                        dve.wait_ge(sem("K_tab"), at("K_tab", b + 1))
                    dve.wait_ge(sem("K_sq"), at("K_sq", n + 1))
                    dve.wait_ge(sem("K_kx"), at("K_kx", n))
                    tab = rope_kt[:, half, :, :]
                    tt(heads(rope_u1), bank(half, HG, DH), tab[:, 0, :].unsqueeze(1).broadcast_to([P, HG, DH]), ALU.mult)
                    tt(heads(rope_v1), bank(half, HG, DH), tab[:, 1, :].unsqueeze(1).broadcast_to([P, HG, DH]), ALU.mult)\
                        .then_inc(sem("K_u"), 1)
                    dve.wait_ge(sem("K_rs"), at("K_rs", 2 * n - 2))
                    dve.tensor_reduce(sumsq[:, half, :], heads(squares[:, half, :]), AX_X, ALU.add)\
                       .then_inc(sem("K_ss"), 1)
                    dve.wait_ge(sem("K_u"), at("K_u", n + 1))
                    dve.wait_ge(sem("K_kt"), at("K_kt", n - 1))
                    dve.wait_ge(sem("K_kr"), at("K_kr", n - 1))
                    tt(swapped(k_tok1[:, half, :]), swapped(rope_u1), swapped(rope_v1)[:, :, ::-1, :], ALU.add)\
                        .then_inc(sem("K_kx"), 1)
                for half in range(2):
                    n = 2 * b + half
                    dve.wait_ge(sem("K_kx"), at("K_kx", n + 1))
                    dve.wait_ge(sem("K_rs"), at("K_rs", 2 * n + 2))
                    tt(heads(k_tok1[:, half, :]), heads(k_tok1[:, half, :]),
                       rms[:, half, :].unsqueeze(2).broadcast_to([P, HG, DH]), ALU.mult).then_inc(sem("K_kr"), 1)

            with dve.Fori(0, NB) as b:
                keys_dve(b)

            def rotate1(n, slot):
                if slot == 0:
                    dve.wait_ge(sem("E_tab"), at("E_tab", n_seq[0] + 1))
                dve.wait_ge(sem("E_qabs"), at("E_qabs", n + 1))
                dve.wait_ge(sem("E_rope"), at("E_rope", n))
                cc, sn = (rope_qt[:, i, :].unsqueeze(1).broadcast_to([P, HG, DH]) for i in range(2))
                tt(heads(rope_u1), heads(q_tok1[:, slot, :]), cc, ALU.mult)
                tt(heads(rope_v1), heads(q_tok1[:, slot, :]), sn, ALU.mult)\
                    .then_inc(sem("E_u"), 1)
                dve.wait_ge(sem("E_sq"), at("E_sq", n + 1))
                dve.wait_ge(sem("E_rq"), at("E_rq", 2 * n - 2))
                dve.tensor_reduce(sumsq[:, slot, :], heads(q_sq), AX_X, ALU.add).then_inc(sem("E_ss"), 1)
                dve.wait_ge(sem("E_u"), at("E_u", n + 1))
                tt(swapped(q_tok1[:, slot, :]), swapped(rope_u1), swapped(rope_v1)[:, :, ::-1, :], ALU.add)\
                    .then_inc(sem("E_rope"), 1)

            def maximum1(n, slot):
                dve.wait_ge(sem("E_sc"), at("E_sc", n + 1))
                dve.wait_ge(sem("E_exp"), at("E_exp", n - 1))
                dve.tensor_reduce(negmax[:, slot, :], PS[:, 2:4, :].rearrange("p a (j k) -> p (a j) k", j=2), AX_X, ALU.max,
                                  negate=True).then_inc(sem("E_nm"), 1)
                dve.wait_ge(sem("E_nm"), at("E_nm", n + 1))
                dve.wait_ge(sem("E_rq"), at("E_rq", 2 * n + 2))
                tt(negmax[:, slot, :], negmax[:, slot, :], rms[:, slot, :], ALU.mult).then_inc(sem("E_max"), 1)

            def copy_p1(n):
                dve.wait_ge(sem("E_tp"), at("E_tp", n + 1))
                dve.wait_ge(sem("E_pv"), at("E_pv", n))
                dve.tensor_copy(probT1, PS[:, 4:6, :]).then_inc(sem("E_pt"), 1)

            def normalise1(n, slot):
                dve.wait_ge(sem("E_pv"), at("E_pv", n + 1))
                dve.wait_ge(sem("E_to"), at("E_to", n))
                dve.reciprocal(rinv[:, 0, :], prob_sum[:, slot, :]).then_inc(sem("E_rc"), 1)
                dve.wait_ge(sem("E_rc"), at("E_rc", n + 1))
                tt(heads(o_norm1), bank(6, HG, DH), rinv[:, 0, :].unsqueeze(2).broadcast_to([P, HG, DH]), ALU.mult)\
                    .then_inc(sem("E_on"), 1)

            def residual1(b):
                dve.wait_ge(sem("E_y"), at("E_y", NG * b + NG))
                tt(z1, X[:, b, :], PS[:, 7, 0:D], ALU.add).then_inc(sem("E_lna"), 1)
                dve.wait_ge(sem("E_lna"), at("E_lna", b + 1))
                dve.bn_stats(stats6, z1).then_inc(sem("E_v"), 1)
                dve.wait_ge(sem("E_v"), at("E_v", 2 * b + 1))
                dve.memset(spare, 0.0)
                dve.bn_aggr(mv, stats6).then_inc(sem("E_v"), 1)

            def layernorm1(b):
                dve.wait_ge(sem("E_v"), at("E_v", 2 * b + 2))
                dve.wait_ge(sem("E_rs"), at("E_rs", 2 * b + 2))
                ts(X[:, b, :], z1, mv[:, 0:1], rstd[:, 0:1], ALU.subtract, ALU.mult).then_inc(sem("E_ln"), 1)

            n_seq = [0]

            def sequence1(b, first=False, last=False):
                for g in range(NG):
                    n = NG * b + g
                    n_seq[0] = b
                    if not (first and g < 2) and not (last and g > 1):
                        normalise1(n - 2, g % 2)
                    if not last:
                        n_seq[0] = b + (g + 1) // NG
                        rotate1(n + 1, (g + 1) % 2)
                        maximum1(n, g % 2)
                    if not (first and g < 1) and not (last and g > 0):
                        copy_p1(n - 1)
                    if g == 2 and not first:
                        residual1(b - 1)
                    if g == 3 and not first:
                        layernorm1(b - 1)

            dve.wait_ge(sem("K_kt"), at("K_kt", 2 * NB))
            rotate1(0, 0)
            sequence1(0, first=True)
            with dve.Fori(1, NB) as b:
                sequence1(b)
            sequence1(NB, last=True)

            for i in range(KD):
                for q in range(4):
                    dve.wait_ge(sem("F_fu"), at("F_fu", 4 * i + q + 1))
                    cols = slice(q * 512, (q + 1) * 512)
                    dve.scalar_tensor_tensor(ug_lo[:, 1 - i, cols], PS[:, 4 * i + q, :], signs16[:, i:i + 1],
                                             ug_hi_f[:, 1 - i, cols], ALU.mult, ALU.subtract).then_inc(sem("F_fl"), 1)
            dve.wait_ge(sem("F_fd"), at("F_fd", 1))
            for f in range(NF):
                ins = ts(w_down[:, f, :], PS[:, f // 2, (f % 2) * D:(f % 2 + 1) * D], ffn_cols[:, 18 + f:19 + f], 1.0 / 32,
                         ALU.mult, ALU.mult)
            ins.then_inc(sem("F_fe"), 1)
            dve.wait_ge(sem("F_fe"), at("F_fe", 1))
            tt(w_down, w_down, wsd.unsqueeze(1).broadcast_to([P, NF, D]), ALU.mult).then_inc(sem("F_fe"), 1)
            with dve.Fori(0, NC_) as c:
                for f in range(NF):
                    n = NF * c + f
                    dve.wait_ge(sem("F_up"), at("F_up", n + 1))
                    dve.wait_ge(sem("F_sg"), at("F_sg", n + 1))
                    dve.wait_ge(sem("F_hl"), at("F_hl", n - 1))
                    dve.scalar_tensor_tensor(hid[:, f % 2, :], PS[:, f % 2, :], ffn_cols[:, 8 + f:9 + f], sgate[:, f % 2, :],
                                             ALU.mult, ALU.mult).then_inc(sem("F_hid"), 1)
                residual4("F", c, 4, z4_last)



def layouts(v):
    import numpy as np

    def rows(w, k=P):
        return w.reshape(-1, k, w.shape[-1]).transpose(1, 0, 2)

    def halves(w):
        return np.concatenate([w[..., 0::2], w[..., 1::2]], axis=-1)

    x, c = v["x"], v["ctx_2048"]
    o = {"x": x.transpose(1, 0, 2), "xT": rows(x.reshape(NT, D).T), "ctxT": rows(c.reshape(NT, D).T)}
    o["ids"] = np.stack([v["pos_BxS2"].T, v["itok_BxS_4096_4607"].T, v["itok_BxS_0_1023"].T], axis=1)
    o["freqs"] = v["L0_attn_freqs_cis"][0:P]
    wq = v["L0_attn_Wq"].reshape(D, NH, DH + RR)
    o["a_wqnT"] = wq[:, :, 0:DH].transpose(2, 1, 0)
    o["a_wqr"] = halves(wq[:, :, DH:]).reshape(KD, P, NH, RR).transpose(1, 0, 2, 3)
    kva = v["L0_attn_Wkv_a"]
    o["a_wkva"] = rows(np.concatenate([kva[:, 0:RK], halves(kva[:, RK:])], axis=1))
    kvb = v["L0_attn_Wkv_b"].reshape(RK, NH, 2 * DH)
    o["a_wkbT"] = kvb[:, :, 0:DH].transpose(2, 1, 0)
    o["a_wvbT"] = kvb[:, :, DH:].transpose(2, 1, 0)
    o["a_wout"] = v["L0_attn_Wout"].reshape(NH, DH, D).transpose(1, 0, 2)
    o["gamma"], o["beta"] = v["L0_attn_kv_gamma"], v["L0_attn_kv_beta"]
    o["b_wdq"], o["b_wkvc"], o["b_wkr"] = rows(v["L0_xattn_W_dq"]), rows(v["L0_xattn_W_kvc"]), v["L0_xattn_W_kr"]
    o["b_wuqT"] = v["L0_xattn_W_uq"].reshape(QC, NH, DH).transpose(2, 1, 0)
    o["b_wukT"] = v["L0_xattn_W_uk"].reshape(RK, NH, DH).transpose(2, 1, 0)
    o["b_wuvT"] = v["L0_xattn_W_uv"].reshape(RK, NH, DH).transpose(2, 1, 0)
    o["b_wqr"] = v["L0_xattn_W_qr"].reshape(QC, NH, RR)
    o["b_wo"] = v["L0_xattn_W_o"].reshape(NH, DH, D).transpose(1, 0, 2)
    w1 = v["L0_ffn_w1"]
    w1 = np.concatenate([w1[:, 0::2], w1[:, 1::2]], axis=1)
    o["w1"] = w1.transpose(0, 2, 1).reshape(NE, KD, P, 512).transpose(0, 2, 1, 3)
    b1 = v["L0_ffn_b1"]
    o["b1"] = np.concatenate([b1[:, 0::2], b1[:, 1::2]], axis=1).reshape(NE, 4, P).transpose(2, 0, 1)
    o["w2"] = v["L0_ffn_w2"].transpose(0, 2, 1).reshape(NE, KD, P, D).transpose(0, 2, 1, 3)
    o["b2"], o["gate_w"] = v["L0_ffn_b2"], rows(v["L0_ffn_gate_w"].T)
    w_x = v["L1_attn_W_x"]
    o["w_in"], o["w_dt"] = rows(v["L1_attn_W_in"]), v["L1_attn_W_dt"]
    o["w_x"] = rows(np.concatenate([w_x, w_x[:, DTR:]], axis=1))
    o["w_ssm"] = rows(v["L1_attn_W_out"])
    col = lambda w: w.reshape(MD, P, -1)
    cols = [col(v["L1_attn_conv_w"]), col(v["L1_attn_conv_b"]), col(v["L1_attn_b_dt"]), col(v["L1_attn_D"]),
            col(v["L1_attn_A_log"]), np.zeros((MD, P, 2), np.float32)]
    o["ssm_cols"] = np.concatenate(cols, axis=2).transpose(1, 0, 2)
    o["e_wq"], o["e_wk"], o["e_wv"] = (rows(v[f"L1_xattn_W{n}"].T) for n in "qkv")
    o["e_wo"] = v["L1_xattn_Wo"].T.reshape(NH, DH, D).transpose(1, 0, 2)
    o["q_norm"], o["k_norm"] = v["L1_xattn_q_norm_w"], v["L1_xattn_k_norm_w"]
    o["w_ug"] = rows(np.concatenate([v["L1_ffn_W_up"], v["L1_ffn_W_gate"]], axis=0).T)
    o["w_down"] = rows(v["L1_ffn_W_down"].T)
    ws = v["L1_ffn_Wscale_ug"].reshape(2, NF, P)
    cols = [ws[1].T, ws[0].T, v["L1_ffn_SU_ug"].reshape(KD, P).T, v["L1_ffn_SU_dp"].reshape(NF, P).T]
    o["ffn_cols"], o["ws_down"] = np.concatenate(cols, axis=1), v["L1_ffn_Wscale_dp"]
    o["norm_w"], o["gate_b"] = v["L0_ffn_norm_w"], v["L0_ffn_gate_b"]
    h = np.array([[1.0]])
    while h.shape[0] < P:
        h = np.block([[h, h], [h, -h]])
    o["consts"] = np.concatenate([np.eye(P), h, np.tile(np.arange(P), (P, 1))], axis=1).astype(np.float32)
    f32 = np.float32
    inv = (f32(1.0) / f32(10000.0) ** (np.arange(RR // 2, dtype=f32) / f32(RR // 2))).astype(f32)
    ang = (np.arange(P, dtype=f32)[:, None] * inv).astype(np.float64)
    cs, sn = np.cos(ang), np.sin(ang)
    o["rope_x"] = np.stack([np.concatenate([cs, cs], 1), np.concatenate([sn, -sn], 1)], axis=1).astype(f32)
    inv = (f32(1.0) / f32(10000.0) ** (np.arange(0, DH, 2, dtype=f32) / f32(DH))).astype(f32)
    o["inv_freq"] = np.tile(inv, (P, 1))
    return {k: np.ascontiguousarray(w) for k, w in o.items()}


def kernel(**inputs):
    import numpy as np
    import concourse.bacc as bacc
    from concourse.bass_utils import run_bass_kernel_spmd

    arrays = layouts({k: np.asarray(v) for k, v in inputs.items()})
    nc = bacc.Bacc("TRN2", target_bir_lowering=False, num_devices=1)
    aps = {k: nc.dram_tensor(k, w.shape, mybir.dt.from_np(w.dtype), kind="ExternalInput").ap()
           for k, w in arrays.items()}
    out = nc.dram_tensor("out", (P, NB, D), F32, kind="ExternalOutput").ap()
    build(nc, aps, out)
    r = run_bass_kernel_spmd(nc, [arrays], core_ids=[0])
    return np.ascontiguousarray(r.results[0]["out"].transpose(1, 0, 2))
```
